# Optimizing a Trainium2 kernel written in Bass

```python
import numpy as np
import jax
import jax.numpy as jnp

def _softmax(x, axis=-1):
    return jax.nn.softmax(x, axis=axis)

def _gelu(x):
    return jax.nn.gelu(x, approximate=True)

def _silu(x):
    return jax.nn.silu(x)

def _sigmoid(x):
    return jax.nn.sigmoid(x)

def _layernorm(x, axis=-1, eps=1e-05):
    m = jnp.mean(x, axis=axis, keepdims=True)
    v = jnp.var(x, axis=axis, keepdims=True)
    return (x - m) / jnp.sqrt(v + eps)

def _scatter_add(tgt, idx, src, axis=0):
    return tgt.at[idx].add(src)

def _segment_sum(src, seg, n):
    return jax.ops.segment_sum(src, seg, n)
kernel_name = 'mk_decoder_preln_d1_seqx_r8_90e990'

def setup_inputs(seed: int=0):
    np.random.seed(seed)
    _w = jnp.asarray

    def _rec_inputs():
        import jax
        import jax.numpy as jnp
        _rk = jax.random.key(seed)
        x = 2.818e-05 + 1 * jax.random.normal(jax.random.fold_in(_rk, 1), (1, 1024, 128), jnp.float32)
        _lenS = 1024 - jax.random.randint(jax.random.fold_in(_rk, 7), (1,), 0, max(1, 1024 // 4) + 1, jnp.int32)
        _lenS2 = 6404 - jax.random.randint(jax.random.fold_in(_rk, 8), (1,), 0, max(1, 6404 // 4) + 1, jnp.int32)
        _ctx_1024P = jax.random.normal(jax.random.fold_in(_rk, 11), (1, 16, 128), jnp.float32)
        _ctx_1024c = jax.random.dirichlet(jax.random.fold_in(_rk, 511), 0.3 * jnp.ones((16,), jnp.float32), (1, 6404))
        _ctx_1024t = jnp.einsum('bsk,bkd->bsd', _ctx_1024c, _ctx_1024P)
        _ctx_1024t = _ctx_1024t * jax.lax.rsqrt(jnp.mean(jnp.square(_ctx_1024t)) + 1e-12) * 0.953939
        ctx_1024 = -0.000392918 + 0.999932 * (_ctx_1024t + 0.3 * jax.random.normal(jax.random.fold_in(_rk, 611), (1, 6404, 128), jnp.float32))
        return (x, ctx_1024)
    x, ctx_1024 = _rec_inputs()

    def _L0_attn_setup():
        import jax, jax.numpy as jnp
        import numpy as np
        B, T, DIM = (8, 512, 128)
        HEADS = 16
        WS = [10, 20]
        SHIFTS = [5, 10]
        DIM_IN = DIM // 2
        DIM_BR = DIM_IN // 2
        H_BR = HEADS // 2
        EPS = 1e-06

        def rmsnorm(x, w):
            return x * jax.lax.rsqrt(jnp.mean(x * x, axis=-1, keepdims=True) + EPS) * w

        def _branch(x, window, shift, qkv_w, qkv_b, pw, pb, rpb, heads):
            Bx, Tn, C = x.shape
            pad = -Tn % window
            xp = jnp.pad(x, ((0, 0), (0, pad), (0, 0)))
            Tp = Tn + pad
            nW = Tp // window
            hd = C // heads
            scale = hd ** (-0.5)
            if shift > 0:
                xp = jnp.roll(xp, -shift, axis=1)
                m = np.zeros(Tp, np.float32)
                m[Tp - window:Tp - shift] = 1.0
                m[Tp - shift:] = 2.0
                mw = m.reshape(nW, window)
                amask = jnp.asarray(np.where(mw[:, :, None] != mw[:, None, :], -100.0, 0.0).astype(np.float32))
            else:
                amask = None
            xw = xp.reshape(Bx, nW, window, C)
            qkv = (xw @ qkv_w + qkv_b).reshape(Bx, nW, window, 3, heads, hd)
            q, k, v = (qkv[:, :, :, 0], qkv[:, :, :, 1], qkv[:, :, :, 2])
            attn = jnp.einsum('bnqhd,bnkhd->bnhqk', q * scale, k)
            coords = np.arange(window)
            ridx = coords[:, None] - coords[None, :] + window - 1
            bias = jnp.transpose(rpb[ridx], (2, 0, 1))
            attn = attn + bias[None, None]
            if amask is not None:
                attn = attn + amask[None, :, None]
            attn = jax.nn.softmax(attn, axis=-1)
            out = jnp.einsum('bnhqk,bnkhd->bnqhd', attn, v).reshape(Bx, nW, window, C)
            out = out @ pw + pb
            out = out.reshape(Bx, Tp, C)
            if shift > 0:
                out = jnp.roll(out, shift, axis=1)
            return out[:, :Tn]
        key = jax.random.key(seed)
        ks = jax.random.split(key, 12)
        w = lambda k, s: (jax.random.normal(k, s) * 0.02).astype(jnp.float32)
        z = lambda n: jnp.zeros((n,), jnp.float32)
        return {'x': jax.random.normal(ks[0], (B, T, DIM), jnp.float32), 'down_w': w(ks[1], (DIM, DIM_IN)), 'down_b': z(DIM_IN), 'up_w': w(ks[2], (DIM_IN, DIM)), 'up_b': z(DIM), 'norm1_w': jnp.ones((DIM_IN,), jnp.float32), 'norm2_w': jnp.ones((DIM,), jnp.float32), 'qkv1_w': w(ks[3], (DIM_BR, 3 * DIM_BR)), 'qkv1_b': z(3 * DIM_BR), 'proj1_w': w(ks[4], (DIM_BR, DIM_BR)), 'proj1_b': z(DIM_BR), 'rpb1': w(ks[5], (2 * WS[0] - 1, H_BR)), 'qkv2_w': w(ks[6], (DIM_BR, 3 * DIM_BR)), 'qkv2_b': z(3 * DIM_BR), 'proj2_w': w(ks[7], (DIM_BR, DIM_BR)), 'proj2_b': z(DIM_BR), 'rpb2': w(ks[8], (2 * WS[1] - 1, H_BR)), 'ffn_w1': w(ks[9], (DIM, 2 * DIM)), 'ffn_b1': z(2 * DIM), 'ffn_w2': w(ks[10], (2 * DIM, DIM)), 'ffn_b2': z(DIM)}
    _L0_attn_all = _L0_attn_setup()
    _L0_attn_in = {k: v for k, v in _L0_attn_all.items() if k in ('down_w', 'down_b', 'up_w', 'up_b', 'norm1_w', 'norm2_w', 'qkv1_w', 'qkv1_b', 'proj1_w', 'proj1_b', 'rpb1', 'qkv2_w', 'qkv2_b', 'proj2_w', 'proj2_b', 'rpb2', 'ffn_w1', 'ffn_b1', 'ffn_w2', 'ffn_b2')}
    del _L0_attn_all

    def _L0_xattn_setup():
        import jax, jax.numpy as jnp
        import numpy as np
        B, L, D = (8, 256, 128)
        key = jax.random.key(seed)
        k1, k2, k3 = jax.random.split(key, 3)
        enc_outputs = jax.random.normal(k1, (B, L, D), dtype=jnp.float32)
        x = jax.random.normal(k2, (B, L, D), dtype=jnp.float32)
        Wq = jax.random.normal(k3, (D, D), dtype=jnp.float32) * (1.0 / np.sqrt(D))
        return {'enc_outputs': enc_outputs, 'x': x, 'Wq': Wq}
    _L0_xattn_all = _L0_xattn_setup()
    _L0_xattn_in = {k: v for k, v in _L0_xattn_all.items() if k in ('Wq',)}
    del _L0_xattn_all

    def _L0_ffn_setup():
        import jax, jax.numpy as jnp
        import numpy as np
        D = 128
        H = 256
        E = 8
        TOP_K = 2
        N_SHARED = 1
        B, S = (2, 128)
        key = jax.random.key(seed)
        ks = jax.random.split(key, 12)
        sc = 0.02
        return {'hidden': jax.random.normal(ks[0], (B, S, D), jnp.float32), 'router_w': jax.random.normal(ks[1], (D, E), jnp.float32) * sc, 'router_b': jnp.zeros((E,), jnp.float32), 'sw1': jax.random.normal(ks[2], (D, H), jnp.float32) * sc, 'sb1': jnp.zeros((H,), jnp.float32), 'sw2': jax.random.normal(ks[3], (H, D), jnp.float32) * sc, 'sb2': jnp.zeros((D,), jnp.float32), 'rw1': jax.random.normal(ks[4], (E, D, H), jnp.float32) * sc, 'rb1': jnp.zeros((E, H), jnp.float32), 'rw2': jax.random.normal(ks[5], (E, H, D), jnp.float32) * sc, 'rb2': jnp.zeros((E, D), jnp.float32)}
    _L0_ffn_all = _L0_ffn_setup()
    _L0_ffn_in = {k: v for k, v in _L0_ffn_all.items() if k in ('router_w', 'router_b', 'sw1', 'sb1', 'sw2', 'sb2', 'rw1', 'rb1', 'rw2', 'rb2')}
    del _L0_ffn_all
    return {'x': x, 'ctx_1024': ctx_1024, 'L0_attn_down_w': _L0_attn_in['down_w'], 'L0_attn_down_b': _L0_attn_in['down_b'], 'L0_attn_up_w': _L0_attn_in['up_w'], 'L0_attn_up_b': _L0_attn_in['up_b'], 'L0_attn_norm1_w': _L0_attn_in['norm1_w'], 'L0_attn_norm2_w': _L0_attn_in['norm2_w'], 'L0_attn_qkv1_w': _L0_attn_in['qkv1_w'], 'L0_attn_qkv1_b': _L0_attn_in['qkv1_b'], 'L0_attn_proj1_w': _L0_attn_in['proj1_w'], 'L0_attn_proj1_b': _L0_attn_in['proj1_b'], 'L0_attn_rpb1': _L0_attn_in['rpb1'], 'L0_attn_qkv2_w': _L0_attn_in['qkv2_w'], 'L0_attn_qkv2_b': _L0_attn_in['qkv2_b'], 'L0_attn_proj2_w': _L0_attn_in['proj2_w'], 'L0_attn_proj2_b': _L0_attn_in['proj2_b'], 'L0_attn_rpb2': _L0_attn_in['rpb2'], 'L0_attn_ffn_w1': _L0_attn_in['ffn_w1'], 'L0_attn_ffn_b1': _L0_attn_in['ffn_b1'], 'L0_attn_ffn_w2': _L0_attn_in['ffn_w2'], 'L0_attn_ffn_b2': _L0_attn_in['ffn_b2'], 'L0_xattn_Wq': _L0_xattn_in['Wq'], 'L0_ffn_router_w': _L0_ffn_in['router_w'], 'L0_ffn_router_b': _L0_ffn_in['router_b'], 'L0_ffn_sw1': _L0_ffn_in['sw1'], 'L0_ffn_sb1': _L0_ffn_in['sb1'], 'L0_ffn_sw2': _L0_ffn_in['sw2'], 'L0_ffn_sb2': _L0_ffn_in['sb2'], 'L0_ffn_rw1': _L0_ffn_in['rw1'], 'L0_ffn_rb1': _L0_ffn_in['rb1'], 'L0_ffn_rw2': _L0_ffn_in['rw2'], 'L0_ffn_rb2': _L0_ffn_in['rb2']}

def reference(x, ctx_1024, L0_attn_down_w, L0_attn_down_b, L0_attn_up_w, L0_attn_up_b, L0_attn_norm1_w, L0_attn_norm2_w, L0_attn_qkv1_w, L0_attn_qkv1_b, L0_attn_proj1_w, L0_attn_proj1_b, L0_attn_rpb1, L0_attn_qkv2_w, L0_attn_qkv2_b, L0_attn_proj2_w, L0_attn_proj2_b, L0_attn_rpb2, L0_attn_ffn_w1, L0_attn_ffn_b1, L0_attn_ffn_w2, L0_attn_ffn_b2, L0_xattn_Wq, L0_ffn_router_w, L0_ffn_router_b, L0_ffn_sw1, L0_ffn_sb1, L0_ffn_sw2, L0_ffn_sb2, L0_ffn_rw1, L0_ffn_rb1, L0_ffn_rw2, L0_ffn_rb2):
    import jax
    import jax.numpy as jnp

    def _L0_attn_ref(x, down_w, down_b, up_w, up_b, norm1_w, norm2_w, qkv1_w, qkv1_b, proj1_w, proj1_b, rpb1, qkv2_w, qkv2_b, proj2_w, proj2_b, rpb2, ffn_w1, ffn_b1, ffn_w2, ffn_b2):
        import jax, jax.numpy as jnp
        import numpy as np
        B, T, DIM = (8, 512, 128)
        HEADS = 16
        WS = [10, 20]
        SHIFTS = [5, 10]
        DIM_IN = DIM // 2
        DIM_BR = DIM_IN // 2
        H_BR = HEADS // 2
        EPS = 1e-06

        def rmsnorm(x, w):
            return x * jax.lax.rsqrt(jnp.mean(x * x, axis=-1, keepdims=True) + EPS) * w

        def _branch(x, window, shift, qkv_w, qkv_b, pw, pb, rpb, heads):
            Bx, Tn, C = x.shape
            pad = -Tn % window
            xp = jnp.pad(x, ((0, 0), (0, pad), (0, 0)))
            Tp = Tn + pad
            nW = Tp // window
            hd = C // heads
            scale = hd ** (-0.5)
            if shift > 0:
                xp = jnp.roll(xp, -shift, axis=1)
                m = np.zeros(Tp, np.float32)
                m[Tp - window:Tp - shift] = 1.0
                m[Tp - shift:] = 2.0
                mw = m.reshape(nW, window)
                amask = jnp.asarray(np.where(mw[:, :, None] != mw[:, None, :], -100.0, 0.0).astype(np.float32))
            else:
                amask = None
            xw = xp.reshape(Bx, nW, window, C)
            qkv = (xw @ qkv_w + qkv_b).reshape(Bx, nW, window, 3, heads, hd)
            q, k, v = (qkv[:, :, :, 0], qkv[:, :, :, 1], qkv[:, :, :, 2])
            attn = jnp.einsum('bnqhd,bnkhd->bnhqk', q * scale, k)
            coords = np.arange(window)
            ridx = coords[:, None] - coords[None, :] + window - 1
            bias = jnp.transpose(rpb[ridx], (2, 0, 1))
            attn = attn + bias[None, None]
            if amask is not None:
                attn = attn + amask[None, :, None]
            attn = jax.nn.softmax(attn, axis=-1)
            out = jnp.einsum('bnhqk,bnkhd->bnqhd', attn, v).reshape(Bx, nW, window, C)
            out = out @ pw + pb
            out = out.reshape(Bx, Tp, C)
            if shift > 0:
                out = jnp.roll(out, shift, axis=1)
            return out[:, :Tn]
        residual = x
        xi = rmsnorm(x @ down_w + down_b, norm1_w)
        x1, x2 = (xi[..., :DIM_BR], xi[..., DIM_BR:])
        o1 = _branch(x1, WS[0], SHIFTS[0], qkv1_w, qkv1_b, proj1_w, proj1_b, rpb1, H_BR)
        o2 = _branch(x2, WS[1], SHIFTS[1], qkv2_w, qkv2_b, proj2_w, proj2_b, rpb2, H_BR)
        xc = jnp.concatenate([o1, o2], axis=-1) @ up_w + up_b
        x = residual + xc
        h = rmsnorm(x, norm2_w)
        ffn = jax.nn.gelu(h @ ffn_w1 + ffn_b1, approximate=False) @ ffn_w2 + ffn_b2
        return x + ffn

    def _L0_xattn_ref(enc_outputs, x, Wq):
        import jax, jax.numpy as jnp
        import numpy as np
        B, L, D = (8, 256, 128)
        d_k = x.shape[-1]
        q = jnp.einsum('bld,hd->blh', x, Wq)
        k = jnp.einsum('bld,hd->blh', enc_outputs, Wq)
        v = k
        scores = jnp.einsum('bqh,bkh->bqk', q, k) / jnp.sqrt(jnp.float32(d_k))
        Lq, Lk = (scores.shape[1], scores.shape[2])
        causal = jnp.tril(jnp.ones((Lq, Lk), dtype=bool))
        scores = jnp.where(causal, scores, -jnp.inf)
        attn = jax.nn.softmax(scores, axis=-1)
        return jnp.einsum('bqk,bkh->bqh', attn, v)

    def _L0_ffn_ref(hidden, router_w, router_b, sw1, sb1, sw2, sb2, rw1, rb1, rw2, rb2):
        import jax, jax.numpy as jnp
        import numpy as np
        D = 128
        H = 256
        E = 8
        TOP_K = 2
        N_SHARED = 1
        B, S = (2, 128)
        b, s, d = hidden.shape
        T = b * s
        flat = hidden.reshape(T, d)
        router_logits = flat @ router_w + router_b
        router_probs = jax.nn.softmax(router_logits, axis=-1)
        topk_probs, topk_idx = jax.lax.top_k(router_probs, TOP_K)
        weights = jnp.zeros_like(router_probs).at[jnp.arange(T)[:, None], topk_idx].add(topk_probs)
        sh = jax.nn.gelu(flat @ sw1 + sb1, approximate=False)
        shared_out = (sh @ sw2 + sb2) / N_SHARED
        h1 = jax.nn.gelu(jnp.einsum('td,edh->teh', flat, rw1) + rb1[None], approximate=False)
        expert_out = jnp.einsum('teh,ehd->ted', h1, rw2) + rb2[None]
        mixed = jnp.einsum('ted,te->td', expert_out, weights)
        return (shared_out + mixed).reshape(b, s, d)
    x = x + _L0_attn_ref(_layernorm(x, axis=-1), L0_attn_down_w, L0_attn_down_b, L0_attn_up_w, L0_attn_up_b, L0_attn_norm1_w, L0_attn_norm2_w, L0_attn_qkv1_w, L0_attn_qkv1_b, L0_attn_proj1_w, L0_attn_proj1_b, L0_attn_rpb1, L0_attn_qkv2_w, L0_attn_qkv2_b, L0_attn_proj2_w, L0_attn_proj2_b, L0_attn_rpb2, L0_attn_ffn_w1, L0_attn_ffn_b1, L0_attn_ffn_w2, L0_attn_ffn_b2)
    x = x + _L0_xattn_ref(ctx_1024, _layernorm(x, axis=-1), L0_xattn_Wq)
    x = x + _L0_ffn_ref(_layernorm(x, axis=-1), L0_ffn_router_w, L0_ffn_router_b, L0_ffn_sw1, L0_ffn_sb1, L0_ffn_sw2, L0_ffn_sb2, L0_ffn_rw1, L0_ffn_rb1, L0_ffn_rw2, L0_ffn_rb2)
    return x

_drawn_inputs = setup_inputs


def setup_inputs(seed=0):
    import zlib

    import numpy as np

    out = dict(_drawn_inputs(seed))
    spreads = {'L0_attn_down_b': (0.0, 0.8),
     'L0_attn_up_b': (0.0, 0.1),
     'L0_attn_norm1_w': (1.0, 0.6),
     'L0_attn_norm2_w': (1.0, 0.6),
     'L0_attn_qkv1_b': (0.0, 0.8),
     'L0_attn_proj1_b': (0.0, 0.8),
     'L0_attn_qkv2_b': (0.0, 0.8),
     'L0_attn_proj2_b': (0.0, 0.8),
     'L0_attn_ffn_b1': (0.0, 0.8),
     'L0_attn_ffn_b2': (0.0, 0.1),
     'L0_ffn_router_b': (0.0, 0.8),
     'L0_ffn_sb1': (0.0, 0.8),
     'L0_ffn_sb2': (0.0, 0.1),
     'L0_ffn_rb1': (0.0, 0.8),
     'L0_ffn_rb2': (0.0, 0.714)}
    factors = {'L0_attn_down_w': 8.0,
     'L0_attn_up_w': 7.149,
     'L0_attn_qkv1_w': 8.0,
     'L0_attn_proj1_w': 8.0,
     'L0_attn_rpb1': 8.0,
     'L0_attn_qkv2_w': 8.0,
     'L0_attn_proj2_w': 8.0,
     'L0_attn_rpb2': 8.0,
     'L0_attn_ffn_w1': 2.986,
     'L0_attn_ffn_w2': 2.68,
     'L0_ffn_router_w': 5.666,
     'L0_ffn_sw1': 3.185,
     'L0_ffn_sw2': 2.863,
     'L0_ffn_rw1': 8.0,
     'L0_ffn_rw2': 8.0}
    for name, (base, spread) in spreads.items():
        noise = np.random.default_rng([zlib.crc32(name.encode()), seed]).standard_normal(out[name].shape)
        drawn = base * np.exp(spread * noise) if base else spread * noise
        out[name] = jnp.asarray(drawn.astype(out[name].dtype))
    for name, factor in factors.items():
        out[name] = (out[name] * factor).astype(out[name].dtype)
    return out
```

```python
from contextlib import ExitStack

import concourse.bass as bass
from concourse import mybir

F32 = mybir.dt.float32
BF16 = mybir.dt.bfloat16
ALU = mybir.AluOpType
ACT = mybir.ActivationFunctionType
AX = mybir.AxisListType

P = 128
T = 1024
D = 128
NT = T // P
HALVES = 2
TH = NT // HALVES
CH = T // HALVES
DI = 64
C = DI // 2
HD = 4
HID = 256
NC = HID // P
E = 8
EX = E + 1
QKV = 3 * C
MASKED = -(2.0 ** 100)

BRANCHES = (dict(w=10, groups=2, windows=(52, 51)), dict(w=20, groups=4, windows=(27, 25)))
for _b in BRANCHES:
    _b["shift"] = _b["w"] // 2
    _b["slots"] = P // _b["groups"]
    _b["nh"] = 8 // _b["groups"]
    _b["cols"] = 3 * HD * _b["nh"]
    _b["chunks"] = -(-_b["w"] // 4)
    _b["first"] = (_b["shift"], _b["shift"] - _b["windows"][0] * _b["w"])
XCOLS = 640
MARGIN = BRANCHES[1]["shift"]

V_N2, V_B1, V_UPB, V_PB, V_N1, V_EB1 = 0, 1, 3, 4, 5, 7
NV = V_EB1 + EX * NC
R_DB, R_B2, R_RB = 0, DI, DI + D
NR = R_RB + E


def spread(ap, axis, n):
    ap = ap.unsqueeze(axis)
    shape = list(ap.shape)
    shape[axis] = n
    return ap.broadcast_to(shape)


def decoder_layer(nc, x, x_t, ctx_t, wq, wq_t, down_w, centre, identity, causal, up_w, proj_t, qkv_w,
                  bias10, bias20, fold, ffn_w1, ffn_w2, router_w, tri, cols, rows, moe_w1, moe_w2, moe_b2, out):
    with ExitStack() as stack:
        def sb(name, shape, dt=F32):
            return stack.enter_context(nc.sbuf_tensor(name, shape, dt))

        def sem(name):
            return stack.enter_context(nc.semaphore(name))

        ps = stack.enter_context(nc.psum_tensor("ps", [P, 8, 512], F32))

        x_sb = sb("x_sb", [P, NT, D])
        xT_sb = sb("xT_sb", [P, T])
        ctxT_sb = sb("ctxT_sb", [P, T])
        wq_sb = sb("wq_sb", [P, D])
        wqT_sb = sb("wqT_sb", [P, D])
        down_sb = sb("down_sb", [P, DI])
        centre_sb = sb("centre_sb", [P, P])
        ident = sb("ident", [P, P])
        causal_sb = sb("causal_sb", [P, P])
        up_sb = sb("up_sb", [C, 2, D])
        upb_sb = sb("upb_sb", [DI, D])
        projT_sb = sb("projT_sb", [C, 2, P])
        qkvw_sb = sb("qkvw_sb", [C + 1, 2, QKV])
        fold_sb = sb("fold_sb", [P, 96])
        ffn_w1_sb = sb("ffn_w1_sb", [P, HID])
        ffn_w2_sb = sb("ffn_w2_sb", [P, NC, D])
        router_sb = sb("router_sb", [P, E])
        tri_sb = sb("tri_sb", [P, E * E])
        cols_sb = sb("cols_sb", [P, NV])
        rows_sb = sb("rows_sb", [P, NR])
        moe_w1_sb = sb("moe_w1_sb", [P, EX, HID])
        moe_w2_sb = sb("moe_w2_sb", [P, EX, NC, D])
        moe_b2_sb = sb("moe_b2_sb", [EX, D])
        elems = [b["w"] * b["nh"] * b["w"] for b in BRANCHES]
        relb = [[sb(f"relb{b['w']}_{h}", [P, n]) for h in range(2)] for b, n in zip(BRANCHES, elems)]

        ident16 = sb("ident16", [P, P], BF16)
        causal16 = sb("causal16", [P, P], BF16)
        minus_half = sb("minus_half", [P, NT])
        downc = sb("downc", [P, DI])
        pu = [sb(f"pu{b['w']}", [P, 4, D]) for b in BRANCHES]
        out_bias = sb("out_bias", [P, 1])

        st = sb("st", [P, NT, 6])
        mv = sb("mv", [P, NT, 2])
        rstd0 = sb("rstd0", [P, NT])
        xn = sb("xn", [P, NT, D])
        xs = sb("xs", [P, NT, D])
        xi = sb("xi", [P, NT, DI])
        xi2 = sb("xi2", [P, NT, DI])
        ss = sb("ss", [P, NT])
        rstd1 = sb("rstd1", [P, NT])
        winT = [sb(f"winT{b['w']}", [C + 1, HALVES * XCOLS]) for b in BRANCHES]
        qkv = [[sb(f"qkv{b['w']}_{h}", [P, b["w"], b["cols"]]) for h in range(2)] for b in BRANCHES]
        prod = sb("prod", [P, HD, elems[1]])
        sc = [sb(f"sc{b['w']}", [P, n]) for b, n in zip(BRANCHES, elems)]
        stat = [sb(f"stat{b['w']}", [P, 3, b["w"] * b["nh"]]) for b in BRANCHES]
        ou = [sb(f"ou{b['w']}", [P, HD, b["w"] * b["nh"]]) for b in BRANCHES]
        ox = [sb(f"ox{b['w']}", [P, 4 * b["chunks"], C]) for b in BRANCHES]
        ot = [sb(f"ot{b['w']}", [P, b["chunks"] * b["slots"]]) for b in BRANCHES]
        xcT = sb("xcT", [P, 1100])

        xp = sb("xp", [P, TH, D])
        sq = sb("sq", [P, TH, D])
        ss2 = sb("ss2", [P, TH])
        rstd2 = sb("rstd2", [P, TH])
        hT = sb("hT", [P, CH])
        hid = sb("hid", [P, 2, NC, CH])
        x1 = sb("x1", [P, TH, D])
        st2 = sb("st2", [P, TH, 6])
        mv2 = sb("mv2", [P, TH, 2])
        rstd3 = sb("rstd3", [P, TH])
        xl = sb("xl", [P, TH, D])
        xlT = sb("xlT", [P, CH])
        kT = sb("kT", [P, T])
        gT = sb("gT", [P, T])
        v_sb = sb("v_sb", [P, NT, D])
        pr = sb("pr", [P, 2, T])
        prT = sb("prT", [P, 2, T])
        nmx = sb("nmx", [P, NT])
        den = sb("den", [P, NT])
        rden = sb("rden", [P, NT])
        x2 = sb("x2", [P, TH, D])
        xfT = sb("xfT", [P, CH])
        lg = sb("lg", [P, TH, E])
        lmx = sb("lmx", [P, TH])
        lsum = sb("lsum", [P, TH])
        gt = sb("gt", [P, TH, E * E])
        eq = sb("eq", [P, TH, E * E])
        wts = sb("wts", [P, TH, EX])
        wT = sb("wT", [EX, CH])
        acc = sb("acc", [P, NT, D])

        ld_down = sem("ld_down")
        ld_xT = sem("ld_xT")
        ld_x = sem("ld_x")
        ld_vec = sem("ld_vec")
        ld_proj = sem("ld_proj")
        ld_ctx = sem("ld_ctx")
        ld_qkvw = sem("ld_qkvw")
        ld_bias = sem("ld_bias")
        ld_ffn = sem("ld_ffn")
        ld_moe = sem("ld_moe")
        ld_router = sem("ld_router")
        stored = sem("stored")
        dve_step = sem("dve_step")
        pool_step = sem("pool_step")
        cleared = sem("cleared")
        casts = sem("casts")
        relb_ready = sem("relb_ready")
        setup_ps = sem("setup_ps")
        downc_ready = sem("downc_ready")
        pu_ready = sem("pu_ready")
        out_bias_ready = sem("out_bias_ready")
        stats0 = sem("stats0")
        rstd0_ready = sem("rstd0_ready")
        xi_ps = sem("xi_ps")
        xi_taken = sem("xi_taken")
        ss_ready = sem("ss_ready")
        rstd1_ready = sem("rstd1_ready")
        xin_ready = sem("xin_ready")
        xn_ready = sem("xn_ready")
        win_ps = [sem("win10_ps"), sem("win20_ps")]
        win_ready = [sem("win10_ready"), sem("win20_ready")]
        qkv_ps = [sem("qkv10_ps"), sem("qkv20_ps")]
        qkv_act = [sem("qkv10_act"), sem("qkv20_act")]
        sc_ready = [sem("sc10_ready"), sem("sc20_ready")]
        exp_ready = [sem("exp10_ready"), sem("exp20_ready")]
        ox_ready = [sem("ox10_ready"), sem("ox20_ready")]
        ot_ps = [sem("ot10_ps"), sem("ot20_ps")]
        ot_ready = [sem("ot10_ready"), sem("ot20_ready")]
        xc_ps = [sem("xc10_ps"), sem("xc20_ps")]
        xc20_ready = sem("xc20_ready")
        xc_ready = sem("xc_ready")
        xc_tok_ps = sem("xc_tok_ps")
        xp_ready = sem("xp_ready")
        xs_ready = sem("xs_ready")
        ss2_ready = sem("ss2_ready")
        rstd2_ready = sem("rstd2_ready")
        h_ready = sem("h_ready")
        hT_ps = sem("hT_ps")
        hT_ready = sem("hT_ready")
        ffn_h_ps = sem("ffn_h_ps")
        ffn_h_ready = sem("ffn_h_ready")
        ffn_ps = sem("ffn_ps")
        x1_ready = sem("x1_ready")
        stats2 = sem("stats2")
        rstd3_ready = sem("rstd3_ready")
        xl_ready = sem("xl_ready")
        xlT_ps = sem("xlT_ps")
        xlT_ready = sem("xlT_ready")
        k_ps = sem("k_ps")
        k_ready = sem("k_ready")
        g_ps = sem("g_ps")
        g_ready = sem("g_ready")
        v_ps = sem("v_ps")
        v_ready = sem("v_ready")
        s_ps = sem("s_ps")
        max_ready = sem("max_ready")
        p_ready = sem("p_ready")
        pT_ps = sem("pT_ps")
        pT_act = sem("pT_act")
        pT_dve = sem("pT_dve")
        pv_ps = sem("pv_ps")
        x2_ready = sem("x2_ready")
        stats3 = sem("stats3")
        rstd4_ready = sem("rstd4_ready")
        xf_ready = sem("xf_ready")
        xfT_ps = sem("xfT_ps")
        xfT_ready = sem("xfT_ready")
        lg_ps = sem("lg_ps")
        lg_ready = sem("lg_ready")
        lexp_ready = sem("lexp_ready")
        wts_ready = sem("wts_ready")
        wT_ps = sem("wT_ps")
        wT_ready = sem("wT_ready")
        b2_ps = sem("b2_ps")
        acc_start = sem("acc_start")
        moe_h_ps = sem("moe_h_ps")
        moe_h_ready = sem("moe_h_ready")
        moe_ps = sem("moe_ps")
        moe_taken = sem("moe_taken")

        block = stack.enter_context(nc.Block())

        def qkv_bank(b, h):
            return 4 * h + 1 - b

        def pT_banks(t):
            if t < 4:
                return [("act" if t % 2 else "dve", 4, t + 1)]
            return [("dve", 4, 4), ("act", 5, t - 3)]

        def pT_count(t, engine):
            return sum(e == engine for u in range(t + 1) for e, _, _ in pT_banks(u))

        @block.sync
        def _(sp):
            sp.dma_start(down_sb[:], down_w).then_inc(ld_down, 16)
            sp.dma_start(centre_sb[:], centre).then_inc(ld_down, 16)
            sp.dma_start(xT_sb[:], x_t).then_inc(ld_xT, 16)
            sp.dma_start(rows_sb[:], rows.partition_broadcast(P)).then_inc(ld_vec, 16)
            sp.dma_start(cols_sb[:], cols).then_inc(ld_vec, 16)
            sp.dma_start(ident[:], identity).then_inc(ld_vec, 16)
            sp.dma_start(qkvw_sb[:], qkv_w).then_inc(ld_qkvw, 16)
            sp.dma_start(projT_sb[:], proj_t).then_inc(ld_proj, 16)
            sp.dma_start(up_sb[:], up_w.rearrange("(b c) n -> c b n", b=2)).then_inc(ld_proj, 16)
            sp.dma_start(upb_sb[:], up_w).then_inc(ld_proj, 16)
            sp.dma_start(relb[1][1][:], bias20).then_inc(ld_bias, 16)
            sp.dma_start(relb[0][1][:], bias10).then_inc(ld_bias, 16)
            sp.dma_start(fold_sb[:], fold).then_inc(ld_ffn, 16)
            sp.dma_start(ffn_w1_sb[:], ffn_w1).then_inc(ld_ffn, 16)
            sp.dma_start(ffn_w2_sb[:], ffn_w2.rearrange("(c p) n -> p c n", p=P)).then_inc(ld_ffn, 16)
            sp.dma_start(moe_w1_sb[:], moe_w1.rearrange("e p n -> p e n")).then_inc(ld_moe, 16)
            sp.dma_start(moe_w2_sb[:], moe_w2.rearrange("e (c p) n -> p e c n", p=P)).then_inc(ld_moe, 16)
            sp.dma_start(moe_b2_sb[:], moe_b2).then_inc(ld_moe, 16)
            out_v = out.rearrange("o (t p) d -> (o p) t d", p=P)
            for h in range(HALVES):
                for t in range(TH):
                    sp.wait_ge(moe_taken, (h * EX + EX - 1) * TH + t + 1)
                    sp.dma_start(out_v[:, h * TH + t, :], acc[:, h * TH + t, :]).then_inc(stored, 16)
            sp.wait_ge(stored, 16 * NT)

        @block.gpsimd
        def _(pool):
            steps = [0]

            def step(ins):
                steps[0] += 1
                ins.then_inc(pool_step, 1)

            def settle():
                pool.wait_ge(pool_step, steps[0])

            pool.dma_start(x_sb[:], x.rearrange("o (t p) d -> (o p) t d", p=P)).then_inc(ld_x, 16)
            pool.dma_start(wqT_sb[:], wq_t).then_inc(ld_ctx, 16)
            pool.dma_start(ctxT_sb[:], ctx_t).then_inc(ld_ctx, 16)
            pool.dma_start(wq_sb[:], wq).then_inc(ld_ctx, 16)
            pool.dma_start(causal_sb[:], causal).then_inc(ld_router, 16)
            pool.dma_start(router_sb[:], router_w).then_inc(ld_router, 16)
            pool.dma_start(tri_sb[:], tri).then_inc(ld_router, 16)
            step(pool.memset(minus_half[:], -0.5))
            pool.memset(pu[0][:], 0.0).then_inc(cleared, 1)
            pool.memset(pu[1][:], 0.0).then_inc(cleared, 1)
            for b in (1, 0):
                pool.memset(winT[b][0:C, :], 0.0).then_inc(cleared, 1)
            pool.wait_ge(cleared, 4)
            pool.memset(winT[1][C:C + 1, :], 1.0).then_inc(cleared, 1)
            pool.wait_ge(cleared, 5)
            pool.memset(winT[0][C:C + 1, :], 1.0).then_inc(cleared, 1)
            pool.wait_ge(cleared, 6)
            pool.memset(ox[1][:], 0.0).then_inc(cleared, 1)
            pool.memset(ox[0][:], 0.0).then_inc(cleared, 1)
            pool.memset(wts[:], 1.0).then_inc(cleared, 1)

            def rstd(dst, src, scale, eps, ready):
                step(pool.tensor_scalar(dst, src, scale, eps, ALU.mult, ALU.add))
                settle()
                pool.tensor_tensor(dst, dst, minus_half[:, 0:dst.shape[1]], ALU.pow).then_inc(ready, 1)

            pool.wait_ge(stats0, NT)
            rstd(rstd0[:], mv[:, :, 1], 1.0, 1e-5, rstd0_ready)
            pool.wait_ge(ss_ready, 1)
            rstd(rstd1[:], ss[:], 1.0 / DI, 1e-6, rstd1_ready)

            pool.wait_ge(ld_bias, 32)
            for b in (1, 0):
                step(pool.tensor_copy(relb[b][0][:], relb[b][1][:]))
            settle()
            parts = 0
            for b in (1, 0):
                br = BRANCHES[b]
                w, s = br["w"], br["shift"]
                for g in range(br["groups"]):
                    p = g * br["slots"]
                    v = relb[b][0][p:p + 1, :].rearrange("p (i h j) -> p i h j", i=w, h=br["nh"])
                    pool.tensor_scalar_add(v[:, 0:s, :, s:w], v[:, 0:s, :, s:w], -100.0).then_inc(relb_ready, 1)
                    parts += 1
                    pool.wait_ge(relb_ready, parts)
                    pool.tensor_scalar_add(v[:, s:w, :, 0:s], v[:, s:w, :, 0:s], -100.0).then_inc(relb_ready, 1)
                    parts += 1
                    pool.wait_ge(relb_ready, parts)
            pool.wait_ge(ld_router, 48)
            pool.wait_ge(ld_vec, 48)
            pool.tensor_copy(ident16[:], ident[:]).then_inc(casts, 1)
            pool.tensor_copy(causal16[:], causal_sb[:]).then_inc(casts, 1)

            for h in range(HALVES):
                hs = slice(h * TH, (h + 1) * TH)
                pool.wait_ge(ss2_ready, h + 1)
                rstd(rstd2[:], ss2[:], 1.0 / D, 1e-6, rstd2_ready)
                step(pool.tensor_tensor(xs[:, hs, :], x_sb[:, hs, :], xp[:], ALU.add))
                settle()
                pool.tensor_tensor(xs[:, hs, :], xs[:, hs, :],
                                   spread(rows_sb[:, R_B2:R_B2 + D], 1, TH), ALU.add).then_inc(xs_ready, 1)
                pool.wait_ge(stats2, TH * (h + 1))
                rstd(rstd3[:], mv2[:, :, 1], 1.0, 1e-5, rstd3_ready)
                pool.wait_ge(stats3, TH * (h + 1))
                rstd(rstd3[:], mv2[:, :, 1], 1.0, 1e-5, rstd4_ready)

        @block.scalar
        def _(act):
            act.wait_ge(setup_ps, 1)
            act.activation(downc[:], ps[:, 0, 0:DI], ACT.Copy).then_inc(downc_ready, 1)
            act.wait_ge(setup_ps, 2)
            act.wait_ge(cleared, 2)
            for b in range(2):
                for g in range(4):
                    r = slice(32 * g, 32 * g + 32)
                    act.activation(pu[b][r, g, :], ps[r, 0, 128 + 128 * b:256 + 128 * b], ACT.Copy).then_inc(pu_ready, 1)
            act.wait_ge(ld_vec, 48)
            act.activation(out_bias[:], ps[:, 0, 400:401], ACT.Identity,
                           bias=cols_sb[:, V_UPB:V_UPB + 1]).then_inc(out_bias_ready, 1)
            act.wait_ge(k_ps, 1)
            act.activation(kT[:].rearrange("p (a n) -> p a n", a=2), ps[:, 6:8, :], ACT.Copy).then_inc(k_ready, 1)

            def window_cols(b):
                act.wait_ge(win_ps[b], 1)
                act.wait_ge(cleared, 6)
                src = ps[0:C, 2 + 2 * b:4 + 2 * b, :].rearrange("p a n -> p (a n)")
                a, z = BRANCHES[b]["first"]
                cut = BRANCHES[b]["windows"][0] * BRANCHES[b]["w"] - a
                act.activation(winT[b][0:C, a:a + cut], src[:, 0:cut], ACT.Copy,
                               scale=cols_sb[0:C, V_N1 + b:V_N1 + b + 1]).then_inc(win_ready[b], 1)
                act.activation(winT[b][0:C, XCOLS + z + cut:XCOLS + z + T], src[:, cut:T], ACT.Copy,
                               scale=cols_sb[0:C, V_N1 + b:V_N1 + b + 1]).then_inc(win_ready[b], 1)

            window_cols(0)

            def qkv_copy(b, h):
                br = BRANCHES[b]
                act.wait_ge(qkv_ps[b], h + 1)
                src = ps[:, qkv_bank(b, h), 0:br["w"] * br["cols"]].rearrange("p (i n) -> p i n", i=br["w"])
                act.activation(qkv[b][h][:], src, ACT.Copy).then_inc(qkv_act[b], 1)

            qkv_copy(1, 0)
            qkv_copy(0, 0)
            act.wait_ge(g_ps, 1)
            act.activation(gT[:].rearrange("p (a n) -> p a n", a=2), ps[:, 6:8, :], ACT.Copy,
                           scale=float(D) ** -0.5).then_inc(g_ready, 1)
            act.wait_ge(v_ps, 1)
            act.activation(v_sb[:].rearrange("p (a t) d -> p a (t d)", a=2), ps[:, 6:8, :], ACT.Copy).then_inc(v_ready, 1)
            qkv_copy(1, 1)
            qkv_copy(0, 1)

            def window_exp(b, h):
                act.wait_ge(sc_ready[b], h + 1)
                act.activation(sc[b][:], sc[b][:], ACT.Exp).then_inc(exp_ready[b], 1)

            def ot_copy(b, h):
                act.wait_ge(ot_ps[b], h + 1)
                if h:
                    act.wait_ge(xc_ps[b], h)
                act.activation(ot[b][:], ps[:, 7 - b, 0:ot[b].shape[1]], ACT.Copy).then_inc(ot_ready[b], 1)

            def xc20_copy(h):
                br = BRANCHES[1]
                act.wait_ge(xc_ps[1], h + 1)
                n = br["windows"][h]
                at = MARGIN - br["first"][h]
                for a in range(2):
                    src = ps[:, a, :].rearrange("p (i c s) -> p i c s", i=2, s=br["slots"])
                    src = src[:, :, 0:br["chunks"], 0:n]
                    dst = xcT[:, at:at + n * br["w"]].rearrange("p (s c i) -> p i c s", c=br["chunks"], i=4)
                    act.activation(dst[:, 2 * a:2 * a + 2], src, ACT.Identity,
                                   bias=out_bias[:, 0:1]).then_inc(xc20_ready, 1)

            def hT_copy(h):
                act.wait_ge(hT_ps, h + 1)
                act.activation(hT[:], ps[:, 5, :], ACT.Copy, scale=cols_sb[:, V_N2:V_N2 + 1]).then_inc(hT_ready, 1)

            def ffn_gelu(h):
                for c in range(NC):
                    act.wait_ge(ffn_h_ps, h * NC + c + 1)
                    act.activation(hid[:, 0, c, :], ps[:, c, :], ACT.Gelu,
                                   bias=cols_sb[:, V_B1 + c:V_B1 + c + 1]).then_inc(ffn_h_ready, 1)

            def xlT_copy(h):
                act.wait_ge(xlT_ps, h + 1)
                act.activation(xlT[:], ps[:, 5, :], ACT.Copy).then_inc(xlT_ready, 1)

            def softmax(t):
                act.wait_ge(max_ready, t + 1)
                if t >= 2:
                    act.wait_ge(pT_ps, t - 1)
                n = P * (t + 1)
                src = ps[:, 2 * (t % 2):2 * (t % 2) + 2, :].rearrange("p a n -> p (a n)")[:, 0:n]
                act.activation(pr[:, t % 2, 0:n], src, ACT.Exp, bias=nmx[:, t:t + 1],
                               accum_out=den[:, t:t + 1]).then_inc(p_ready, 1)

            def pT_copy(t):
                for engine, bank, n in pT_banks(t):
                    if engine == "act":
                        act.wait_ge(pT_ps, t + 1)
                        if t >= 2:
                            act.wait_ge(pv_ps, t - 1)
                        at = (bank - 4) * 512
                        act.activation(prT[:, t % 2, at:at + n * P], ps[:, bank, 0:n * P], ACT.Copy).then_inc(pT_act, 1)

            def xfT_copy(h):
                act.wait_ge(xfT_ps, h + 1)
                if h:
                    act.wait_ge(moe_h_ps, h * EX * NC)
                act.activation(xfT[:], ps[:, 4, :], ACT.Copy).then_inc(xfT_ready, 1)

            def router_exp(h):
                act.wait_ge(lg_ready, h + 1)
                act.activation(lg[:], lg[:], ACT.Exp).then_inc(lexp_ready, 1)

            def wT_copy(h):
                act.wait_ge(wT_ps, h + 1)
                act.activation(wT[:], ps[0:EX, 6, :], ACT.Copy).then_inc(wT_ready, 1)

            def moe_gelu(h, e):
                k = h * EX + e
                for c in range(NC):
                    act.wait_ge(moe_h_ps, k * NC + c + 1)
                    if k >= 2:
                        act.wait_ge(moe_ps, TH * (k - 1))
                    i = V_EB1 + e * NC + c
                    act.activation(hid[:, k % 2, c, :], ps[:, 2 * (k % 2) + c, :], ACT.Gelu,
                                   bias=cols_sb[:, i:i + 1]).then_inc(moe_h_ready, 1)

            for h in range(HALVES):
                if h == 0:
                    window_exp(1, 0)
                    window_exp(0, 0)
                ot_copy(1, h)
                xc20_copy(h)
                ot_copy(0, h)
                hT_copy(h)
                ffn_gelu(h)
                xlT_copy(h)
                for t in range(h * TH, (h + 1) * TH):
                    softmax(t)
                    if t > h * TH:
                        pT_copy(t - 1)
                pT_copy((h + 1) * TH - 1)
                xfT_copy(h)
                router_exp(h)
                wT_copy(h)
                for e in range(EX):
                    moe_gelu(h, e)
                    if h == 0 and e == 2:
                        window_exp(1, 1)
                    if h == 0 and e == 4:
                        window_exp(0, 1)

        @block.vector
        def _(dve):
            steps = [0]

            def step(ins):
                steps[0] += 1
                ins.then_inc(dve_step, 1)

            def settle():
                dve.wait_ge(dve_step, steps[0])

            dve.wait_ge(ld_x, 16)
            for t in range(NT):
                step(dve.bn_stats(st[:, t, :], x_sb[:, t, :]))
            settle()
            for t in range(NT):
                dve.bn_aggr(mv[:, t, :], st[:, t, :]).then_inc(stats0, 1)
            dve.wait_ge(rstd0_ready, 1)
            dve.wait_ge(xi_ps, 1)
            dve.wait_ge(ld_vec, 48)
            dve.tensor_tensor(xi[:], ps[:, 1, :].rearrange("p (t n) -> p t n", t=NT),
                              spread(rstd0[:], 2, DI), ALU.mult).then_inc(xi_taken, 1)
            dve.wait_ge(xi_taken, 1)
            step(dve.tensor_tensor(xi[:], xi[:], spread(rows_sb[:, R_DB:R_DB + DI], 1, NT), ALU.add))
            settle()
            step(dve.tensor_tensor(xi2[:], xi[:], xi[:], ALU.mult))
            settle()
            dve.tensor_reduce(ss[:], xi2[:], AX.X, ALU.add).then_inc(ss_ready, 1)
            dve.wait_ge(stats0, NT)
            for t in range(NT):
                step(dve.tensor_scalar(xn[:, t, :], x_sb[:, t, :], mv[:, t, 0:1], rstd0[:, t:t + 1],
                                       ALU.subtract, ALU.mult))
            dve.wait_ge(rstd1_ready, 1)
            dve.tensor_tensor(xi2[:], xi[:], spread(rstd1[:], 2, DI), ALU.mult).then_inc(xin_ready, 1)
            dve.wait_ge(win_ps[1], 1)
            dve.wait_ge(cleared, 6)
            src = ps[0:C, 4:6, :].rearrange("p a n -> p (a n)")
            a, z = BRANCHES[1]["first"]
            cut = BRANCHES[1]["windows"][0] * BRANCHES[1]["w"] - a
            n1 = cols_sb[0:C, V_N1 + 1:V_N1 + 2]
            dve.tensor_scalar(winT[1][0:C, a:a + cut], src[:, 0:cut], n1, None, ALU.mult).then_inc(win_ready[1], 1)
            dve.tensor_scalar(winT[1][0:C, XCOLS + z + cut:XCOLS + z + T], src[:, cut:T], n1, None,
                              ALU.mult).then_inc(win_ready[1], 1)

            def heads(ap, nh, d):
                return ap.rearrange("p i (h d) -> p i h d", d=HD)[:, :, :, d]

            def window_scores(b, h):
                br = BRANCHES[b]
                w, nh, n = br["w"], br["nh"], elems[b]
                dve.wait_ge(qkv_act[b], h + 1)
                t = qkv[b][h]
                shape = "p (i h j) -> p i h j"
                for d in range(HD):
                    q = heads(t[:, :, 0:HD * nh], nh, d)
                    k = heads(t[:, :, HD * nh:2 * HD * nh], nh, d).rearrange("p j h -> p h j")
                    step(dve.tensor_tensor(prod[:, d, 0:n].rearrange(shape, i=w, h=nh),
                                           spread(q, 3, w), spread(k, 1, w), ALU.mult))
                settle()
                step(dve.tensor_tensor(prod[:, 0:2, 0:n], prod[:, 0:2, 0:n], prod[:, 2:4, 0:n], ALU.add))
                settle()
                step(dve.tensor_tensor(prod[:, 0, 0:n], prod[:, 0, 0:n], prod[:, 1, 0:n], ALU.add))
                settle()
                if h == 0:
                    dve.wait_ge(relb_ready, 8 if b else 12)
                step(dve.scalar_tensor_tensor(sc[b][:], prod[:, 0, 0:n], float(HD) ** -0.5, relb[b][h][:],
                                              ALU.mult, ALU.add))
                settle()
                rows3 = sc[b][:].rearrange("p (r j) -> p r j", j=w)
                step(dve.tensor_reduce(stat[b][:, 0, :], rows3, AX.X, ALU.max))
                settle()
                dve.tensor_tensor(rows3, rows3, spread(stat[b][:, 0, :], 2, w), ALU.subtract).then_inc(sc_ready[b], 1)

            def window_values(b, h):
                br = BRANCHES[b]
                w, nh, n = br["w"], br["nh"], elems[b]
                dve.wait_ge(exp_ready[b], h + 1)
                rows3 = sc[b][:].rearrange("p (r j) -> p r j", j=w)
                step(dve.tensor_reduce(stat[b][:, 1, :], rows3, AX.X, ALU.add))
                settle()
                step(dve.reciprocal(stat[b][:, 2, :], stat[b][:, 1, :]))
                t = qkv[b][h]
                shape = "p (i h j) -> p i h j"
                for d in range(HD):
                    v = heads(t[:, :, 2 * HD * nh:3 * HD * nh], nh, d).rearrange("p j h -> p h j")
                    step(dve.tensor_tensor(prod[:, d, 0:n].rearrange(shape, i=w, h=nh),
                                           sc[b][:].rearrange(shape, i=w, h=nh), spread(v, 1, w), ALU.mult))
                settle()
                step(dve.tensor_reduce(ou[b][:], prod[:, :, 0:n].rearrange("p d (r j) -> p d r j", j=w), AX.X, ALU.add))
                settle()
                dve.wait_ge(cleared, 9)
                if h:
                    dve.wait_ge(ot_ps[b], h)
                for g in range(br["groups"]):
                    r = slice(g * br["slots"], (g + 1) * br["slots"])
                    dst = ox[b][r, 0:w, g * HD * nh:(g + 1) * HD * nh].rearrange("p i (h d) -> p d i h", d=HD)
                    src = ou[b][r, :, :].rearrange("p d (i h) -> p d i h", h=nh)
                    rec = spread(stat[b][r, 2, :].rearrange("p (i h) -> p i h", h=nh), 1, HD)
                    dve.tensor_tensor(dst, src, rec, ALU.mult).then_inc(ox_ready[b], 1)

            def xc_add(h):
                br = BRANCHES[0]
                dve.wait_ge(xc_ps[0], h + 1)
                dve.wait_ge(xc20_ready, 2 * (h + 1))
                n = br["windows"][h]
                at = MARGIN - br["first"][h]
                for a in range(2):
                    chunks = br["chunks"] - a
                    src = ps[:, 2 + a, :].rearrange("p (i c s) -> p i c s", i=2, s=br["slots"])
                    dst = xcT[:, at:at + (n + 1) * br["w"]]
                    for i in range(2):
                        j = 2 * a + i
                        d = dst[:, j:j + n * br["w"]].rearrange("p (s k) -> p k s", k=br["w"])[:, 0:4 * chunks - 3:4, :]
                        dve.tensor_tensor(d, src[:, i, 0:chunks, 0:n], d, ALU.add).then_inc(xc_ready, 1)

            def xp_and_h(h):
                hs = slice(h * TH, (h + 1) * TH)
                dve.wait_ge(xc_tok_ps, h + 1)
                if h:
                    dve.wait_ge(xs_ready, h)
                dve.tensor_tensor(xp[:], ps[:, 4, :].rearrange("p (t d) -> p t d", t=TH), xn[:, hs, :],
                                  ALU.add).then_inc(xp_ready, 1)
                dve.wait_ge(xp_ready, h + 1)
                step(dve.tensor_tensor(sq[:], xp[:], xp[:], ALU.mult))
                settle()
                dve.tensor_reduce(ss2[:], sq[:], AX.X, ALU.add).then_inc(ss2_ready, 1)
                dve.wait_ge(rstd2_ready, h + 1)
                dve.tensor_tensor(sq[:], xp[:], spread(rstd2[:], 2, D), ALU.mult).then_inc(h_ready, 1)

            def layernorm(src, stats, count, rstd_ready, ready):
                for t in range(TH):
                    step(dve.bn_stats(st2[:, t, :], src[:, t, :]))
                settle()
                for t in range(TH):
                    dve.bn_aggr(mv2[:, t, :], st2[:, t, :]).then_inc(stats, 1)
                dve.wait_ge(stats, TH * (count + 1))
                dve.wait_ge(rstd_ready, count + 1)
                for t in range(TH):
                    dve.tensor_scalar(xl[:, t, :], src[:, t, :], mv2[:, t, 0:1], rstd3[:, t:t + 1],
                                      ALU.subtract, ALU.mult).then_inc(ready, 1)

            def x1_and_norm(h):
                dve.wait_ge(ffn_ps, h + 1)
                dve.wait_ge(xs_ready, h + 1)
                dve.tensor_tensor(x1[:], ps[:, 4, :].rearrange("p (t d) -> p t d", t=TH),
                                  xs[:, h * TH:(h + 1) * TH, :], ALU.add).then_inc(x1_ready, 1)
                dve.wait_ge(x1_ready, h + 1)
                layernorm(x1, stats2, h, rstd3_ready, xl_ready)

            def row_max(t):
                dve.wait_ge(s_ps, t + 1)
                src = ps[:, 2 * (t % 2):2 * (t % 2) + 2, :].rearrange("p a n -> p (a n)")[:, 0:P * (t + 1)]
                dve.tensor_reduce(nmx[:, t:t + 1], src, AX.X, ALU.max, negate=True).then_inc(max_ready, 1)

            def pT_copy(t):
                for engine, bank, n in pT_banks(t):
                    if engine == "dve":
                        dve.wait_ge(pT_ps, t + 1)
                        if t >= 2:
                            dve.wait_ge(pv_ps, t - 1)
                        at = (bank - 4) * 512
                        dve.tensor_copy(prT[:, t % 2, at:at + n * P], ps[:, bank, 0:n * P]).then_inc(pT_dve, 1)

            def x2_tile(t):
                dve.wait_ge(p_ready, t + 1)
                step(dve.reciprocal(rden[:, t:t + 1], den[:, t:t + 1]))
                settle()
                dve.wait_ge(pv_ps, t + 1)
                dve.scalar_tensor_tensor(x2[:, t % TH, :], ps[:, 6 + t % 2, 0:D], rden[:, t:t + 1],
                                         x1[:, t % TH, :], ALU.mult, ALU.add).then_inc(x2_ready, 1)

            def router(h):
                dve.wait_ge(lg_ps, h + 1)
                logits = ps[:, 5, 0:TH * E].rearrange("p (t e) -> p t e", t=TH)
                step(dve.tensor_tensor(lg[:], logits, spread(rows_sb[:, R_RB:R_RB + E], 1, TH), ALU.add))
                settle()
                step(dve.tensor_reduce(lmx[:], lg[:], AX.X, ALU.max))
                settle()
                dve.tensor_tensor(lg[:], lg[:], spread(lmx[:], 2, E), ALU.subtract).then_inc(lg_ready, 1)
                dve.wait_ge(lexp_ready, h + 1)
                step(dve.tensor_reduce(lsum[:], lg[:], AX.X, ALU.add))
                settle()
                step(dve.reciprocal(lmx[:], lsum[:]))
                settle()
                step(dve.tensor_tensor(lg[:], lg[:], spread(lmx[:], 2, E), ALU.mult))
                settle()
                for op, dst in ((ALU.is_gt, gt), (ALU.is_equal, eq)):
                    step(dve.tensor_tensor(dst[:].rearrange("p t (e f) -> p t e f", e=E), spread(lg[:], 2, E),
                                           spread(lg[:], 3, E), op))
                settle()
                step(dve.tensor_tensor(eq[:], eq[:], spread(tri_sb[:], 1, TH), ALU.mult))
                settle()
                step(dve.tensor_tensor(gt[:], gt[:], eq[:], ALU.add))
                settle()
                step(dve.tensor_reduce(eq[:, :, 0:E], gt[:].rearrange("p t (e f) -> p t e f", e=E), AX.X, ALU.add))
                settle()
                if h:
                    dve.wait_ge(moe_taken, h * EX * TH)
                dve.scalar_tensor_tensor(wts[:, :, 0:E], eq[:, :, 0:E], 2.0, lg[:], ALU.is_lt, ALU.mult)\
                   .then_inc(wts_ready, 1)

            def acc_begin(h):
                dve.wait_ge(b2_ps, h + 1)
                dve.tensor_tensor(acc[:, h * TH:(h + 1) * TH, :], ps[:, 7, :].rearrange("p (t d) -> p t d", t=TH),
                                  x2[:], ALU.add).then_inc(acc_start, 1)
                dve.wait_ge(acc_start, h + 1)

            def moe_add(h, e):
                k = h * EX + e
                if e == 0:
                    dve.wait_ge(wts_ready, h + 1)
                else:
                    dve.wait_ge(moe_taken, k * TH)
                dve.wait_ge(moe_ps, (k + 1) * TH)
                for t in range(TH):
                    g = h * TH + t
                    dve.scalar_tensor_tensor(acc[:, g, :], ps[:, 4 + k % 2, t * D:(t + 1) * D], wts[:, t, e:e + 1],
                                             acc[:, g, :], ALU.mult, ALU.add).then_inc(moe_taken, 1)

            for h in range(HALVES):
                if h == 0:
                    window_scores(1, 0)
                    window_scores(0, 0)
                    window_values(1, 0)
                    window_values(0, 0)
                xc_add(h)
                xp_and_h(h)
                x1_and_norm(h)
                row_max(h * TH)
                for t in range(h * TH, (h + 1) * TH):
                    if t + 1 < (h + 1) * TH:
                        row_max(t + 1)
                    pT_copy(t)
                    x2_tile(t)
                dve.wait_ge(x2_ready, TH * (h + 1))
                layernorm(x2, stats3, h, rstd4_ready, xf_ready)
                router(h)
                acc_begin(h)
                for e in range(EX):
                    moe_add(h, e)
                    if h == 0 and e == 0:
                        window_scores(1, 1)
                    if h == 0 and e == 2:
                        window_scores(0, 1)
                    if h == 0 and e == 3:
                        window_values(1, 1)
                    if h == 0 and e == 5:
                        window_values(0, 1)

        @block.tensor
        def _(pe):
            def mm(dst, lhs, rhs, start=True, stop=True):
                return pe.matmul(dst, lhs, rhs, start=start, stop=stop)

            pe.wait_ge(ld_down, 32)
            mm(ps[:, 0, 0:DI], centre_sb[:], down_sb[:]).then_inc(setup_ps, 1)
            pe.wait_ge(ld_xT, 16)
            pe.wait_ge(downc_ready, 1)
            for t in range(NT):
                last = mm(ps[:, 1, t * DI:(t + 1) * DI], xT_sb[:, t * P:(t + 1) * P], downc[:])
            last.then_inc(xi_ps, 1)
            pe.wait_ge(ld_proj, 48)
            pe.wait_ge(ld_vec, 48)
            for b in range(2):
                mm(ps[:, 0, 128 + 128 * b:256 + 128 * b], projT_sb[:, b, :], up_sb[:, b, :])
            mm(ps[:, 0, 400:401], upb_sb[:], cols_sb[0:DI, V_PB:V_PB + 1]).then_inc(setup_ps, 1)
            pe.wait_ge(ld_ctx, 48)
            for a in range(2):
                last = mm(ps[:, 6 + a, :], wqT_sb[:], ctxT_sb[:, a * 512:(a + 1) * 512])
            last.then_inc(k_ps, 1)
            pe.wait_ge(xin_ready, 1)
            for b in (1, 0):
                for t in range(NT):
                    last = pe.transpose(ps[0:C, 2 + 2 * b + t // 4, (t % 4) * P:(t % 4 + 1) * P],
                                        xi2[:, t, b * C:(b + 1) * C], ident[:])
                last.then_inc(win_ps[b], 1)

            def qkv_rows(b, h):
                br = BRANCHES[b]
                pe.wait_ge(win_ready[b], h + 1)
                if h == 0:
                    pe.wait_ge(ld_qkvw, 16)
                    pe.wait_ge(cleared, 6)
                cols = winT[b][:, h * XCOLS:h * XCOLS + br["slots"] * br["w"]]
                cols = cols.rearrange("p (s i) -> p i s", i=br["w"])
                n, s = br["cols"], br["slots"]
                for i in range(br["w"]):
                    for g in range(br["groups"]):
                        last = mm(ps[g * s:(g + 1) * s, qkv_bank(b, h), i * n:(i + 1) * n], cols[:, i, :],
                                  qkvw_sb[:, b, g * n:(g + 1) * n])
                last.then_inc(qkv_ps[b], 1)

            pe.wait_ge(out_bias_ready, 1)
            pe.wait_ge(xi_taken, 1)
            qkv_rows(1, 0)
            qkv_rows(0, 0)
            pe.wait_ge(k_ready, 1)
            for a in range(2):
                last = mm(ps[:, 6 + a, :], wq_sb[:], kT[:, a * 512:(a + 1) * 512])
            last.then_inc(g_ps, 1)
            pe.wait_ge(g_ready, 1)
            for t in range(NT):
                last = pe.transpose(ps[:, 6 + t // 4, (t % 4) * P:(t % 4 + 1) * P], kT[:, t * P:(t + 1) * P], ident[:])
            last.then_inc(v_ps, 1)
            qkv_rows(1, 1)
            qkv_rows(0, 1)

            def attention_out(b, h):
                br = BRANCHES[b]
                pe.wait_ge(ox_ready[b], br["groups"] * (h + 1))
                if h == 0:
                    pe.wait_ge(ld_ffn, 48)
                    pe.wait_ge(v_ready, 1)
                elif b == 1:
                    pe.wait_ge(wT_ready, h)
                else:
                    pe.wait_ge(acc_start, h)
                s, n = br["slots"], br["chunks"]
                fold_ap = fold_sb[:, 0:64] if b == 0 else fold_sb[:, 64:96]
                for c in range(n):
                    last = mm(ps[:, 7 - b, c * s:(c + 1) * s],
                              ox[b][:, 4 * c:4 * c + 4, :].rearrange("p i c -> p (i c)"), fold_ap)
                last.then_inc(ot_ps[b], 1)
                pe.wait_ge(ot_ready[b], h + 1)
                if h == 0:
                    pe.wait_ge(pu_ready, 8)
                    pe.wait_ge(qkv_act[1], 1)
                    pe.wait_ge(qkv_act[0], 1)
                    pe.wait_ge(win_ready[0], 2)
                else:
                    pe.wait_ge(moe_h_ready, h * EX * NC)
                at = 2 - 2 * b
                for i in range(4):
                    cols = (n if i < 2 or br["w"] % 4 == 0 else n - 1) * s
                    last = mm(ps[:, at + i // 2, (i % 2) * 256:(i % 2) * 256 + cols], pu[b][:, i, :], ot[b][:, 0:cols])
                last.then_inc(xc_ps[b], 1)

            def to_tokens(h):
                pe.wait_ge(xc_ready, 4 * (h + 1))
                if h == 0:
                    pe.wait_ge(qkv_act[1], 2)
                    pe.wait_ge(qkv_act[0], 2)
                else:
                    pe.wait_ge(moe_taken, h * EX * TH)
                for t in range(TH):
                    at = MARGIN + (h * TH + t) * P
                    last = pe.transpose(ps[:, 4, t * P:(t + 1) * P], xcT[:, at:at + P], ident[:])
                last.then_inc(xc_tok_ps, 1)

            def ffn(h):
                pe.wait_ge(h_ready, h + 1)
                for t in range(TH):
                    last = pe.transpose(ps[:, 5, t * P:(t + 1) * P], sq[:, t, :], ident[:])
                last.then_inc(hT_ps, 1)
                pe.wait_ge(hT_ready, h + 1)
                pe.wait_ge(xc20_ready, 2 * (h + 1))
                for c in range(NC):
                    mm(ps[:, c, :], ffn_w1_sb[:, c * P:(c + 1) * P], hT[:]).then_inc(ffn_h_ps, 1)
                pe.wait_ge(xp_ready, h + 1)
                pe.wait_ge(ffn_h_ready, NC * (h + 1))
                for t in range(TH):
                    for c in range(NC):
                        last = mm(ps[:, 4, t * D:(t + 1) * D], hid[:, 0, c, t * P:(t + 1) * P], ffn_w2_sb[:, c, :],
                                  start=(c == 0), stop=(c == NC - 1))
                last.then_inc(ffn_ps, 1)

            def xl_columns(h):
                pe.wait_ge(xl_ready, TH * (h + 1))
                pe.wait_ge(hT_ready, h + 1)
                for t in range(TH):
                    last = pe.transpose(ps[:, 5, t * P:(t + 1) * P], xl[:, t, :], ident[:])
                last.then_inc(xlT_ps, 1)

            def scores(t):
                h = t // TH
                if t % TH == 0:
                    pe.wait_ge(xlT_ready, h + 1)
                    pe.wait_ge(g_ready, 1)
                    pe.wait_ge(casts, 2)
                    pe.wait_ge(ffn_h_ready, NC * (h + 1))
                    pe.wait_ge(xc_ready, 4 * (h + 1))
                if t >= 2:
                    pe.wait_ge(p_ready, t - 1)
                q = xlT[:, (t % TH) * P:(t % TH + 1) * P]
                for a in range(t // 4 + 1):
                    n = min(512, P * (t + 1) - a * 512)
                    bank = 2 * (t % 2) + a
                    diagonal = a == t // 4
                    last = mm(ps[:, bank, 0:n], q, gT[:, a * 512:a * 512 + n], stop=not diagonal)
                    if diagonal:
                        last = mm(ps[:, bank, n - P:n], ident16[:], causal16[:], start=False)
                last.then_inc(s_ps, 1)

            def values(t):
                pe.wait_ge(p_ready, t + 1)
                if t % TH == 0:
                    pe.wait_ge(x1_ready, t // TH + 1)
                if t:
                    pe.wait_ge(pT_act, pT_count(t - 1, "act")) if pT_count(t - 1, "act") else None
                    pe.wait_ge(pT_dve, pT_count(t - 1, "dve"))
                for k in range(t + 1):
                    last = pe.transpose(ps[:, 4 + k // 4, (k % 4) * P:(k % 4 + 1) * P],
                                        pr[:, t % 2, k * P:(k + 1) * P], ident[:])
                last.then_inc(pT_ps, 1)
                if pT_count(t, "act"):
                    pe.wait_ge(pT_act, pT_count(t, "act"))
                pe.wait_ge(pT_dve, pT_count(t, "dve"))
                if t == 0:
                    pe.wait_ge(v_ready, 1)
                if t % TH == 0:
                    pe.wait_ge(ot_ready[0], t // TH + 1)
                    pe.wait_ge(ot_ready[1], t // TH + 1)
                if t >= 2:
                    pe.wait_ge(x2_ready, t - 1)
                for k in range(t + 1):
                    last = mm(ps[:, 6 + t % 2, 0:D], prT[:, t % 2, k * P:(k + 1) * P], v_sb[:, k, :],
                              start=(k == 0), stop=(k == t))
                last.then_inc(pv_ps, 1)

            def route(h):
                pe.wait_ge(xf_ready, TH * (h + 1))
                for t in range(TH):
                    last = pe.transpose(ps[:, 4, t * P:(t + 1) * P], xl[:, t, :], ident[:])
                last.then_inc(xfT_ps, 1)
                pe.wait_ge(xfT_ready, h + 1)
                if h == 0:
                    pe.wait_ge(ld_router, 48)
                for t in range(TH):
                    last = mm(ps[:, 5, t * E:(t + 1) * E], xfT[:, t * P:(t + 1) * P], router_sb[:])
                last.then_inc(lg_ps, 1)

            def expert_bias(h):
                pe.wait_ge(wts_ready, h + 1)
                pe.wait_ge(x2_ready, TH * (h + 1))
                for t in range(TH):
                    last = pe.transpose(ps[0:EX, 6, t * P:(t + 1) * P], wts[:, t, :], ident[:])
                last.then_inc(wT_ps, 1)
                pe.wait_ge(wT_ready, h + 1)
                for t in range(TH):
                    last = mm(ps[:, 7, t * D:(t + 1) * D], wT[:, t * P:(t + 1) * P], moe_b2_sb[:])
                last.then_inc(b2_ps, 1)

            def hidden(h, e):
                k = h * EX + e
                if e == 0 and h == 0:
                    pe.wait_ge(ld_moe, 48)
                if e >= 2:
                    pe.wait_ge(moe_h_ready, NC * (k - 1))
                for c in range(NC):
                    mm(ps[:, 2 * (k % 2) + c, :], moe_w1_sb[:, e, c * P:(c + 1) * P], xfT[:]).then_inc(moe_h_ps, 1)

            def output(h, e):
                k = h * EX + e
                pe.wait_ge(moe_h_ready, NC * (k + 1))
                if e == 0:
                    pe.wait_ge(lg_ready, h + 1)
                if e >= 2:
                    pe.wait_ge(moe_taken, TH * (k - 1))
                for t in range(TH):
                    for c in range(NC):
                        last = mm(ps[:, 4 + k % 2, t * D:(t + 1) * D], hid[:, k % 2, c, t * P:(t + 1) * P],
                                  moe_w2_sb[:, e, c, :], start=(c == 0), stop=(c == NC - 1))
                    last.then_inc(moe_ps, 1)

            for h in range(HALVES):
                attention_out(1, h)
                attention_out(0, h)
                to_tokens(h)
                ffn(h)
                xl_columns(h)
                scores(h * TH)
                for t in range(h * TH, (h + 1) * TH):
                    if t + 1 < (h + 1) * TH:
                        scores(t + 1)
                    values(t)
                route(h)
                pe.wait_ge(p_ready, TH * (h + 1))
                hidden(h, 0)
                expert_bias(h)
                for e in range(EX):
                    if e + 1 < EX:
                        hidden(h, e + 1)
                    output(h, e)


def kernel(**inputs):
    import numpy as np
    import concourse.bacc as bacc
    from concourse.bass_utils import run_bass_kernel_spmd

    a = {n: np.asarray(v) for n, v in inputs.items()}
    f = np.float32

    def attn(name):
        return a["L0_attn_" + name]

    def moe(name):
        return a["L0_ffn_" + name]

    def grouped(n, groups):
        w = np.concatenate([attn(f"qkv{n}_w"), attn(f"qkv{n}_b")[None]], 0)
        return w.reshape(C + 1, 3, groups, -1).transpose(0, 2, 1, 3).reshape(C + 1, QKV)

    def relative(n, br):
        i = np.arange(br["w"])
        r = attn(f"rpb{n}")[i[:, None] - i[None, :] + br["w"] - 1]
        r = r.reshape(br["w"], br["w"], br["groups"], br["nh"]).transpose(2, 0, 3, 1)
        return np.repeat(r.reshape(br["groups"], -1), br["slots"], 0)

    cols = np.zeros((P, NV), f)
    cols[:, V_N2] = attn("norm2_w")
    cols[:, V_B1:V_B1 + NC] = attn("ffn_b1").reshape(NC, P).T
    cols[:, V_UPB] = attn("up_b")
    cols[:DI, V_PB] = np.concatenate([attn("proj1_b"), attn("proj2_b")])
    cols[:C, V_N1:V_N1 + 2] = attn("norm1_w").reshape(2, C).T
    b1 = np.concatenate([moe("rb1"), moe("sb1")[None]], 0)
    cols[:, V_EB1:] = b1.reshape(EX * NC, P).T
    rows = np.concatenate([attn("down_b"), attn("ffn_b2"), moe("router_b")])
    slot = np.arange(P)
    arrays = {
        "x": a["x"],
        "x_t": a["x"][0].T,
        "ctx_t": a["ctx_1024"][0, :T].T,
        "wq": a["L0_xattn_Wq"],
        "wq_t": a["L0_xattn_Wq"].T,
        "down_w": attn("down_w"),
        "centre": (np.eye(P) - 1.0 / P).astype(f),
        "identity": np.eye(P, dtype=f),
        "causal": np.triu(np.full((P, P), MASKED, f), 1),
        "up_w": attn("up_w"),
        "proj_t": np.stack([np.tile(attn(f"proj{n}_w").T, (1, 4)) for n in (1, 2)], 1),
        "qkv_w": np.stack([grouped(n, br["groups"]) for n, br in zip((1, 2), BRANCHES)], 1),
        "bias10": relative(1, BRANCHES[0]),
        "bias20": relative(2, BRANCHES[1]),
        "fold": np.concatenate([slot[:, None] % br["slots"] == np.arange(br["slots"]) for br in BRANCHES], 1).astype(f),
        "ffn_w1": attn("ffn_w1"),
        "ffn_w2": attn("ffn_w2"),
        "router_w": moe("router_w"),
        "tri": np.tile(np.tril(np.ones((E, E), f), -1).reshape(1, -1), (P, 1)),
        "cols": cols,
        "rows": rows,
        "moe_w1": np.concatenate([moe("rw1"), moe("sw1")[None]], 0),
        "moe_w2": np.concatenate([moe("rw2"), moe("sw2")[None]], 0),
        "moe_b2": np.concatenate([moe("rb2"), moe("sb2")[None]], 0),
    }
    arrays = {n: np.ascontiguousarray(v) for n, v in arrays.items()}
    nc = bacc.Bacc("TRN2", target_bir_lowering=False, num_devices=1)
    args = {n: nc.dram_tensor("in_" + n, v.shape, F32, kind="ExternalInput").ap() for n, v in arrays.items()}
    out = nc.dram_tensor("out", (1, T, D), F32, kind="ExternalOutput").ap()
    decoder_layer(nc, out=out, **args)
    r = run_bass_kernel_spmd(nc, [{"in_" + n: v for n, v in arrays.items()}], core_ids=[0])
    return r.results[0]["out"]
```

```python
from contextlib import ExitStack

import concourse.bass as bass
from concourse import mybir

F32 = mybir.dt.float32
BF16 = mybir.dt.bfloat16
ALU = mybir.AluOpType
ACT = mybir.ActivationFunctionType
AX = mybir.AxisListType

P = 128
T = 1024
D = 128
NT = T // P
HALVES = 2
TH = NT // HALVES
CH = T // HALVES
DI = 64
C = DI // 2
HD = 4
HID = 256
NC = HID // P
E = 8
EX = E + 1
QKV = 3 * C
MASKED = -(2.0 ** 100)

BRANCHES = (dict(w=10, groups=2, windows=(52, 51)), dict(w=20, groups=4, windows=(27, 25)))
for _b in BRANCHES:
    _b["shift"] = _b["w"] // 2
    _b["slots"] = P // _b["groups"]
    _b["nh"] = 8 // _b["groups"]
    _b["cols"] = 3 * HD * _b["nh"]
    _b["chunks"] = -(-_b["w"] // 4)
    _b["first"] = (_b["shift"], _b["shift"] - _b["windows"][0] * _b["w"])
XCOLS = 640
MARGIN = BRANCHES[1]["shift"]

V_N2, V_B1, V_UPB, V_PB, V_N1, V_EB1 = 0, 1, 3, 4, 5, 7
NV = V_EB1 + EX * NC
R_DB, R_B2, R_RB = 0, DI, DI + D
NR = R_RB + E


def spread(ap, axis, n):
    ap = ap.unsqueeze(axis)
    shape = list(ap.shape)
    shape[axis] = n
    return ap.broadcast_to(shape)


def decoder_layer(nc, x, x_t, ctx_t, wq, wq_t, down_w, centre, identity, causal, up_w, proj_t, qkv_w,
                  bias10, bias20, fold, ffn_w1, ffn_w2, router_w, tri, cols, rows, moe_w1, moe_w2, moe_b2, out):
    with ExitStack() as stack:
        def sb(name, shape, dt=F32):
            return stack.enter_context(nc.sbuf_tensor(name, shape, dt))

        def sem(name):
            return stack.enter_context(nc.semaphore(name))

        ps = stack.enter_context(nc.psum_tensor("ps", [P, 8, 512], F32))

        x_sb = sb("x_sb", [P, NT, D])
        xT_sb = sb("xT_sb", [P, T])
        ctxT_sb = sb("ctxT_sb", [P, T])
        wq_sb = sb("wq_sb", [P, D])
        wqT_sb = sb("wqT_sb", [P, D])
        down_sb = sb("down_sb", [P, DI])
        centre_sb = sb("centre_sb", [P, P])
        ident = sb("ident", [P, P])
        causal_sb = sb("causal_sb", [P, P])
        up_sb = sb("up_sb", [C, 2, D])
        upb_sb = sb("upb_sb", [DI, D])
        projT_sb = sb("projT_sb", [C, 2, P])
        qkvw_sb = sb("qkvw_sb", [C + 1, 2, QKV])
        fold_sb = sb("fold_sb", [P, 96])
        ffn_w1_sb = sb("ffn_w1_sb", [P, HID])
        ffn_w2_sb = sb("ffn_w2_sb", [P, NC, D])
        router_sb = sb("router_sb", [P, E])
        tri_sb = sb("tri_sb", [P, E * E])
        cols_sb = sb("cols_sb", [P, NV])
        rows_sb = sb("rows_sb", [P, NR])
        moe_w1_sb = sb("moe_w1_sb", [P, EX, HID])
        moe_w2_sb = sb("moe_w2_sb", [P, EX, NC, D])
        moe_b2_sb = sb("moe_b2_sb", [EX, D])
        elems = [b["w"] * b["nh"] * b["w"] for b in BRANCHES]
        relb = [[sb(f"relb{b['w']}_{h}", [P, n]) for h in range(2)] for b, n in zip(BRANCHES, elems)]

        ident16 = sb("ident16", [P, P], BF16)
        causal16 = sb("causal16", [P, P], BF16)
        minus_half = sb("minus_half", [P, NT])
        downc = sb("downc", [P, DI])
        pu = [sb(f"pu{b['w']}", [P, 4, D]) for b in BRANCHES]
        out_bias = sb("out_bias", [P, 1])

        st = sb("st", [P, NT, 6])
        mv = sb("mv", [P, NT, 2])
        rstd0 = sb("rstd0", [P, NT])
        xn = sb("xn", [P, NT, D])
        xs = sb("xs", [P, NT, D])
        xi = sb("xi", [P, NT, DI])
        xi2 = sb("xi2", [P, NT, DI])
        ss = sb("ss", [P, NT])
        rstd1 = sb("rstd1", [P, NT])
        winT = [sb(f"winT{b['w']}", [C + 1, HALVES * XCOLS]) for b in BRANCHES]
        qkv = [[sb(f"qkv{b['w']}_{h}", [P, b["w"], b["cols"]]) for h in range(2)] for b in BRANCHES]
        prod = [sb(f"prod{b['w']}", [P, HD, n]) for b, n in zip(BRANCHES, elems)]
        half_ident = sb("half_ident", [P, P])
        sc = [sb(f"sc{b['w']}", [P, n]) for b, n in zip(BRANCHES, elems)]
        stat = [sb(f"stat{b['w']}", [P, 3, b["w"] * b["nh"]]) for b in BRANCHES]
        ou = sb("ou", [P, HD, BRANCHES[0]["w"] * BRANCHES[0]["nh"]])
        ox = [sb(f"ox{b['w']}", [P, 4 * b["chunks"], C]) for b in BRANCHES]
        ot = [sb(f"ot{b['w']}", [P, b["chunks"] * b["slots"]]) for b in BRANCHES]
        xcT = sb("xcT", [P, 1100])

        xp = [sb(f"xp_{h}", [P, TH, D]) for h in range(2)]
        sq = [sb(f"sq_{h}", [P, TH, D]) for h in range(2)]
        ss2 = [sb(f"ss2_{h}", [P, TH]) for h in range(2)]
        rstd2 = [sb(f"rstd2_{h}", [P, TH]) for h in range(2)]
        hT = [sb(f"hT_{h}", [P, CH]) for h in range(2)]
        ffn_hid = [sb(f"ffn_hid_{h}", [P, NC, CH]) for h in range(2)]
        hid = sb("hid", [P, 2, NC, CH])
        x1 = [sb(f"x1_{h}", [P, TH, D]) for h in range(2)]
        st2 = [sb(f"st2_{h}", [P, TH, 6]) for h in range(2)]
        mv2 = [sb(f"mv2_{h}", [P, TH, 2]) for h in range(2)]
        rstd3 = [sb(f"rstd3_{h}", [P, TH]) for h in range(2)]
        xl = [sb(f"xl_{h}", [P, TH, D]) for h in range(2)]
        xlT = [sb(f"xlT_{h}", [P, CH]) for h in range(2)]
        kT = sb("kT", [P, T])
        gT = sb("gT", [P, T])
        v_sb = sb("v_sb", [P, NT, D])
        pr = sb("pr", [P, 2, T])
        prT = sb("prT", [P, 2, T])
        nmx = sb("nmx", [P, NT])
        den = sb("den", [P, NT])
        rden = sb("rden", [P, NT])
        xfT = [sb(f"xfT_{h}", [P, CH]) for h in range(2)]
        lg = [sb(f"lg_{h}", [P, TH, E]) for h in range(2)]
        lmx = [sb(f"lmx_{h}", [P, TH]) for h in range(2)]
        lsum = [sb(f"lsum_{h}", [P, TH]) for h in range(2)]
        gt = [sb(f"gt_{h}", [P, TH, E * E]) for h in range(2)]
        eq = [sb(f"eq_{h}", [P, TH, E * E]) for h in range(2)]
        wts = [sb(f"wts_{h}", [P, TH, EX]) for h in range(2)]
        wT = [sb(f"wT_{h}", [EX, CH]) for h in range(2)]
        acc = sb("acc", [P, NT, D])
        x2 = [acc[:, h * TH:(h + 1) * TH, :] for h in range(2)]

        ld_down = sem("ld_down")
        ld_xT = sem("ld_xT")
        ld_x = sem("ld_x")
        ld_vec = sem("ld_vec")
        ld_proj = sem("ld_proj")
        ld_ctx = sem("ld_ctx")
        ld_qkvw = sem("ld_qkvw")
        ld_bias = sem("ld_bias")
        ld_ffn = sem("ld_ffn")
        ld_moe = sem("ld_moe")
        ld_router = sem("ld_router")
        stored = sem("stored")
        dve_step = sem("dve_step")
        pool_step = sem("pool_step")
        cleared = sem("cleared")
        win_clear = sem("win_clear")
        casts = sem("casts")
        relb_ready = sem("relb_ready")
        setup_ps = sem("setup_ps")
        downc_ready = sem("downc_ready")
        pu_ready = sem("pu_ready")
        out_bias_ready = sem("out_bias_ready")
        stats0 = sem("stats0")
        rstd0_ready = sem("rstd0_ready")
        xi_ps = sem("xi_ps")
        xi_taken = sem("xi_taken")
        ss_ready = sem("ss_ready")
        rstd1_ready = sem("rstd1_ready")
        xin_ready = sem("xin_ready")
        xn_ready = sem("xn_ready")
        win_ps = [sem("win10_ps"), sem("win20_ps")]
        win_ready = [sem("win10_ready"), sem("win20_ready")]
        qkv_ps = [sem("qkv10_ps"), sem("qkv20_ps")]
        qkv_act = [sem("qkv10_act"), sem("qkv20_act")]
        half_ready = sem("half_ready")
        qk_ready = [sem("qk10_ready"), sem("qk20_ready")]
        qk_ps = [sem("qk10_ps"), sem("qk20_ps")]
        wv_ready = [sem("wv10_ready"), sem("wv20_ready")]
        wv_ps = [sem("wv10_ps"), sem("wv20_ps")]
        sc_ready = [sem("sc10_ready"), sem("sc20_ready")]
        exp_ready = [sem("exp10_ready"), sem("exp20_ready")]
        ox_ready = [sem("ox10_ready"), sem("ox20_ready")]
        ot_ps = [sem("ot10_ps"), sem("ot20_ps")]
        ot_ready = [sem("ot10_ready"), sem("ot20_ready")]
        xc_ps = [sem("xc10_ps"), sem("xc20_ps")]
        xc20_ready = sem("xc20_ready")
        xc_ready = sem("xc_ready")
        xc_tok_ps = sem("xc_tok_ps")
        xp_ready = sem("xp_ready")
        xs_ready = sem("xs_ready")
        ss2_ready = sem("ss2_ready")
        rstd2_ready = sem("rstd2_ready")
        h_ready = sem("h_ready")
        hT_ps = sem("hT_ps")
        hT_ready = sem("hT_ready")
        ffn_h_ps = sem("ffn_h_ps")
        ffn_h_ready = sem("ffn_h_ready")
        ffn_ps = sem("ffn_ps")
        x1_ready = sem("x1_ready")
        stats2 = sem("stats2")
        rstd3_ready = sem("rstd3_ready")
        xl_ready = sem("xl_ready")
        xlT_ps = sem("xlT_ps")
        xlT_ready = sem("xlT_ready")
        k_ps = sem("k_ps")
        k_ready = sem("k_ready")
        g_ps = sem("g_ps")
        g_ready = sem("g_ready")
        v_ps = sem("v_ps")
        v_ready = sem("v_ready")
        s_ps = sem("s_ps")
        max_ready = sem("max_ready")
        p_ready = sem("p_ready")
        pT_ps = sem("pT_ps")
        pT_act = sem("pT_act")
        pT_dve = sem("pT_dve")
        pv_ps = sem("pv_ps")
        x2_ready = sem("x2_ready")
        stats3 = sem("stats3")
        rstd4_ready = sem("rstd4_ready")
        xf_ready = sem("xf_ready")
        xfT_ps = sem("xfT_ps")
        xfT_ready = sem("xfT_ready")
        lg_ps = sem("lg_ps")
        lg_ready = sem("lg_ready")
        lexp_ready = sem("lexp_ready")
        wts_ready = sem("wts_ready")
        wT_ps = sem("wT_ps")
        wT_ready = sem("wT_ready")
        b2_ps = sem("b2_ps")
        acc_start = sem("acc_start")
        moe_h_ps = sem("moe_h_ps")
        moe_h_ready = sem("moe_h_ready")
        moe_ps = sem("moe_ps")
        moe_taken = sem("moe_taken")

        block = stack.enter_context(nc.Block())

        def qkv_bank(b, h):
            return 4 * h + 1 - b

        def window_sum(b, h):
            if b == 0:
                return ps[:, 4 * h + 1:4 * h + 2, 0:400]
            return ps[:, 4 * h + 2:4 * h + 4, 0:400]

        def window_out(b, h):
            return ps[:, 4 * h + 1 - b, 0:HD * BRANCHES[b]["w"] * BRANCHES[b]["nh"]]

        def qk_parts(h):
            return 2 if h == 0 else HD

        def values_on_pe(b, h):
            return b == 1 or h == 1

        def wv_before(b, h):
            return sum(values_on_pe(b, u) for u in range(h + 1))

        def bank(h, n):
            return 4 * h + n

        def pT_parts(t):
            if t < 4:
                return [("act" if t % 2 else "dve", 0, t + 1)]
            return [("dve", 0, 4), ("act", 4, t + 1)]

        def pT_count(t, engine):
            return sum(e == engine for u in range(t + 1) for e, _, _ in pT_parts(u))

        def score_banks(t):
            if t < TH:
                return ps[:, t % 2, :]
            return ps[:, 4:6, :].rearrange("p a n -> p (a n)")

        def parts_before(t):
            return sum(len(pT_parts(u)) for u in range(t))

        @block.sync
        def _(sp):
            sp.dma_start(xT_sb[:], x_t).then_inc(ld_xT, 16)
            sp.dma_start(rows_sb[:], rows.partition_broadcast(P)).then_inc(ld_vec, 16)
            sp.dma_start(cols_sb[:], cols).then_inc(ld_vec, 16)
            sp.dma_start(ident[:], identity).then_inc(ld_vec, 16)
            sp.dma_start(qkvw_sb[:], qkv_w).then_inc(ld_qkvw, 16)
            sp.dma_start(wqT_sb[:], wq_t).then_inc(ld_ctx, 16)
            sp.dma_start(ctxT_sb[:], ctx_t).then_inc(ld_ctx, 16)
            sp.dma_start(wq_sb[:], wq).then_inc(ld_ctx, 16)
            sp.dma_start(projT_sb[:], proj_t).then_inc(ld_proj, 16)
            sp.dma_start(up_sb[:], up_w.rearrange("(b c) n -> c b n", b=2)).then_inc(ld_proj, 16)
            sp.dma_start(upb_sb[:], up_w).then_inc(ld_proj, 16)
            sp.dma_start(relb[1][1][:], bias20).then_inc(ld_bias, 16)
            sp.dma_start(relb[0][1][:], bias10).then_inc(ld_bias, 16)
            sp.dma_start(fold_sb[:], fold).then_inc(ld_ffn, 16)
            sp.dma_start(ffn_w1_sb[:], ffn_w1).then_inc(ld_ffn, 16)
            sp.dma_start(ffn_w2_sb[:], ffn_w2.rearrange("(c p) n -> p c n", p=P)).then_inc(ld_ffn, 16)
            sp.dma_start(causal_sb[:], causal).then_inc(ld_router, 16)
            sp.dma_start(router_sb[:], router_w).then_inc(ld_router, 16)
            sp.dma_start(tri_sb[:], tri).then_inc(ld_router, 16)
            sp.dma_start(moe_w1_sb[:], moe_w1.rearrange("e p n -> p e n")).then_inc(ld_moe, 16)
            sp.dma_start(moe_w2_sb[:], moe_w2.rearrange("e (c p) n -> p e c n", p=P)).then_inc(ld_moe, 16)
            sp.dma_start(moe_b2_sb[:], moe_b2).then_inc(ld_moe, 16)
            out_v = out.rearrange("o (t p) d -> (o p) t d", p=P)
            for h in range(HALVES):
                for t in range(TH):
                    sp.wait_ge(moe_taken, (h * EX + EX - 1) * TH + t + 1)
                    sp.dma_start(out_v[:, h * TH + t, :], acc[:, h * TH + t, :]).then_inc(stored, 16)
            sp.wait_ge(stored, 16 * NT)

        @block.gpsimd
        def _(pool):
            steps = [0]

            def step(ins):
                steps[0] += 1
                ins.then_inc(pool_step, 1)

            def settle():
                pool.wait_ge(pool_step, steps[0])

            step(pool.memset(minus_half[:], -0.5))
            pool.memset(pu[0][:], 0.0).then_inc(cleared, 1)
            pool.memset(pu[1][:], 0.0).then_inc(cleared, 1)
            settle()

            def rstd(dst, src, scale, eps, ready):
                step(pool.tensor_scalar(dst, src, scale, eps, ALU.mult, ALU.add))
                settle()
                pool.tensor_tensor(dst, dst, minus_half[:, 0:dst.shape[1]], ALU.pow).then_inc(ready, 1)

            pool.wait_ge(stats0, NT)
            rstd(rstd0[:], mv[:, :, 1], 1.0, 1e-5, rstd0_ready)
            pool.wait_ge(ss_ready, 1)
            rstd(rstd1[:], ss[:], 1.0 / DI, 1e-6, rstd1_ready)

            pool.wait_ge(ld_bias, 32)
            parts = 0
            for b in (1, 0):
                br = BRANCHES[b]
                w, s = br["w"], br["shift"]
                step(pool.tensor_copy(relb[b][0][:], relb[b][1][:]))
                settle()
                for g in range(br["groups"]):
                    p = g * br["slots"]
                    v = relb[b][0][p:p + 1, :].rearrange("p (i h j) -> p i h j", i=w, h=br["nh"])
                    pool.tensor_scalar_add(v[:, 0:s, :, s:w], v[:, 0:s, :, s:w], -100.0).then_inc(relb_ready, 1)
                    parts += 1
                    pool.wait_ge(relb_ready, parts)
                    pool.tensor_scalar_add(v[:, s:w, :, 0:s], v[:, s:w, :, 0:s], -100.0).then_inc(relb_ready, 1)
                    parts += 1
                    pool.wait_ge(relb_ready, parts)
            pool.memset(ox[1][:], 0.0).then_inc(cleared, 1)
            pool.memset(ox[0][:], 0.0).then_inc(cleared, 1)
            for h in range(HALVES):
                pool.memset(wts[h][:], 1.0).then_inc(cleared, 1)
            pool.wait_ge(ld_router, 48)
            pool.wait_ge(ld_vec, 48)
            pool.tensor_copy(ident16[:], ident[:]).then_inc(casts, 1)
            pool.tensor_copy(causal16[:], causal_sb[:]).then_inc(casts, 1)

            pool.wait_ge(ld_x, 16)
            step(pool.tensor_tensor(xs[:], x_sb[:], spread(rows_sb[:, R_B2:R_B2 + D], 1, NT), ALU.add))
            settle()

            def rstd2_pow(h):
                pool.wait_ge(ss2_ready, h + 1)
                rstd(rstd2[h][:], ss2[h][:], 1.0 / D, 1e-6, rstd2_ready)

            def xs_add(h):
                hs = slice(h * TH, (h + 1) * TH)
                pool.wait_ge(xp_ready, h + 1)
                pool.tensor_tensor(xs[:, hs, :], xs[:, hs, :], xp[h][:], ALU.add).then_inc(xs_ready, 1)

            def rstd3_pow(h):
                pool.wait_ge(stats2, TH * (h + 1))
                rstd(rstd3[h][:], mv2[h][:, :, 1], 1.0, 1e-5, rstd3_ready)

            def rstd4_pow(h):
                pool.wait_ge(xl_ready, TH * (h + 1))
                pool.wait_ge(stats3, TH * (h + 1))
                rstd(rstd3[h][:], mv2[h][:, :, 1], 1.0, 1e-5, rstd4_ready)

            rstd2_pow(0)
            xs_add(0)
            xs_add(1)
            rstd2_pow(1)
            rstd3_pow(0)
            rstd3_pow(1)
            rstd4_pow(0)
            rstd4_pow(1)

        def window_part(b, h):
            a, z = BRANCHES[b]["first"]
            cut = BRANCHES[b]["windows"][0] * BRANCHES[b]["w"] - a
            src = ps[0:C, 2 + 2 * b:4 + 2 * b, :].rearrange("p a n -> p (a n)")
            if h == 0:
                return winT[b][0:C, a:a + cut], src[:, 0:cut]
            return winT[b][0:C, XCOLS + z + cut:XCOLS + z + T], src[:, cut:T]

        @block.scalar
        def _(act):
            act.dma_start(down_sb[:], down_w).then_inc(ld_down, 16)
            act.dma_start(centre_sb[:], centre).then_inc(ld_down, 16)
            act.dma_start(x_sb[:], x.rearrange("o (t p) d -> (o p) t d", p=P)).then_inc(ld_x, 16)
            act.wait_ge(setup_ps, 1)
            act.activation(downc[:], ps[:, 7, 0:DI], ACT.Copy).then_inc(downc_ready, 1)
            act.wait_ge(ld_vec, 48)
            act.activation(half_ident[:], ident[:], ACT.Copy, scale=0.5).then_inc(half_ready, 1)

            def window_cols(b, h):
                act.wait_ge(win_ps[b], 1)
                act.wait_ge(win_clear, 4)
                dst, src = window_part(b, h)
                act.activation(dst, src, ACT.Copy, scale=cols_sb[0:C, V_N1 + b:V_N1 + b + 1]).then_inc(win_ready[b], 1)

            act.wait_ge(win_ready[1], 1)
            window_cols(1, 1)
            window_cols(0, 0)
            window_cols(0, 1)

            def qkv_copy(b, h):
                br = BRANCHES[b]
                act.wait_ge(qkv_ps[b], h + 1)
                src = ps[:, qkv_bank(b, h), 0:br["w"] * br["cols"]].rearrange("p (i n) -> p i n", i=br["w"])
                act.activation(qkv[b][h][:], src, ACT.Copy).then_inc(qkv_act[b], 1)

            qkv_copy(1, 0)
            qkv_copy(0, 0)

            def k_copy():
                act.wait_ge(k_ps, 1)
                act.activation(kT[:].rearrange("p (a n) -> p a n", a=2), ps[:, 6:8, :], ACT.Copy).then_inc(k_ready, 1)

            def pu_copy():
                act.wait_ge(setup_ps, 2)
                act.wait_ge(cleared, 2)
                for b in range(2):
                    for g in range(4):
                        r = slice(32 * g, 32 * g + 32)
                        act.activation(pu[b][r, g, :], ps[r, 0, 128 * b:128 + 128 * b], ACT.Copy).then_inc(pu_ready, 1)
                act.activation(out_bias[:], ps[:, 0, 256:257], ACT.Identity,
                               bias=cols_sb[:, V_UPB:V_UPB + 1]).then_inc(out_bias_ready, 1)

            def g_copy():
                act.wait_ge(g_ps, 1)
                act.activation(gT[:].rearrange("p (a n) -> p a n", a=2), ps[:, 0:2, :], ACT.Copy,
                               scale=float(D) ** -0.5).then_inc(g_ready, 1)

            def v_copy():
                act.wait_ge(v_ps, 1)
                act.activation(v_sb[:].rearrange("p (a t) d -> p a (t d)", a=2), ps[:, 0:2, :],
                               ACT.Copy).then_inc(v_ready, 1)

            def window_exp(b, h):
                act.wait_ge(sc_ready[b], h + 1)
                act.activation(sc[b][:], sc[b][:], ACT.Exp).then_inc(exp_ready[b], 1)

            def ot_copy(b, h):
                act.wait_ge(ot_ps[b], h + 1)
                if h:
                    act.wait_ge(xc_ps[b], h)
                act.activation(ot[b][:], ps[:, bank(h, 1 - b), 0:ot[b].shape[1]], ACT.Copy).then_inc(ot_ready[b], 1)

            def xc20_copy(h):
                br = BRANCHES[1]
                act.wait_ge(xc_ps[1], h + 1)
                n = br["windows"][h]
                at = MARGIN - br["first"][h]
                for a in range(2):
                    src = ps[:, bank(h, 2 + a), :].rearrange("p (i c s) -> p i c s", i=2, s=br["slots"])
                    src = src[:, :, 0:br["chunks"], 0:n]
                    dst = xcT[:, at:at + n * br["w"]].rearrange("p (s c i) -> p i c s", c=br["chunks"], i=4)
                    act.activation(dst[:, 2 * a:2 * a + 2], src, ACT.Identity,
                                   bias=out_bias[:, 0:1]).then_inc(xc20_ready, 1)

            def hT_copy(h):
                act.wait_ge(hT_ps, h + 1)
                act.activation(hT[h][:], ps[:, bank(h, 3), :], ACT.Copy,
                               scale=cols_sb[:, V_N2:V_N2 + 1]).then_inc(hT_ready, 1)

            def ffn_gelu(h, c):
                act.wait_ge(ffn_h_ps, h * NC + c + 1)
                act.activation(ffn_hid[h][:, c, :], ps[:, bank(h, c), :], ACT.Gelu,
                               bias=cols_sb[:, V_B1 + c:V_B1 + c + 1]).then_inc(ffn_h_ready, 1)

            def xlT_copy(h):
                act.wait_ge(xlT_ps, h + 1)
                act.activation(xlT[h][:], ps[:, bank(h, 3), :], ACT.Copy).then_inc(xlT_ready, 1)

            def softmax(t):
                act.wait_ge(max_ready, t + 1)
                if t >= 2:
                    act.wait_ge(pT_ps, parts_before(t - 1))
                n = P * (t + 1)
                act.activation(pr[:, t % 2, 0:n], score_banks(t)[:, 0:n], ACT.Exp, bias=nmx[:, t:t + 1],
                               accum_out=den[:, t:t + 1]).then_inc(p_ready, 1)

            def pT_copy(t):
                for n, (engine, a, z) in enumerate(pT_parts(t)):
                    if engine == "act":
                        act.wait_ge(pT_ps, parts_before(t) + n + 1)
                        if t >= 2:
                            act.wait_ge(pv_ps, t - 1)
                        act.activation(prT[:, t % 2, a * P:z * P], ps[:, bank(t // TH, 2), 0:(z - a) * P],
                                       ACT.Copy).then_inc(pT_act, 1)

            def xfT_copy(h):
                act.wait_ge(xfT_ps, h + 1)
                act.activation(xfT[h][:], ps[:, bank(h, 2), :], ACT.Copy).then_inc(xfT_ready, 1)

            def router_exp(h):
                act.wait_ge(lg_ready, h + 1)
                act.activation(lg[h][:], lg[h][:], ACT.Exp).then_inc(lexp_ready, 1)

            def wT_copy(h):
                act.wait_ge(wT_ps, h + 1)
                act.activation(wT[h][:], ps[0:EX, bank(h, 2), :], ACT.Copy).then_inc(wT_ready, 1)

            def moe_gelu(h, e, c):
                k = h * EX + e
                act.wait_ge(moe_h_ps, k * NC + c + 1)
                if k >= 2:
                    act.wait_ge(moe_ps, k - 1)
                i = V_EB1 + e * NC + c
                act.activation(hid[:, k % 2, c, :], ps[:, c, :], ACT.Gelu,
                               bias=cols_sb[:, i:i + 1]).then_inc(moe_h_ready, 1)

            k_copy()
            pu_copy()
            qkv_copy(0, 1)
            window_exp(1, 0)
            qkv_copy(1, 1)
            window_exp(0, 0)
            ot_copy(1, 0)
            ot_copy(0, 0)
            xc20_copy(0)
            window_exp(1, 1)
            window_exp(0, 1)
            ot_copy(1, 1)
            ot_copy(0, 1)
            xc20_copy(1)
            hT_copy(0)
            ffn_gelu(0, 0)
            ffn_gelu(0, 1)
            g_copy()
            hT_copy(1)
            v_copy()
            ffn_gelu(1, 0)
            xlT_copy(0)
            ffn_gelu(1, 1)
            softmax(0)
            softmax(1)
            softmax(2)
            pT_copy(1)
            softmax(3)
            xlT_copy(1)
            pT_copy(3)
            softmax(4)
            pT_copy(4)
            softmax(5)
            xfT_copy(0)
            pT_copy(5)
            softmax(6)
            router_exp(0)
            moe_gelu(0, 0, 0)
            moe_gelu(0, 0, 1)
            moe_gelu(0, 1, 0)
            moe_gelu(0, 1, 1)
            wT_copy(0)
            softmax(7)
            moe_gelu(0, 2, 0)
            pT_copy(6)
            moe_gelu(0, 2, 1)
            pT_copy(7)
            moe_gelu(0, 3, 0)
            moe_gelu(0, 3, 1)
            moe_gelu(0, 4, 0)
            moe_gelu(0, 4, 1)
            moe_gelu(0, 5, 0)
            moe_gelu(0, 5, 1)
            moe_gelu(0, 6, 0)
            moe_gelu(0, 6, 1)
            xfT_copy(1)
            moe_gelu(0, 7, 0)
            moe_gelu(0, 7, 1)
            router_exp(1)
            moe_gelu(0, 8, 0)
            moe_gelu(0, 8, 1)
            moe_gelu(1, 0, 0)
            wT_copy(1)
            moe_gelu(1, 0, 1)
            moe_gelu(1, 1, 0)
            moe_gelu(1, 1, 1)
            moe_gelu(1, 2, 0)
            moe_gelu(1, 2, 1)
            moe_gelu(1, 3, 0)
            moe_gelu(1, 3, 1)
            moe_gelu(1, 4, 0)
            moe_gelu(1, 4, 1)
            moe_gelu(1, 5, 0)
            moe_gelu(1, 5, 1)
            moe_gelu(1, 6, 0)
            moe_gelu(1, 6, 1)
            moe_gelu(1, 7, 0)
            moe_gelu(1, 7, 1)
            moe_gelu(1, 8, 0)
            moe_gelu(1, 8, 1)

        @block.vector
        def _(dve):
            steps = [0]

            def step(ins):
                steps[0] += 1
                ins.then_inc(dve_step, 1)

            def settle():
                dve.wait_ge(dve_step, steps[0])

            for b in (1, 0):
                a, z = BRANCHES[b]["first"]
                cut = BRANCHES[b]["windows"][0] * BRANCHES[b]["w"] - a
                dve.memset(winT[b][0:C, 0:a], 0.0)
                dve.memset(winT[b][0:C, a + cut:XCOLS + z + cut], 0.0)
                dve.memset(winT[b][0:C, XCOLS + z + T:2 * XCOLS], 0.0).then_inc(win_clear, 1)
                dve.memset(winT[b][C:C + 1, :], 1.0).then_inc(win_clear, 1)
            dve.wait_ge(ld_x, 16)
            for t in range(NT):
                step(dve.bn_stats(st[:, t, :], x_sb[:, t, :]))
            settle()
            for t in range(NT):
                dve.bn_aggr(mv[:, t, :], st[:, t, :]).then_inc(stats0, 1)
            dve.wait_ge(rstd0_ready, 1)
            dve.wait_ge(xi_ps, 1)
            dve.wait_ge(ld_vec, 48)
            dve.tensor_tensor(xi[:], ps[:, 1, :].rearrange("p (t n) -> p t n", t=NT),
                              spread(rstd0[:], 2, DI), ALU.mult).then_inc(xi_taken, 1)
            dve.wait_ge(xi_taken, 1)
            step(dve.tensor_tensor(xi[:], xi[:], spread(rows_sb[:, R_DB:R_DB + DI], 1, NT), ALU.add))
            settle()
            step(dve.tensor_tensor(xi2[:], xi[:], xi[:], ALU.mult))
            settle()
            dve.tensor_reduce(ss[:], xi2[:], AX.X, ALU.add).then_inc(ss_ready, 1)
            dve.wait_ge(stats0, NT)
            for t in range(NT):
                step(dve.tensor_scalar(xn[:, t, :], x_sb[:, t, :], mv[:, t, 0:1], rstd0[:, t:t + 1],
                                       ALU.subtract, ALU.mult))
            dve.wait_ge(rstd1_ready, 1)
            dve.tensor_tensor(xi2[:], xi[:], spread(rstd1[:], 2, DI), ALU.mult).then_inc(xin_ready, 1)
            dve.wait_ge(win_clear, 4)
            dve.wait_ge(win_ps[1], 1)
            dst, src = window_part(1, 0)
            dve.tensor_scalar(dst, src, cols_sb[0:C, V_N1 + 1:V_N1 + 2], None, ALU.mult).then_inc(win_ready[1], 1)

            def heads(ap, nh, d):
                return ap.rearrange("p i (h d) -> p i h d", d=HD)[:, :, :, d]

            SHAPE = "p (i h j) -> p i h j"

            def window_product(b, h, d):
                br = BRANCHES[b]
                w, nh = br["w"], br["nh"]
                if d == 0:
                    dve.wait_ge(qkv_act[b], h + 1)
                    if h and values_on_pe(b, h - 1):
                        dve.wait_ge(wv_ps[b], wv_before(b, h - 1))
                t = qkv[b][h]
                q = heads(t[:, :, 0:HD * nh], nh, d)
                k = heads(t[:, :, HD * nh:2 * HD * nh], nh, d).rearrange("p j h -> p h j")
                product = dve.tensor_tensor(prod[b][:, d, :].rearrange(SHAPE, i=w, h=nh),
                                            spread(q, 3, w), spread(k, 1, w), ALU.mult)
                if qk_parts(h) == HD:
                    product.then_inc(qk_ready[b], 1)
                    return
                step(product)
                if d % 2:
                    settle()
                    dve.tensor_tensor(prod[b][:, d - 1, :], prod[b][:, d - 1, :], prod[b][:, d, :],
                                      ALU.add).then_inc(qk_ready[b], 1)

            def window_scores(b, h):
                w = BRANCHES[b]["w"]
                dve.wait_ge(qk_ps[b], h + 1)
                scores = window_sum(b, h).rearrange("p a (r j) -> p a r j", j=w)
                rows4 = sc[b][:].rearrange("p (a r j) -> p a r j", a=b + 1, j=w)
                top = stat[b][:, 0, :].rearrange("p (a r) -> p a r", a=b + 1)
                step(dve.tensor_reduce(top, scores, AX.X, ALU.max))
                settle()
                dve.tensor_tensor(rows4, scores, spread(top, 3, w), ALU.subtract).then_inc(sc_ready[b], 1)

            def window_weighted(b, h, d):
                br = BRANCHES[b]
                w, nh = br["w"], br["nh"]
                if d == 0:
                    dve.wait_ge(exp_ready[b], h + 1)
                v = heads(qkv[b][h][:, :, 2 * HD * nh:3 * HD * nh], nh, d).rearrange("p j h -> p h j")
                dve.tensor_tensor(prod[b][:, d, :].rearrange(SHAPE, i=w, h=nh), sc[b][:].rearrange(SHAPE, i=w, h=nh),
                                  spread(v, 1, w), ALU.mult).then_inc(wv_ready[b], 1)

            def window_sums(b, h):
                dve.wait_ge(exp_ready[b], h + 1)
                rows3 = sc[b][:].rearrange("p (r j) -> p r j", j=BRANCHES[b]["w"])
                step(dve.tensor_reduce(stat[b][:, 1, :], rows3, AX.X, ALU.add))
                settle()
                step(dve.reciprocal(stat[b][:, 2, :], stat[b][:, 1, :]))

            def window_values(b, h):
                br = BRANCHES[b]
                w, nh = br["w"], br["nh"]
                if values_on_pe(b, h):
                    dve.wait_ge(wv_ps[b], wv_before(b, h))
                    values = window_out(b, h).rearrange("p (d r) -> p d r", d=HD)
                else:
                    dve.wait_ge(wv_ready[b], HD * (h + 1))
                    step(dve.tensor_reduce(ou[:], prod[b][:].rearrange("p d (r j) -> p d r j", j=w), AX.X, ALU.add))
                    values = ou[:]
                settle()
                dve.wait_ge(cleared, 4)
                if h:
                    dve.wait_ge(ot_ps[b], h)
                for g in range(br["groups"]):
                    r = slice(g * br["slots"], (g + 1) * br["slots"])
                    dst = ox[b][r, 0:w, g * HD * nh:(g + 1) * HD * nh].rearrange("p i (h d) -> p d i h", d=HD)
                    src = values[r].rearrange("p d (i h) -> p d i h", h=nh)
                    rec = spread(stat[b][r, 2, :].rearrange("p (i h) -> p i h", h=nh), 1, HD)
                    dve.tensor_tensor(dst, src, rec, ALU.mult).then_inc(ox_ready[b], 1)

            def xc_add(h):
                br = BRANCHES[0]
                dve.wait_ge(xc_ps[0], h + 1)
                dve.wait_ge(xc20_ready, 2 * (h + 1))
                n = br["windows"][h]
                at = MARGIN - br["first"][h]
                for a in range(2):
                    chunks = br["chunks"] - a
                    src = ps[:, bank(h, a), :].rearrange("p (i c s) -> p i c s", i=2, s=br["slots"])
                    dst = xcT[:, at:at + (n + 1) * br["w"]]
                    for i in range(2):
                        j = 2 * a + i
                        d = dst[:, j:j + n * br["w"]].rearrange("p (s k) -> p k s", k=br["w"])[:, 0:4 * chunks - 3:4, :]
                        dve.tensor_tensor(d, src[:, i, 0:chunks, 0:n], d, ALU.add).then_inc(xc_ready, 1)

            def xp_squares(h):
                hs = slice(h * TH, (h + 1) * TH)
                dve.wait_ge(xc_tok_ps, h + 1)
                dve.tensor_tensor(xp[h][:], ps[:, bank(h, 2), :].rearrange("p (t d) -> p t d", t=TH), xn[:, hs, :],
                                  ALU.add).then_inc(xp_ready, 1)
                dve.wait_ge(xp_ready, h + 1)
                step(dve.tensor_tensor(sq[h][:], xp[h][:], xp[h][:], ALU.mult))
                settle()
                dve.tensor_reduce(ss2[h][:], sq[h][:], AX.X, ALU.add).then_inc(ss2_ready, 1)

            def xp_norm(h):
                dve.wait_ge(rstd2_ready, h + 1)
                dve.tensor_tensor(sq[h][:], xp[h][:], spread(rstd2[h][:], 2, D), ALU.mult).then_inc(h_ready, 1)

            def moments(src, h, stats):
                for t in range(TH):
                    step(dve.bn_stats(st2[h][:, t, :], src[:, t, :]))
                settle()
                for t in range(TH):
                    dve.bn_aggr(mv2[h][:, t, :], st2[h][:, t, :]).then_inc(stats, 1)

            def layernorm(src, h, stats, rstd_ready, ready):
                dve.wait_ge(stats, TH * (h + 1))
                dve.wait_ge(rstd_ready, h + 1)
                for t in range(TH):
                    dve.tensor_scalar(xl[h][:, t, :], src[:, t, :], mv2[h][:, t, 0:1], rstd3[h][:, t:t + 1],
                                      ALU.subtract, ALU.mult).then_inc(ready, 1)

            def x1_moments(h):
                dve.wait_ge(ffn_ps, h + 1)
                dve.wait_ge(xs_ready, h + 1)
                dve.tensor_tensor(x1[h][:], ps[:, bank(h, 2), :].rearrange("p (t d) -> p t d", t=TH),
                                  xs[:, h * TH:(h + 1) * TH, :], ALU.add).then_inc(x1_ready, 1)
                dve.wait_ge(x1_ready, h + 1)
                moments(x1[h], h, stats2)

            def x1_norm(h):
                layernorm(x1[h], h, stats2, rstd3_ready, xl_ready)

            def row_max(t):
                dve.wait_ge(s_ps, t + 1)
                dve.tensor_reduce(nmx[:, t:t + 1], score_banks(t)[:, 0:P * (t + 1)], AX.X, ALU.max,
                                  negate=True).then_inc(max_ready, 1)

            def pT_copy(t):
                for n, (engine, a, z) in enumerate(pT_parts(t)):
                    if engine == "dve":
                        dve.wait_ge(pT_ps, parts_before(t) + n + 1)
                        if t >= 2:
                            dve.wait_ge(pv_ps, t - 1)
                        dve.tensor_copy(prT[:, t % 2, a * P:z * P],
                                        ps[:, bank(t // TH, 2), 0:(z - a) * P]).then_inc(pT_dve, 1)

            def x2_tile(t):
                h = t // TH
                dve.wait_ge(p_ready, t + 1)
                step(dve.reciprocal(rden[:, t:t + 1], den[:, t:t + 1]))
                settle()
                dve.wait_ge(pv_ps, t + 1)
                dve.scalar_tensor_tensor(x2[h][:, t % TH, :], ps[:, bank(h, 3), 0:D], rden[:, t:t + 1],
                                         x1[h][:, t % TH, :], ALU.mult, ALU.add).then_inc(x2_ready, 1)

            def x2_moments(h):
                dve.wait_ge(x2_ready, TH * (h + 1))
                moments(x2[h], h, stats3)

            def x2_norm(h):
                layernorm(x2[h], h, stats3, rstd4_ready, xf_ready)

            def router_logits(h):
                dve.wait_ge(lg_ps, h + 1)
                logits = ps[:, bank(h, 3), 0:TH * E].rearrange("p (t e) -> p t e", t=TH)
                step(dve.tensor_tensor(lg[h][:], logits, spread(rows_sb[:, R_RB:R_RB + E], 1, TH), ALU.add))
                settle()
                step(dve.tensor_reduce(lmx[h][:], lg[h][:], AX.X, ALU.max))
                settle()
                dve.tensor_tensor(lg[h][:], lg[h][:], spread(lmx[h][:], 2, E), ALU.subtract).then_inc(lg_ready, 1)

            def router(h):
                dve.wait_ge(lexp_ready, h + 1)
                step(dve.tensor_reduce(lsum[h][:], lg[h][:], AX.X, ALU.add))
                settle()
                step(dve.reciprocal(lmx[h][:], lsum[h][:]))
                settle()
                step(dve.tensor_tensor(lg[h][:], lg[h][:], spread(lmx[h][:], 2, E), ALU.mult))
                settle()
                for op, dst in ((ALU.is_gt, gt[h]), (ALU.is_equal, eq[h])):
                    step(dve.tensor_tensor(dst[:].rearrange("p t (e f) -> p t e f", e=E), spread(lg[h][:], 2, E),
                                           spread(lg[h][:], 3, E), op))
                settle()
                step(dve.tensor_tensor(eq[h][:], eq[h][:], spread(tri_sb[:], 1, TH), ALU.mult))
                settle()
                step(dve.tensor_tensor(gt[h][:], gt[h][:], eq[h][:], ALU.add))
                settle()
                step(dve.tensor_reduce(eq[h][:, :, 0:E], gt[h][:].rearrange("p t (e f) -> p t e f", e=E), AX.X, ALU.add))
                settle()
                dve.scalar_tensor_tensor(wts[h][:, :, 0:E], eq[h][:, :, 0:E], 2.0, lg[h][:], ALU.is_lt, ALU.mult)\
                   .then_inc(wts_ready, 1)

            def acc_begin(h):
                dve.wait_ge(b2_ps, h + 1)
                dve.wait_ge(xf_ready, TH * (h + 1))
                dve.tensor_tensor(x2[h], ps[:, bank(h, 3), :].rearrange("p (t d) -> p t d", t=TH), x2[h], ALU.add).then_inc(acc_start, 1)

            def moe_add(h, e):
                k = h * EX + e
                if e == 0:
                    dve.wait_ge(wts_ready, h + 1)
                    dve.wait_ge(acc_start, h + 1)
                else:
                    dve.wait_ge(moe_taken, k * TH)
                dve.wait_ge(moe_ps, k + 1)
                for t in range(TH):
                    g = h * TH + t
                    dve.scalar_tensor_tensor(acc[:, g, :], ps[:, 2 + k % 2, t * D:(t + 1) * D], wts[h][:, t, e:e + 1],
                                             acc[:, g, :], ALU.mult, ALU.add).then_inc(moe_taken, 1)

            window_product(0, 0, 0)
            window_product(1, 0, 0)
            window_product(1, 0, 1)
            window_product(1, 0, 2)
            window_product(1, 0, 3)
            window_product(0, 0, 1)
            window_product(0, 0, 2)
            window_product(0, 0, 3)
            window_scores(1, 0)
            window_weighted(1, 0, 0)
            window_weighted(1, 0, 1)
            window_weighted(1, 0, 2)
            window_weighted(1, 0, 3)
            window_scores(0, 0)
            window_sums(1, 0)
            window_weighted(0, 0, 0)
            window_weighted(0, 0, 1)
            window_weighted(0, 0, 2)
            window_weighted(0, 0, 3)
            window_values(1, 0)
            window_product(1, 1, 0)
            window_product(1, 1, 1)
            window_product(1, 1, 2)
            window_product(1, 1, 3)
            window_sums(0, 0)
            window_values(0, 0)
            window_product(0, 1, 0)
            window_product(0, 1, 1)
            window_product(0, 1, 2)
            window_product(0, 1, 3)
            window_scores(1, 1)
            xc_add(0)
            window_weighted(1, 1, 0)
            window_weighted(1, 1, 1)
            window_sums(1, 1)
            window_scores(0, 1)
            window_weighted(1, 1, 2)
            window_weighted(1, 1, 3)
            window_sums(0, 1)
            window_weighted(0, 1, 0)
            window_weighted(0, 1, 1)
            window_weighted(0, 1, 2)
            window_weighted(0, 1, 3)
            xp_squares(0)
            window_values(1, 1)
            window_values(0, 1)
            xp_norm(0)
            xc_add(1)
            xp_squares(1)
            x1_moments(0)
            xp_norm(1)
            x1_norm(0)
            row_max(0)
            row_max(1)
            x1_moments(1)
            row_max(2)
            pT_copy(0)
            row_max(3)
            x1_norm(1)
            x2_tile(0)
            pT_copy(2)
            x2_tile(1)
            row_max(4)
            x2_tile(2)
            x2_tile(3)
            x2_moments(0)
            pT_copy(4)
            row_max(5)
            x2_norm(0)
            x2_tile(4)
            pT_copy(5)
            row_max(6)
            router_logits(0)
            router(0)
            row_max(7)
            pT_copy(6)
            acc_begin(0)
            moe_add(0, 0)
            x2_tile(5)
            pT_copy(7)
            x2_tile(6)
            moe_add(0, 1)
            moe_add(0, 2)
            x2_tile(7)
            x2_moments(1)
            x2_norm(1)
            moe_add(0, 3)
            moe_add(0, 4)
            moe_add(0, 5)
            router_logits(1)
            router(1)
            moe_add(0, 6)
            moe_add(0, 7)
            acc_begin(1)
            moe_add(0, 8)
            moe_add(1, 0)
            moe_add(1, 1)
            moe_add(1, 2)
            moe_add(1, 3)
            moe_add(1, 4)
            moe_add(1, 5)
            moe_add(1, 6)
            moe_add(1, 7)
            moe_add(1, 8)

        @block.tensor
        def _(pe):
            def mm(dst, lhs, rhs, start=True, stop=True):
                return pe.matmul(dst, lhs, rhs, start=start, stop=stop)

            pe.wait_ge(ld_down, 32)
            mm(ps[:, 7, 0:DI], centre_sb[:], down_sb[:]).then_inc(setup_ps, 1)
            pe.wait_ge(ld_xT, 16)
            pe.wait_ge(downc_ready, 1)
            for t in range(NT):
                last = mm(ps[:, 1, t * DI:(t + 1) * DI], xT_sb[:, t * P:(t + 1) * P], downc[:])
            last.then_inc(xi_ps, 1)
            pe.wait_ge(ld_ctx, 48)
            for a in range(2):
                last = mm(ps[:, 6 + a, :], wqT_sb[:], ctxT_sb[:, a * 512:(a + 1) * 512])
            last.then_inc(k_ps, 1)

            def channels(b):
                for t in range(NT):
                    last = pe.transpose(ps[0:C, 2 + 2 * b + t // 4, (t % 4) * P:(t % 4 + 1) * P],
                                        xi2[:, t, b * C:(b + 1) * C], ident[:])
                last.then_inc(win_ps[b], 1)

            def qkv_rows(b, h):
                br = BRANCHES[b]
                pe.wait_ge(win_ready[b], h + 1)
                if h == 1:
                    pe.wait_ge(win_ready[1], 2)
                cols = winT[b][:, h * XCOLS:h * XCOLS + br["slots"] * br["w"]]
                cols = cols.rearrange("p (s i) -> p i s", i=br["w"])
                n, s = br["cols"], br["slots"]
                for i in range(br["w"]):
                    for g in range(br["groups"]):
                        last = mm(ps[g * s:(g + 1) * s, qkv_bank(b, h), i * n:(i + 1) * n], cols[:, i, :],
                                  qkvw_sb[:, b, g * n:(g + 1) * n])
                last.then_inc(qkv_ps[b], 1)

            pe.wait_ge(xin_ready, 1)
            pe.wait_ge(ld_vec, 48)
            channels(1)
            channels(0)
            pe.wait_ge(ld_qkvw, 16)
            pe.wait_ge(win_clear, 4)
            qkv_rows(1, 0)
            pe.wait_ge(xi_taken, 1)
            qkv_rows(0, 0)

            def proj_up():
                pe.wait_ge(ld_proj, 48)
                pe.wait_ge(qkv_act[1], 1)
                for b in range(2):
                    mm(ps[:, 0, 128 * b:128 + 128 * b], projT_sb[:, b, :], up_sb[:, b, :])
                mm(ps[:, 0, 256:257], upb_sb[:], cols_sb[0:DI, V_PB:V_PB + 1]).then_inc(setup_ps, 1)

            def qk_sum(b, h, n):
                banks = window_sum(b, h)
                if n == 0:
                    pe.wait_ge(qkv_act[b], h + 1)
                    if b == 1 and h == 0:
                        pe.wait_ge(win_ready[0], 2)
                        pe.wait_ge(half_ready, 1)
                    if b == 1 and h == 1:
                        pe.wait_ge(k_ready, 1)
                pe.wait_ge(qk_ready[b], sum(qk_parts(u) for u in range(h)) + n + 1)
                src = prod[b][:, n * HD // qk_parts(h), :]
                for a in range(b + 1):
                    last = mm(banks[:, a, :], half_ident[:], src[:, 400 * a:400 * a + 400],
                              start=(n == 0), stop=(n == qk_parts(h) - 1))
                if n == qk_parts(h) - 1:
                    last.then_inc(qk_ps[b], 1)
                if n == 0:
                    if h == 0:
                        pe.wait_ge(relb_ready, 8 if b else 12)
                    else:
                        pe.wait_ge(ld_bias, 32)
                    for a in range(b + 1):
                        mm(banks[:, a, :], ident[:], relb[b][h][:, 400 * a:400 * a + 400], start=False, stop=False)

            def value_sum(b, h, d):
                w = BRANCHES[b]["w"]
                n = w * BRANCHES[b]["nh"]
                if b == 1 and h == 0:
                    pe.wait_ge(pu_ready, 8)
                    pe.wait_ge(out_bias_ready, 1)
                pe.wait_ge(wv_ready[b], HD * h + d + 2)
                src = prod[b][:, d:d + 2, :].rearrange("p d (r j) -> p d r j", j=w)
                dst = window_out(b, h)[:, d * n:(d + 2) * n].rearrange("p (d r) -> p d r", d=2)
                for j in range(w):
                    last = mm(dst, ident[:], src[:, :, :, j], start=(j == 0), stop=(j == w - 1))
                if d + 2 == HD:
                    last.then_inc(wv_ps[b], 1)

            def scores_side():
                pe.wait_ge(ffn_h_ready, NC)
                for a in range(2):
                    last = mm(ps[:, a, :], wq_sb[:], kT[:, a * 512:(a + 1) * 512])
                last.then_inc(g_ps, 1)

            def v_rows():
                pe.wait_ge(g_ready, 1)
                for t in range(NT):
                    last = pe.transpose(ps[:, t // 4, (t % 4) * P:(t % 4 + 1) * P], kT[:, t * P:(t + 1) * P], ident[:])
                last.then_inc(v_ps, 1)

            def out_columns(b, h):
                br = BRANCHES[b]
                pe.wait_ge(ox_ready[b], br["groups"] * (h + 1))
                if h == 0:
                    pe.wait_ge(ld_ffn, 48)
                s = br["slots"]
                fold_ap = fold_sb[:, 0:64] if b == 0 else fold_sb[:, 64:96]
                for c in range(br["chunks"]):
                    last = mm(ps[:, bank(h, 1 - b), c * s:(c + 1) * s],
                              ox[b][:, 4 * c:4 * c + 4, :].rearrange("p i c -> p (i c)"), fold_ap)
                last.then_inc(ot_ps[b], 1)

            def out_project(b, h):
                br = BRANCHES[b]
                s, n = br["slots"], br["chunks"]
                pe.wait_ge(ot_ready[b], h + 1)
                at = bank(h, 2 * b)
                for i in range(4):
                    cols = (n if i < 2 or br["w"] % 4 == 0 else n - 1) * s
                    last = mm(ps[:, at + i // 2, (i % 2) * 256:(i % 2) * 256 + cols], pu[b][:, i, :], ot[b][:, 0:cols])
                last.then_inc(xc_ps[b], 1)

            def to_tokens(h):
                pe.wait_ge(xc_ready, 4 * (h + 1))
                pe.wait_ge(xc20_ready, 2 * (h + 1))
                for t in range(TH):
                    at = MARGIN + (h * TH + t) * P
                    last = pe.transpose(ps[:, bank(h, 2), t * P:(t + 1) * P], xcT[:, at:at + P], ident[:])
                last.then_inc(xc_tok_ps, 1)

            def h_columns(h):
                pe.wait_ge(h_ready, h + 1)
                for t in range(TH):
                    last = pe.transpose(ps[:, bank(h, 3), t * P:(t + 1) * P], sq[h][:, t, :], ident[:])
                last.then_inc(hT_ps, 1)

            def ffn_hidden(h, c):
                pe.wait_ge(hT_ready, h + 1)
                mm(ps[:, bank(h, c), :], ffn_w1_sb[:, c * P:(c + 1) * P], hT[h][:]).then_inc(ffn_h_ps, 1)

            def ffn_output(h):
                pe.wait_ge(xp_ready, h + 1)
                pe.wait_ge(ffn_h_ready, NC * (h + 1))
                for t in range(TH):
                    for c in range(NC):
                        last = mm(ps[:, bank(h, 2), t * D:(t + 1) * D], ffn_hid[h][:, c, t * P:(t + 1) * P],
                                  ffn_w2_sb[:, c, :], start=(c == 0), stop=(c == NC - 1))
                last.then_inc(ffn_ps, 1)

            def xl_columns(h):
                pe.wait_ge(xl_ready, TH * (h + 1))
                for t in range(TH):
                    last = pe.transpose(ps[:, bank(h, 3), t * P:(t + 1) * P], xl[h][:, t, :], ident[:])
                last.then_inc(xlT_ps, 1)

            def scores(t):
                h = t // TH
                if t % TH == 0:
                    pe.wait_ge(xlT_ready, h + 1)
                    pe.wait_ge(ffn_h_ready, NC * (h + 1))
                if t == 0:
                    pe.wait_ge(v_ready, 1)
                    pe.wait_ge(casts, 2)
                back = 2 if h == 0 else 1
                if t % TH >= back:
                    pe.wait_ge(p_ready, t - back + 1)
                q = xlT[h][:, (t % TH) * P:(t % TH + 1) * P]
                for a in range(t // 4 + 1):
                    n = min(512, P * (t + 1) - a * 512)
                    dst = score_banks(t)[:, a * 512:a * 512 + n]
                    diagonal = a == t // 4
                    last = mm(dst, q, gT[:, a * 512:a * 512 + n], stop=not diagonal)
                    if diagonal:
                        last = mm(dst[:, n - P:n], ident16[:], causal16[:], start=False)
                last.then_inc(s_ps, 1)

            def columns_copied(t, n):
                before = [e for u in range(t) for e, _, _ in pT_parts(u)] + [e for e, _, _ in pT_parts(t)[:n]]
                if before.count("act"):
                    pe.wait_ge(pT_act, before.count("act"))
                if before.count("dve"):
                    pe.wait_ge(pT_dve, before.count("dve"))

            def p_columns(t, n):
                pe.wait_ge(p_ready, t + 1)
                if t % TH == 0:
                    pe.wait_ge(x1_ready, t // TH + 1)
                columns_copied(t, n)
                _, a, z = pT_parts(t)[n]
                for k in range(a, z):
                    last = pe.transpose(ps[:, bank(t // TH, 2), (k - a) * P:(k - a + 1) * P],
                                        pr[:, t % 2, k * P:(k + 1) * P], ident[:])
                last.then_inc(pT_ps, 1)

            def values(t):
                columns_copied(t, len(pT_parts(t)))
                if t % TH:
                    pe.wait_ge(x2_ready, t)
                for k in range(t + 1):
                    last = mm(ps[:, bank(t // TH, 3), 0:D], prT[:, t % 2, k * P:(k + 1) * P], v_sb[:, k, :],
                              start=(k == 0), stop=(k == t))
                last.then_inc(pv_ps, 1)

            def xf_columns(h):
                pe.wait_ge(xf_ready, TH * (h + 1))
                for t in range(TH):
                    last = pe.transpose(ps[:, bank(h, 2), t * P:(t + 1) * P], xl[h][:, t, :], ident[:])
                last.then_inc(xfT_ps, 1)

            def router_logits(h):
                pe.wait_ge(xfT_ready, h + 1)
                pe.wait_ge(ld_router, 48)
                for t in range(TH):
                    last = mm(ps[:, bank(h, 3), t * E:(t + 1) * E], xfT[h][:, t * P:(t + 1) * P], router_sb[:])
                last.then_inc(lg_ps, 1)

            def weight_rows(h):
                pe.wait_ge(wts_ready, h + 1)
                for t in range(TH):
                    last = pe.transpose(ps[0:EX, bank(h, 2), t * P:(t + 1) * P], wts[h][:, t, :], ident[:])
                last.then_inc(wT_ps, 1)

            def expert_bias(h):
                pe.wait_ge(wT_ready, h + 1)
                pe.wait_ge(ld_moe, 48)
                for t in range(TH):
                    last = mm(ps[:, bank(h, 3), t * D:(t + 1) * D], wT[h][:, t * P:(t + 1) * P], moe_b2_sb[:])
                last.then_inc(b2_ps, 1)

            def hidden(h, e, c):
                k = h * EX + e
                if e == 0:
                    pe.wait_ge(xfT_ready, h + 1)
                if k == 0:
                    pe.wait_ge(ld_moe, 48)
                    pe.wait_ge(p_ready, TH)
                else:
                    pe.wait_ge(moe_h_ready, NC * (k - 1) + c + 1)
                mm(ps[:, c, :], moe_w1_sb[:, e, c * P:(c + 1) * P], xfT[h][:]).then_inc(moe_h_ps, 1)

            def output(h, e):
                k = h * EX + e
                pe.wait_ge(moe_h_ready, NC * (k + 1))
                if k == 0:
                    pe.wait_ge(wT_ready, 1)
                elif k == 1:
                    pe.wait_ge(acc_start, 1)
                else:
                    pe.wait_ge(moe_taken, TH * (k - 1))
                for t in range(TH):
                    for c in range(NC):
                        last = mm(ps[:, 2 + k % 2, t * D:(t + 1) * D], hid[:, k % 2, c, t * P:(t + 1) * P],
                                  moe_w2_sb[:, e, c, :], start=(c == 0), stop=(c == NC - 1))
                last.then_inc(moe_ps, 1)

            proj_up()
            qkv_rows(0, 1)
            qk_sum(1, 0, 0)
            qk_sum(1, 0, 1)
            qkv_rows(1, 1)
            qk_sum(0, 0, 0)
            qk_sum(0, 0, 1)
            value_sum(1, 0, 0)
            value_sum(1, 0, 2)
            out_columns(1, 0)
            qk_sum(1, 1, 0)
            qk_sum(1, 1, 1)
            qk_sum(1, 1, 2)
            qk_sum(1, 1, 3)
            out_columns(0, 0)
            out_project(1, 0)
            out_project(0, 0)
            qk_sum(0, 1, 0)
            qk_sum(0, 1, 1)
            to_tokens(0)
            qk_sum(0, 1, 2)
            qk_sum(0, 1, 3)
            value_sum(1, 1, 0)
            value_sum(1, 1, 2)
            value_sum(0, 1, 0)
            value_sum(0, 1, 2)
            out_columns(1, 1)
            out_columns(0, 1)
            out_project(1, 1)
            h_columns(0)
            out_project(0, 1)
            ffn_hidden(0, 0)
            ffn_hidden(0, 1)
            to_tokens(1)
            ffn_output(0)
            scores_side()
            h_columns(1)
            v_rows()
            ffn_hidden(1, 0)
            xl_columns(0)
            ffn_hidden(1, 1)
            scores(0)
            scores(1)
            ffn_output(1)
            scores(2)
            p_columns(0, 0)
            scores(3)
            p_columns(1, 0)
            values(0)
            p_columns(2, 0)
            xl_columns(1)
            values(1)
            p_columns(3, 0)
            scores(4)
            values(2)
            values(3)
            p_columns(4, 0)
            scores(5)
            p_columns(4, 1)
            values(4)
            xf_columns(0)
            p_columns(5, 0)
            scores(6)
            p_columns(5, 1)
            router_logits(0)
            hidden(0, 0, 0)
            hidden(0, 0, 1)
            scores(7)
            hidden(0, 1, 0)
            hidden(0, 1, 1)
            weight_rows(0)
            hidden(0, 2, 0)
            p_columns(6, 0)
            output(0, 0)
            p_columns(6, 1)
            expert_bias(0)
            hidden(0, 2, 1)
            values(5)
            p_columns(7, 0)
            hidden(0, 3, 0)
            values(6)
            hidden(0, 3, 1)
            p_columns(7, 1)
            output(0, 1)
            output(0, 2)
            hidden(0, 4, 0)
            values(7)
            hidden(0, 4, 1)
            hidden(0, 5, 0)
            output(0, 3)
            hidden(0, 5, 1)
            output(0, 4)
            output(0, 5)
            hidden(0, 6, 0)
            hidden(0, 6, 1)
            xf_columns(1)
            hidden(0, 7, 0)
            hidden(0, 7, 1)
            router_logits(1)
            hidden(0, 8, 0)
            output(0, 6)
            output(0, 7)
            hidden(0, 8, 1)
            hidden(1, 0, 0)
            weight_rows(1)
            hidden(1, 0, 1)
            hidden(1, 1, 0)
            expert_bias(1)
            hidden(1, 1, 1)
            output(0, 8)
            output(1, 0)
            hidden(1, 2, 0)
            hidden(1, 2, 1)
            output(1, 1)
            output(1, 2)
            hidden(1, 3, 0)
            hidden(1, 3, 1)
            hidden(1, 4, 0)
            hidden(1, 4, 1)
            output(1, 3)
            output(1, 4)
            hidden(1, 5, 0)
            hidden(1, 5, 1)
            hidden(1, 6, 0)
            hidden(1, 6, 1)
            output(1, 5)
            output(1, 6)
            hidden(1, 7, 0)
            hidden(1, 7, 1)
            hidden(1, 8, 0)
            hidden(1, 8, 1)
            output(1, 7)
            output(1, 8)


def kernel(**inputs):
    import numpy as np
    import concourse.bacc as bacc
    from concourse.bass_utils import run_bass_kernel_spmd

    a = {n: np.asarray(v) for n, v in inputs.items()}
    f = np.float32

    def attn(name):
        return a["L0_attn_" + name]

    def moe(name):
        return a["L0_ffn_" + name]

    def grouped(n, groups):
        w = np.concatenate([attn(f"qkv{n}_w"), attn(f"qkv{n}_b")[None]], 0)
        return w.reshape(C + 1, 3, groups, -1).transpose(0, 2, 1, 3).reshape(C + 1, QKV)

    def relative(n, br):
        i = np.arange(br["w"])
        r = attn(f"rpb{n}")[i[:, None] - i[None, :] + br["w"] - 1]
        r = r.reshape(br["w"], br["w"], br["groups"], br["nh"]).transpose(2, 0, 3, 1)
        return np.repeat(r.reshape(br["groups"], -1), br["slots"], 0)

    cols = np.zeros((P, NV), f)
    cols[:, V_N2] = attn("norm2_w")
    cols[:, V_B1:V_B1 + NC] = attn("ffn_b1").reshape(NC, P).T
    cols[:, V_UPB] = attn("up_b")
    cols[:DI, V_PB] = np.concatenate([attn("proj1_b"), attn("proj2_b")])
    cols[:C, V_N1:V_N1 + 2] = attn("norm1_w").reshape(2, C).T
    b1 = np.concatenate([moe("rb1"), moe("sb1")[None]], 0)
    cols[:, V_EB1:] = b1.reshape(EX * NC, P).T
    rows = np.concatenate([attn("down_b"), attn("ffn_b2"), moe("router_b")])
    slot = np.arange(P)
    arrays = {
        "x": a["x"],
        "x_t": a["x"][0].T,
        "ctx_t": a["ctx_1024"][0, :T].T,
        "wq": a["L0_xattn_Wq"],
        "wq_t": a["L0_xattn_Wq"].T,
        "down_w": attn("down_w"),
        "centre": (np.eye(P) - 1.0 / P).astype(f),
        "identity": np.eye(P, dtype=f),
        "causal": np.triu(np.full((P, P), MASKED, f), 1),
        "up_w": attn("up_w"),
        "proj_t": np.stack([np.tile(attn(f"proj{n}_w").T, (1, 4)) for n in (1, 2)], 1),
        "qkv_w": np.stack([grouped(n, br["groups"]) for n, br in zip((1, 2), BRANCHES)], 1),
        "bias10": relative(1, BRANCHES[0]),
        "bias20": relative(2, BRANCHES[1]),
        "fold": np.concatenate([slot[:, None] % br["slots"] == np.arange(br["slots"]) for br in BRANCHES], 1).astype(f),
        "ffn_w1": attn("ffn_w1"),
        "ffn_w2": attn("ffn_w2"),
        "router_w": moe("router_w"),
        "tri": np.tile(np.tril(np.ones((E, E), f), -1).reshape(1, -1), (P, 1)),
        "cols": cols,
        "rows": rows,
        "moe_w1": np.concatenate([moe("rw1"), moe("sw1")[None]], 0),
        "moe_w2": np.concatenate([moe("rw2"), moe("sw2")[None]], 0),
        "moe_b2": np.concatenate([moe("rb2"), moe("sb2")[None]], 0),
    }
    arrays = {n: np.ascontiguousarray(v) for n, v in arrays.items()}
    nc = bacc.Bacc("TRN2", target_bir_lowering=False, num_devices=1)
    args = {n: nc.dram_tensor("in_" + n, v.shape, F32, kind="ExternalInput").ap() for n, v in arrays.items()}
    out = nc.dram_tensor("out", (1, T, D), F32, kind="ExternalOutput").ap()
    decoder_layer(nc, out=out, **args)
    r = run_bass_kernel_spmd(nc, [{"in_" + n: v for n, v in arrays.items()}], core_ids=[0])
    return r.results[0]["out"]
```

```python
from contextlib import ExitStack

import concourse.bass as bass
from concourse import mybir

F32 = mybir.dt.float32
F32R = mybir.dt.float32r
BF16 = mybir.dt.bfloat16
ALU = mybir.AluOpType
ACT = mybir.ActivationFunctionType
AX = mybir.AxisListType

P = 128
T = 1024
D = 128
NT = T // P
HALVES = 2
TH = NT // HALVES
CH = T // HALVES
DI = 64
C = DI // 2
HD = 4
HID = 256
NC = HID // P
E = 8
EX = E + 1
QKV = 3 * C
MASKED = -(2.0 ** 100)

BRANCHES = (dict(w=10, groups=2, windows=(52, 51)), dict(w=20, groups=4, windows=(27, 25)))
for _b in BRANCHES:
    _b["shift"] = _b["w"] // 2
    _b["slots"] = P // _b["groups"]
    _b["nh"] = 8 // _b["groups"]
    _b["cols"] = 3 * HD * _b["nh"]
    _b["chunks"] = -(-_b["w"] // 4)
    _b["first"] = (_b["shift"], _b["shift"] - _b["windows"][0] * _b["w"])
FRONT = -(-max(_b["windows"][0] * _b["w"] - _b["shift"] for _b in BRANCHES) // P)
PARTS = (slice(0, FRONT), slice(FRONT, NT))

BIAS_AT = (BRANCHES[1]["w"] * BRANCHES[1]["nh"] * BRANCHES[1]["w"], 0)
BIAS_SEL = BIAS_AT[0] + BRANCHES[0]["w"] * BRANCHES[0]["nh"] * BRANCHES[0]["w"]
BIAS_COLS = BIAS_SEL + 2 * P
BIAS_LOW, BIAS_MASK, BIAS_ROWS = 32, 64, 65
XCOLS = 640
MARGIN = BRANCHES[1]["shift"]

V_N2, V_B1, V_UPB, V_PB, V_N1, V_EB1 = 0, 1, 3, 4, 5, 7
NV = V_EB1 + EX * NC
R_DB, R_B2, R_RB = 0, DI, DI + D
NR = R_RB + E


def spread(ap, axis, n):
    ap = ap.unsqueeze(axis)
    shape = list(ap.shape)
    shape[axis] = n
    return ap.broadcast_to(shape)


def decoder_layer(nc, x, x_t, ctx_t, wq, wq_t, down_centre, identity, causal, up_w, proj_t, qkv_w,
                  bias, fold, ffn_w1, ffn_w2, router_w, tri, cols, rows, moe_w1, moe_w2, moe_b2, out):
    with ExitStack() as stack:
        def sb(name, shape, dt=F32):
            return stack.enter_context(nc.sbuf_tensor(name, shape, dt))

        def sem(name):
            return stack.enter_context(nc.semaphore(name))

        ps = stack.enter_context(nc.psum_tensor("ps", [P, 8, 512], F32))

        x_sb = sb("x_sb", [P, NT, D])
        wq_sb = sb("wq_sb", [P, D])
        ident = sb("ident", [P, P])
        causal_sb = sb("causal_sb", [P, P])
        up_sb = sb("up_sb", [C, 2, D])
        upb_sb = sb("upb_sb", [DI, D])
        projT_sb = sb("projT_sb", [C, 2, P])
        qkvw_sb = sb("qkvw_sb", [C + 1, 2, QKV])
        fold_sb = sb("fold_sb", [P, 96])
        ffn_w1_sb = sb("ffn_w1_sb", [P, HID])
        ffn_w2_sb = sb("ffn_w2_sb", [P, NC, D])
        router_sb = sb("router_sb", [P, E])
        tri_sb = sb("tri_sb", [P, E * E])
        cols_sb = sb("cols_sb", [P, NV])
        rows_sb = sb("rows_sb", [P, NR])
        moe_w1_sb = sb("moe_w1_sb", [P, EX, HID])
        moe_w2_sb = sb("moe_w2_sb", [P, EX, NC, D])
        moe_b2_sb = sb("moe_b2_sb", [EX, D])
        elems = [b["w"] * b["nh"] * b["w"] for b in BRANCHES]

        bias_parts = sb("bias_parts", [BIAS_ROWS, BIAS_COLS], F32R)
        ident16 = sb("ident16", [P, P], BF16)
        causal16 = sb("causal16", [P, P], BF16)
        minus_half = sb("minus_half", [P, NT])
        downc = sb("downc", [P, DI])
        pu = [sb(f"pu{b['w']}", [P, 4, D]) for b in BRANCHES]
        out_bias = sb("out_bias", [P, 1])

        st = sb("st", [P, NT, 6])
        mv = sb("mv", [P, NT, 2])
        rstd0 = sb("rstd0", [P, NT])
        xn = sb("xn", [P, NT, D])
        xs = sb("xs", [P, NT, D])
        xi = sb("xi", [P, NT, DI])
        xi2 = sb("xi2", [P, NT, DI])
        ss = sb("ss", [P, NT])
        rstd1 = sb("rstd1", [P, NT])
        qkv = [[sb(f"qkv{b['w']}_{h}", [P, b["w"], b["cols"]]) for h in range(2)] for b in BRANCHES]
        prod = [sb(f"prod{b['w']}", [P, HD, n]) for b, n in zip(BRANCHES, elems)]
        half_ident = sb("half_ident", [P, P])
        sc = [sb(f"sc{b['w']}", [P, n]) for b, n in zip(BRANCHES, elems)]
        stat = [sb(f"stat{b['w']}", [P, 3, b["w"] * b["nh"]]) for b in BRANCHES]
        ox = [sb(f"ox{b['w']}", [P, 4 * b["chunks"], C]) for b in BRANCHES]
        ot = [sb(f"ot{b['w']}", [P, b["chunks"] * b["slots"]]) for b in BRANCHES]
        xcT = sb("xcT", [P, 1100])

        xp = [sb(f"xp_{h}", [P, TH, D]) for h in range(2)]
        ss2 = [sb(f"ss2_{h}", [P, TH]) for h in range(2)]
        rstd2 = [sb(f"rstd2_{h}", [P, TH]) for h in range(2)]
        ffn_hid = [sb(f"ffn_hid_{h}", [P, NC, CH]) for h in range(2)]
        hid = sb("hid", [P, 2, NC, CH])
        bias_sb = hid[0:BIAS_ROWS].rearrange("p a c n -> p (a c n)")[:, 0:BIAS_COLS]
        x1 = [sb(f"x1_{h}", [P, TH, D]) for h in range(2)]
        st2 = [sb(f"st2_{h}", [P, TH, 6]) for h in range(2)]
        mv2 = [sb(f"mv2_{h}", [P, TH, 2]) for h in range(2)]
        rstd3 = [sb(f"rstd3_{h}", [P, TH]) for h in range(2)]
        xl = [sb(f"xl_{h}", [P, TH, D]) for h in range(2)]
        xlT = [sb(f"xlT_{h}", [P, CH]) for h in range(2)]
        kT = sb("kT", [P, T])
        gT = sb("gT", [P, T])
        v_sb = sb("v_sb", [P, NT, D])
        pr = sb("pr", [P, 2, T])
        prT = sb("prT", [P, 2, T])
        nmx = sb("nmx", [P, NT])
        den = sb("den", [P, NT])
        rden = sb("rden", [P, NT])
        xfT = [sb(f"xfT_{h}", [P, CH]) for h in range(2)]
        lg = [sb(f"lg_{h}", [P, TH, E]) for h in range(2)]
        lmx = [sb(f"lmx_{h}", [P, TH]) for h in range(2)]
        lsum = [sb(f"lsum_{h}", [P, TH]) for h in range(2)]
        gt = [sb(f"gt_{h}", [P, TH, E * E]) for h in range(2)]
        eq = [sb(f"eq_{h}", [P, TH, E * E]) for h in range(2)]
        wts = [sb(f"wts_{h}", [P, TH, EX]) for h in range(2)]
        wT = [sb(f"wT_{h}", [EX, CH]) for h in range(2)]
        acc = sb("acc", [P, NT, D])
        x2 = [acc[:, h * TH:(h + 1) * TH, :] for h in range(2)]

        with ExitStack() as first:
            def sb1(name, shape):
                return first.enter_context(nc.sbuf_tensor(name, shape, F32))

            xT_sb = sb1("xT_sb", [P, T])
            ctxT_sb = sb1("ctxT_sb", [P, T])
            down_sb = sb1("down_sb", [P, DI + P])
            wqT_sb = sb1("wqT_sb", [P, D])
            winT = [sb1(f"winT{b['w']}", [C + 1, HALVES * XCOLS]) for b in BRANCHES]
            hT, sq = [None] * HALVES, [None] * HALVES
            for h in range(HALVES):
                hT[h] = sb1(f"hT_{h}", [P, CH])
                sq[h] = sb1(f"sq_{h}", [P, TH, D])
        w1_hi = sb("w1_hi", [P, EX, HID], F32R)
        sb("w1_gap_1", [P, DI])
        w1_lo = sb("w1_lo", [P, EX, HID], F32R)
        sb("w1_gap_2", [P, 2 * HALVES * XCOLS - EX * HID])
        xf_hi, xf_lo = [None] * HALVES, [None] * HALVES
        for h in range(HALVES):
            xf_hi[h] = sb(f"xf_hi_{h}", [P, CH], F32R)
            xf_lo[h] = sb(f"xf_lo_{h}", [P, CH], F32R)
        assert 2 * T + P + D == EX * HID and P * TH * D == P * CH

        ld_down = sem("ld_down")
        ld_xT = sem("ld_xT")
        ld_x = [sem("ld_x_0"), sem("ld_x_1")]
        ld_vec = sem("ld_vec")
        ld_proj = sem("ld_proj")
        ld_ctx = sem("ld_ctx")
        ld_qkvw = sem("ld_qkvw")
        ld_bias = sem("ld_bias")
        ld_ffn = sem("ld_ffn")
        ld_moe = sem("ld_moe")
        ld_router = sem("ld_router")
        stored = sem("stored")
        dve_step = sem("dve_step")
        pool_step = sem("pool_step")
        cleared = sem("cleared")
        win_clear = sem("win_clear")
        casts = sem("casts")
        bias_high = sem("bias_high")
        bias_ready = sem("bias_ready")
        w1_high_ready = sem("w1_high_ready")
        w1_low_ready = sem("w1_low_ready")
        xf_high_ready = sem("xf_high_ready")
        xf_low_ready = sem("xf_low_ready")
        setup_ps = sem("setup_ps")
        downc_ready = sem("downc_ready")
        pu_ready = sem("pu_ready")
        out_bias_ready = sem("out_bias_ready")
        stats0 = sem("stats0")
        rstd0_ready = sem("rstd0_ready")
        xi_ps = sem("xi_ps")
        xi_taken = sem("xi_taken")
        ss_ready = sem("ss_ready")
        rstd1_ready = sem("rstd1_ready")
        xin_ready = sem("xin_ready")
        win_ps = [sem("win10_ps"), sem("win20_ps")]
        win_ready = [sem("win10_ready"), sem("win20_ready")]
        qkv_ps = [sem("qkv10_ps"), sem("qkv20_ps")]
        qkv_act = [sem("qkv10_act"), sem("qkv20_act")]
        half_ready = sem("half_ready")
        qk_ready = [sem("qk10_ready"), sem("qk20_ready")]
        qk_ps = [sem("qk10_ps"), sem("qk20_ps")]
        wv_ready = [sem("wv10_ready"), sem("wv20_ready")]
        va_ready = [sem("va10_ready"), sem("va20_ready")]
        wv_ps = [sem("wv10_ps"), sem("wv20_ps")]
        sc_ready = [sem("sc10_ready"), sem("sc20_ready")]
        exp_ready = [sem("exp10_ready"), sem("exp20_ready")]
        ox_ready = [sem("ox10_ready"), sem("ox20_ready")]
        ot_ps = [sem("ot10_ps"), sem("ot20_ps")]
        ot_ready = [sem("ot10_ready"), sem("ot20_ready")]
        xc_ps = [sem("xc10_ps"), sem("xc20_ps")]
        xc20_ready = sem("xc20_ready")
        xc_ready = sem("xc_ready")
        xc_tok_ps = sem("xc_tok_ps")
        xp_ready = sem("xp_ready")
        xs_ready = sem("xs_ready")
        ss2_ready = sem("ss2_ready")
        rstd2_ready = sem("rstd2_ready")
        h_ready = sem("h_ready")
        hT_ps = sem("hT_ps")
        hT_ready = sem("hT_ready")
        ffn_h_ps = sem("ffn_h_ps")
        ffn_h_ready = sem("ffn_h_ready")
        ffn_ps = sem("ffn_ps")
        x1_ready = sem("x1_ready")
        stats2 = sem("stats2")
        rstd3_ready = sem("rstd3_ready")
        xl_ready = sem("xl_ready")
        xlT_ps = sem("xlT_ps")
        xlT_ready = sem("xlT_ready")
        k_ps = sem("k_ps")
        k_ready = sem("k_ready")
        g_ps = sem("g_ps")
        g_ready = sem("g_ready")
        v_ps = sem("v_ps")
        v_ready = sem("v_ready")
        s_ps = sem("s_ps")
        max_ready = sem("max_ready")
        p_ready = sem("p_ready")
        pT_ps = sem("pT_ps")
        pT_act = sem("pT_act")
        pT_dve = sem("pT_dve")
        pv_ps = sem("pv_ps")
        x2_ready = sem("x2_ready")
        stats3 = sem("stats3")
        rstd4_ready = sem("rstd4_ready")
        xf_ready = sem("xf_ready")
        xfT_ps = sem("xfT_ps")
        xfT_ready = sem("xfT_ready")
        lg_ps = sem("lg_ps")
        lg_ready = sem("lg_ready")
        lexp_ready = sem("lexp_ready")
        wts_ready = sem("wts_ready")
        wT_ps = sem("wT_ps")
        wT_ready = sem("wT_ready")
        b2_ps = sem("b2_ps")
        acc_start = sem("acc_start")
        moe_h_ps = sem("moe_h_ps")
        moe_h_ready = sem("moe_h_ready")
        moe_ps = sem("moe_ps")
        moe_taken = sem("moe_taken")

        block = stack.enter_context(nc.Block())

        def qkv_bank(b, h):
            return 4 * h + 1 - b

        def window_sum(b, h):
            if b == 0:
                return ps[:, 4 * h + 1:4 * h + 2, 0:400]
            return ps[:, 4 * h + 2:4 * h + 4, 0:400]

        def window_out(b, h):
            return ps[:, 4 * h + 1 - b, 0:HD * BRANCHES[b]["w"] * BRANCHES[b]["nh"]]

        def qk_parts(h):
            return 2 if h == 0 else HD

        def halved(b, h):
            return b == 1 or h == 1

        def bank(h, n):
            return 4 * h + n

        def pT_parts(t):
            if t < 4:
                return [("act" if t % 2 else "dve", 0, t + 1)]
            return [("dve", 0, 4), ("act", 4, t + 1)]

        def pT_count(t, engine):
            return sum(e == engine for u in range(t + 1) for e, _, _ in pT_parts(u))

        def score_banks(t):
            if t < TH:
                return ps[:, t % 2, :]
            return ps[:, 4:6, :].rearrange("p a n -> p (a n)")

        def parts_before(t):
            return sum(len(pT_parts(u)) for u in range(t))

        @block.sync
        def _(sp):
            sp.dma_start(xT_sb[:], x_t).then_inc(ld_xT, 16)
            sp.dma_start(rows_sb[:], rows.partition_broadcast(P)).then_inc(ld_vec, 16)
            sp.dma_start(cols_sb[:], cols).then_inc(ld_vec, 16)
            sp.dma_start(ident[:], identity).then_inc(ld_vec, 16)
            sp.dma_start(qkvw_sb[:], qkv_w).then_inc(ld_qkvw, 16)
            sp.dma_start(bias_sb, bias).then_inc(ld_bias, 16)
            sp.dma_start(wqT_sb[:], wq_t).then_inc(ld_ctx, 16)
            sp.dma_start(ctxT_sb[:], ctx_t).then_inc(ld_ctx, 16)
            sp.dma_start(wq_sb[:], wq).then_inc(ld_ctx, 16)
            sp.dma_start(projT_sb[:], proj_t).then_inc(ld_proj, 16)
            sp.dma_start(up_sb[:], up_w.rearrange("(b c) n -> c b n", b=2)).then_inc(ld_proj, 16)
            sp.dma_start(upb_sb[:], up_w).then_inc(ld_proj, 16)
            sp.dma_start(fold_sb[:], fold).then_inc(ld_ffn, 16)
            sp.dma_start(ffn_w1_sb[:], ffn_w1).then_inc(ld_ffn, 16)
            sp.dma_start(ffn_w2_sb[:], ffn_w2.rearrange("(c p) n -> p c n", p=P)).then_inc(ld_ffn, 16)
            sp.dma_start(causal_sb[:], causal).then_inc(ld_router, 16)
            sp.dma_start(router_sb[:], router_w).then_inc(ld_router, 16)
            sp.dma_start(tri_sb[:], tri).then_inc(ld_router, 16)
            sp.dma_start(moe_w1_sb[:], moe_w1.rearrange("e p n -> p e n")).then_inc(ld_moe, 16)
            sp.dma_start(moe_w2_sb[:], moe_w2.rearrange("e (c p) n -> p e c n", p=P)).then_inc(ld_moe, 16)
            sp.dma_start(moe_b2_sb[:], moe_b2).then_inc(ld_moe, 16)
            out_v = out.rearrange("o (t p) d -> (o p) t d", p=P)
            for h in range(HALVES):
                for t in range(TH):
                    sp.wait_ge(moe_taken, (h * EX + EX - 1) * TH + t + 1)
                    sp.dma_start(out_v[:, h * TH + t, :], acc[:, h * TH + t, :]).then_inc(stored, 16)
            sp.wait_ge(stored, 16 * NT)

        @block.gpsimd
        def _(pool):
            steps = [0]

            def step(ins):
                steps[0] += 1
                ins.then_inc(pool_step, 1)

            def settle():
                pool.wait_ge(pool_step, steps[0])

            step(pool.memset(minus_half[:], -0.5))
            pool.memset(pu[0][:], 0.0).then_inc(cleared, 1)
            pool.memset(pu[1][:], 0.0).then_inc(cleared, 1)
            settle()

            def rstd(dst, src, scale, eps, ready):
                step(pool.tensor_scalar(dst, src, scale, eps, ALU.mult, ALU.add))
                settle()
                pool.tensor_tensor(dst, dst, minus_half[:, 0:dst.shape[1]], ALU.pow).then_inc(ready, 1)

            for part in PARTS:
                pool.wait_ge(stats0, part.stop)
                rstd(rstd0[:, part], mv[:, part, 1], 1.0, 1e-5, rstd0_ready)
            for n, part in enumerate(PARTS):
                pool.wait_ge(ss_ready, n + 1)
                rstd(rstd1[:, part], ss[:, part], 1.0 / DI, 1e-6, rstd1_ready)

            pool.memset(ox[1][:], 0.0).then_inc(cleared, 1)
            pool.memset(ox[0][:], 0.0).then_inc(cleared, 1)
            for h in range(HALVES):
                pool.memset(wts[h][:], 1.0).then_inc(cleared, 1)
            pool.wait_ge(ld_router, 48)
            pool.wait_ge(ld_vec, 48)
            pool.tensor_copy(ident16[:], ident[:]).then_inc(casts, 1)
            pool.tensor_copy(causal16[:], causal_sb[:]).then_inc(casts, 1)

            pool.wait_ge(ld_x[0], 16)
            pool.wait_ge(ld_x[1], 16)
            step(pool.tensor_tensor(xs[:], x_sb[:], spread(rows_sb[:, R_B2:R_B2 + D], 1, NT), ALU.add))
            settle()

            def w1_low():
                pool.wait_ge(w1_high_ready, 1)
                pool.wait_ge(qkv_ps[0], 2)
                pool.wait_ge(qkv_ps[1], 2)
                pool.tensor_tensor(w1_lo[:], moe_w1_sb[:], w1_hi[:].bitcast(F32), ALU.subtract).then_inc(w1_low_ready, 1)

            def rstd2_pow(h):
                pool.wait_ge(ss2_ready, TH * (h + 1))
                rstd(rstd2[h][:], ss2[h][:], 1.0 / D, 1e-6, rstd2_ready)

            def xs_add(h):
                hs = slice(h * TH, (h + 1) * TH)
                pool.wait_ge(xp_ready, h + 1)
                pool.tensor_tensor(xs[:, hs, :], xs[:, hs, :], xp[h][:], ALU.add).then_inc(xs_ready, 1)

            def rstd3_pow(h):
                pool.wait_ge(stats2, TH * (h + 1))
                rstd(rstd3[h][:], mv2[h][:, :, 1], 1.0, 1e-5, rstd3_ready)

            def rstd4_pow(h):
                pool.wait_ge(xl_ready, TH * (h + 1))
                pool.wait_ge(stats3, TH * (h + 1))
                rstd(rstd3[h][:], mv2[h][:, :, 1], 1.0, 1e-5, rstd4_ready)

            w1_low()
            xs_add(0)
            rstd2_pow(0)
            rstd3_pow(0)
            xs_add(1)
            rstd2_pow(1)
            rstd4_pow(0)
            rstd3_pow(1)
            rstd4_pow(1)

        def window_part(b, h):
            a, z = BRANCHES[b]["first"]
            cut = BRANCHES[b]["windows"][0] * BRANCHES[b]["w"] - a
            src = ps[0:C, 2 + 2 * b:4 + 2 * b, :].rearrange("p a n -> p (a n)")
            if h == 0:
                return winT[b][0:C, a:a + cut], src[:, 0:cut]
            return winT[b][0:C, XCOLS + z + cut:XCOLS + z + T], src[:, cut:T]

        @block.scalar
        def _(act):
            act.dma_start(down_sb[:], down_centre).then_inc(ld_down, 16)
            x_v = x.rearrange("o (t p) d -> (o p) t d", p=P)
            for n, part in enumerate(PARTS):
                act.dma_start(x_sb[:, part, :], x_v[:, part, :]).then_inc(ld_x[n], 16)
            act.wait_ge(setup_ps, 1)
            act.activation(downc[:], ps[:, 7, 0:DI], ACT.Copy).then_inc(downc_ready, 1)
            act.wait_ge(ld_vec, 48)
            act.activation(half_ident[:], ident[:], ACT.Copy, scale=0.5).then_inc(half_ready, 1)
            act.wait_ge(ld_bias, 16)
            act.activation(bias_parts[:], bias_sb, ACT.Copy).then_inc(bias_high, 1)

            def window_cols(b, h):
                act.wait_ge(win_ps[b], h + 1)
                act.wait_ge(win_clear, 4)
                dst, src = window_part(b, h)
                act.activation(dst, src, ACT.Copy, scale=cols_sb[0:C, V_N1 + b:V_N1 + b + 1]).then_inc(win_ready[b], 1)

            act.wait_ge(k_ps, 1)
            act.activation(kT[:].rearrange("p (a n) -> p a n", a=2), ps[:, 6:8, :], ACT.Copy).then_inc(k_ready, 1)
            window_cols(0, 0)

            def qkv_copy(b, h):
                br = BRANCHES[b]
                act.wait_ge(qkv_ps[b], h + 1)
                src = ps[:, qkv_bank(b, h), 0:br["w"] * br["cols"]].rearrange("p (i n) -> p i n", i=br["w"])
                act.activation(qkv[b][h][:], src, ACT.Copy).then_inc(qkv_act[b], 1)

            qkv_copy(1, 0)
            qkv_copy(0, 0)
            window_cols(1, 1)
            window_cols(0, 1)

            def g_copy():
                act.wait_ge(g_ps, 1)
                act.activation(gT[:].rearrange("p (a n) -> p a n", a=2), ps[:, 6:8, :], ACT.Copy,
                               scale=float(D) ** -0.5).then_inc(g_ready, 1)

            def w1_high():
                act.wait_ge(ld_moe, 48)
                act.wait_ge(k_ps, 1)
                act.activation(w1_hi[:], moe_w1_sb[:], ACT.Copy).then_inc(w1_high_ready, 1)

            def pu_copy():
                act.wait_ge(setup_ps, 2)
                act.wait_ge(cleared, 2)
                for b in range(2):
                    for g in range(4):
                        r = slice(32 * g, 32 * g + 32)
                        act.activation(pu[b][r, g, :], ps[r, 0, 128 * b:128 + 128 * b], ACT.Copy).then_inc(pu_ready, 1)
                act.activation(out_bias[:], ps[:, 0, 256:257], ACT.Identity,
                               bias=cols_sb[:, V_UPB:V_UPB + 1]).then_inc(out_bias_ready, 1)

            def v_copy():
                act.wait_ge(v_ps, 1)
                act.activation(v_sb[:].rearrange("p (a t) d -> p a (t d)", a=2), ps[:, 6:8, :],
                               ACT.Copy).then_inc(v_ready, 1)

            def window_exp(b, h):
                act.wait_ge(sc_ready[b], h + 1)
                act.activation(sc[b][:], sc[b][:], ACT.Exp).then_inc(exp_ready[b], 1)

            def ot_copy(b, h):
                act.wait_ge(ot_ps[b], h + 1)
                if h:
                    act.wait_ge(xc_ps[b], h)
                act.activation(ot[b][:], ps[:, bank(h, 1 - b), 0:ot[b].shape[1]], ACT.Copy).then_inc(ot_ready[b], 1)

            def xc20_copy(h):
                br = BRANCHES[1]
                act.wait_ge(xc_ps[1], h + 1)
                n = br["windows"][h]
                at = MARGIN - br["first"][h]
                for a in range(2):
                    src = ps[:, bank(h, 2 + a), :].rearrange("p (i c s) -> p i c s", i=2, s=br["slots"])
                    src = src[:, :, 0:br["chunks"], 0:n]
                    dst = xcT[:, at:at + n * br["w"]].rearrange("p (s c i) -> p i c s", c=br["chunks"], i=4)
                    act.activation(dst[:, 2 * a:2 * a + 2], src, ACT.Identity,
                                   bias=out_bias[:, 0:1]).then_inc(xc20_ready, 1)

            def xp_squares(h):
                act.wait_ge(xp_ready, h + 1)
                for t in range(TH):
                    act.activation(sq[h][:, t, :], xp[h][:, t, :], ACT.Square,
                                   accum_out=ss2[h][:, t:t + 1]).then_inc(ss2_ready, 1)

            def hT_copy(h):
                act.wait_ge(hT_ps, h + 1)
                act.activation(hT[h][:], ps[:, bank(h, 3), :], ACT.Copy,
                               scale=cols_sb[:, V_N2:V_N2 + 1]).then_inc(hT_ready, 1)

            def ffn_gelu(h, c):
                act.wait_ge(ffn_h_ps, h * NC + c + 1)
                act.activation(ffn_hid[h][:, c, :], ps[:, bank(h, c), :], ACT.Gelu,
                               bias=cols_sb[:, V_B1 + c:V_B1 + c + 1]).then_inc(ffn_h_ready, 1)

            def xlT_copy(h):
                act.wait_ge(xlT_ps, h + 1)
                act.activation(xlT[h][:], ps[:, bank(h, 3), :], ACT.Copy).then_inc(xlT_ready, 1)

            def softmax(t):
                act.wait_ge(max_ready, t + 1)
                if t >= 2:
                    act.wait_ge(pT_ps, parts_before(t - 1))
                n = P * (t + 1)
                act.activation(pr[:, t % 2, 0:n], score_banks(t)[:, 0:n], ACT.Exp, bias=nmx[:, t:t + 1],
                               accum_out=den[:, t:t + 1]).then_inc(p_ready, 1)

            def pT_copy(t):
                for n, (engine, a, z) in enumerate(pT_parts(t)):
                    if engine == "act":
                        act.wait_ge(pT_ps, parts_before(t) + n + 1)
                        if t >= 2:
                            act.wait_ge(pv_ps, t - 1)
                        act.activation(prT[:, t % 2, a * P:z * P], ps[:, bank(t // TH, 2), 0:(z - a) * P],
                                       ACT.Copy).then_inc(pT_act, 1)

            def xfT_copy(h):
                act.wait_ge(xfT_ps, h + 1)
                act.activation(xfT[h][:], ps[:, bank(h, 2), :], ACT.Copy).then_inc(xfT_ready, 1)

            def xf_high(h):
                act.wait_ge(xfT_ready, h + 1)
                act.activation(xf_hi[h][:], xfT[h][:], ACT.Copy).then_inc(xf_high_ready, 1)

            def router_exp(h):
                act.wait_ge(lg_ready, h + 1)
                act.activation(lg[h][:], lg[h][:], ACT.Exp).then_inc(lexp_ready, 1)

            def wT_copy(h):
                act.wait_ge(wT_ps, h + 1)
                act.activation(wT[h][:], ps[0:EX, bank(h, 2), :], ACT.Copy).then_inc(wT_ready, 1)

            def moe_gelu(h, e, c):
                k = h * EX + e
                act.wait_ge(moe_h_ps, k * NC + c + 1)
                if k >= 2:
                    act.wait_ge(moe_ps, k - 1)
                i = V_EB1 + e * NC + c
                act.activation(hid[:, k % 2, c, :], ps[:, c, :], ACT.Gelu,
                               bias=cols_sb[:, i:i + 1]).then_inc(moe_h_ready, 1)

            w1_high()
            pu_copy()
            window_exp(1, 0)
            window_exp(0, 0)
            g_copy()
            qkv_copy(0, 1)
            v_copy()
            qkv_copy(1, 1)
            ot_copy(0, 0)
            ot_copy(1, 0)
            xc20_copy(0)
            window_exp(0, 1)
            xp_squares(0)
            hT_copy(0)
            window_exp(1, 1)
            ffn_gelu(0, 0)
            ffn_gelu(0, 1)
            ot_copy(0, 1)
            ot_copy(1, 1)
            xlT_copy(0)
            xc20_copy(1)
            for t in range(3):
                softmax(t)
            pT_copy(1)
            softmax(3)
            xp_squares(1)
            pT_copy(3)
            hT_copy(1)
            ffn_gelu(1, 0)
            ffn_gelu(1, 1)
            xfT_copy(0)
            xf_high(0)
            moe_gelu(0, 0, 0)
            moe_gelu(0, 0, 1)
            router_exp(0)
            moe_gelu(0, 1, 0)
            xlT_copy(1)
            moe_gelu(0, 1, 1)
            wT_copy(0)
            softmax(4)
            moe_gelu(0, 2, 0)
            moe_gelu(0, 2, 1)
            pT_copy(4)
            softmax(5)
            moe_gelu(0, 3, 0)
            moe_gelu(0, 3, 1)
            pT_copy(5)
            softmax(6)
            moe_gelu(0, 4, 0)
            moe_gelu(0, 4, 1)
            pT_copy(6)
            softmax(7)
            moe_gelu(0, 5, 0)
            moe_gelu(0, 5, 1)
            pT_copy(7)
            moe_gelu(0, 6, 0)
            moe_gelu(0, 6, 1)
            moe_gelu(0, 7, 0)
            moe_gelu(0, 7, 1)
            xfT_copy(1)
            xf_high(1)
            moe_gelu(0, 8, 0)
            moe_gelu(0, 8, 1)
            router_exp(1)
            moe_gelu(1, 0, 0)
            moe_gelu(1, 0, 1)
            moe_gelu(1, 1, 0)
            wT_copy(1)
            moe_gelu(1, 1, 1)
            moe_gelu(1, 2, 0)
            moe_gelu(1, 2, 1)
            moe_gelu(1, 3, 0)
            moe_gelu(1, 3, 1)
            moe_gelu(1, 4, 0)
            moe_gelu(1, 4, 1)
            moe_gelu(1, 5, 0)
            moe_gelu(1, 5, 1)
            moe_gelu(1, 6, 0)
            moe_gelu(1, 6, 1)
            moe_gelu(1, 7, 0)
            moe_gelu(1, 7, 1)
            moe_gelu(1, 8, 0)
            moe_gelu(1, 8, 1)

        @block.vector
        def _(dve):
            steps = [0]

            def step(ins):
                steps[0] += 1
                ins.then_inc(dve_step, 1)

            def settle():
                dve.wait_ge(dve_step, steps[0])

            for b in (1, 0):
                a, z = BRANCHES[b]["first"]
                cut = BRANCHES[b]["windows"][0] * BRANCHES[b]["w"] - a
                dve.memset(winT[b][0:C, 0:a], 0.0)
                dve.memset(winT[b][0:C, a + cut:XCOLS + z + cut], 0.0)
                dve.memset(winT[b][0:C, XCOLS + z + T:2 * XCOLS], 0.0).then_inc(win_clear, 1)
                dve.memset(winT[b][C:C + 1, :], 1.0).then_inc(win_clear, 1)
            for n, part in enumerate(PARTS):
                dve.wait_ge(ld_x[n], 16)
                for t in range(part.start, part.stop):
                    step(dve.bn_stats(st[:, t, :], x_sb[:, t, :]))
                settle()
                for t in range(part.start, part.stop):
                    dve.bn_aggr(mv[:, t, :], st[:, t, :]).then_inc(stats0, 1)
            for n, part in enumerate(PARTS):
                tiles = part.stop - part.start
                dve.wait_ge(rstd0_ready, n + 1)
                dve.wait_ge(xi_ps, n + 1)
                dve.wait_ge(ld_vec, 48)
                dve.tensor_tensor(xi[:, part, :], ps[:, 1 - n, 0:tiles * DI].rearrange("p (t n) -> p t n", t=tiles),
                                  spread(rstd0[:, part], 2, DI), ALU.mult).then_inc(xi_taken, 1)
                dve.wait_ge(xi_taken, n + 1)
                step(dve.tensor_tensor(xi[:, part, :], xi[:, part, :], spread(rows_sb[:, R_DB:R_DB + DI], 1, tiles),
                                       ALU.add))
                settle()
                step(dve.tensor_tensor(xi2[:, part, :], xi[:, part, :], xi[:, part, :], ALU.mult))
                settle()
                dve.tensor_reduce(ss[:, part], xi2[:, part, :], AX.X, ALU.add).then_inc(ss_ready, 1)
            for n, part in enumerate(PARTS):
                dve.wait_ge(ss_ready, n + 1)
                dve.wait_ge(rstd1_ready, n + 1)
                dve.tensor_tensor(xi2[:, part, :], xi[:, part, :], spread(rstd1[:, part], 2, DI),
                                  ALU.mult).then_inc(xin_ready, 1)
            dve.wait_ge(win_clear, 4)
            dve.wait_ge(win_ps[1], 1)
            dst, src = window_part(1, 0)
            dve.tensor_scalar(dst, src, cols_sb[0:C, V_N1 + 1:V_N1 + 2], None, ALU.mult).then_inc(win_ready[1], 1)
            dve.wait_ge(bias_high, 1)
            low = slice(BIAS_LOW, BIAS_MASK)
            dve.tensor_tensor(bias_parts[low, 0:BIAS_SEL], bias_sb[low, 0:BIAS_SEL],
                              bias_parts[low, 0:BIAS_SEL].bitcast(F32), ALU.subtract).then_inc(bias_ready, 1)
            dve.wait_ge(stats0, NT)
            for t in range(NT):
                step(dve.tensor_scalar(xn[:, t, :], x_sb[:, t, :], mv[:, t, 0:1], rstd0[:, t:t + 1],
                                       ALU.subtract, ALU.mult))

            def heads(ap, nh, d):
                return ap.rearrange("p i (h d) -> p i h d", d=HD)[:, :, :, d]

            SHAPE = "p (i h j) -> p i h j"

            def window_product(b, h, d):
                br = BRANCHES[b]
                w, nh = br["w"], br["nh"]
                if d == 0:
                    dve.wait_ge(qkv_act[b], h + 1)
                    if h:
                        dve.wait_ge(wv_ps[b], h)
                t = qkv[b][h]
                q = heads(t[:, :, 0:HD * nh], nh, d)
                k = heads(t[:, :, HD * nh:2 * HD * nh], nh, d).rearrange("p j h -> p h j")
                product = dve.tensor_tensor(prod[b][:, d, :].rearrange(SHAPE, i=w, h=nh),
                                            spread(q, 3, w), spread(k, 1, w), ALU.mult)
                if qk_parts(h) == HD:
                    product.then_inc(qk_ready[b], 1)
                    return
                step(product)
                if d % 2:
                    settle()
                    dve.tensor_tensor(prod[b][:, d - 1, :], prod[b][:, d - 1, :], prod[b][:, d, :],
                                      ALU.add).then_inc(qk_ready[b], 1)

            def window_scores(b, h):
                w = BRANCHES[b]["w"]
                dve.wait_ge(qk_ps[b], h + 1)
                scores = window_sum(b, h).rearrange("p a (r j) -> p a r j", j=w)
                rows4 = sc[b][:].rearrange("p (a r j) -> p a r j", a=b + 1, j=w)
                top = stat[b][:, 0, :].rearrange("p (a r) -> p a r", a=b + 1)
                step(dve.tensor_reduce(top, scores, AX.X, ALU.max))
                settle()
                dve.tensor_tensor(rows4, scores, spread(top, 3, w), ALU.subtract).then_inc(sc_ready[b], 1)

            def window_weighted(b, h, d):
                br = BRANCHES[b]
                w, nh = br["w"], br["nh"]
                if d == 0:
                    dve.wait_ge(exp_ready[b], h + 1)
                v = heads(qkv[b][h][:, :, 2 * HD * nh:3 * HD * nh], nh, d).rearrange("p j h -> p h j")
                dve.tensor_tensor(prod[b][:, d, :].rearrange(SHAPE, i=w, h=nh), sc[b][:].rearrange(SHAPE, i=w, h=nh),
                                  spread(v, 1, w), ALU.mult).then_inc(wv_ready[b], 1)

            def window_sums(b, h):
                dve.wait_ge(exp_ready[b], h + 1)
                rows3 = sc[b][:].rearrange("p (r j) -> p r j", j=BRANCHES[b]["w"])
                step(dve.tensor_reduce(stat[b][:, 1, :], rows3, AX.X, ALU.add))
                settle()
                step(dve.reciprocal(stat[b][:, 2, :], stat[b][:, 1, :]))

            def value_add(b, h):
                w = BRANCHES[b]["w"]
                dve.wait_ge(wv_ready[b], HD * (h + 1))
                halves = prod[b][:].rearrange("p d (r j) -> p d r j", j=w)
                dve.tensor_tensor(halves[:, :, :, 0:w // 2], halves[:, :, :, 0:w // 2], halves[:, :, :, w // 2:w],
                                  ALU.add).then_inc(va_ready[b], 1)

            def window_values(b, h):
                br = BRANCHES[b]
                w, nh = br["w"], br["nh"]
                dve.wait_ge(wv_ps[b], h + 1)
                values = window_out(b, h).rearrange("p (d r) -> p d r", d=HD)
                settle()
                dve.wait_ge(cleared, 4)
                if h:
                    dve.wait_ge(ot_ps[b], h)
                for g in range(br["groups"]):
                    r = slice(g * br["slots"], (g + 1) * br["slots"])
                    dst = ox[b][r, 0:w, g * HD * nh:(g + 1) * HD * nh].rearrange("p i (h d) -> p d i h", d=HD)
                    src = values[r].rearrange("p d (i h) -> p d i h", h=nh)
                    rec = spread(stat[b][r, 2, :].rearrange("p (i h) -> p i h", h=nh), 1, HD)
                    dve.tensor_tensor(dst, src, rec, ALU.mult).then_inc(ox_ready[b], 1)

            def xc_add(h):
                br = BRANCHES[0]
                dve.wait_ge(xc_ps[0], h + 1)
                dve.wait_ge(xc20_ready, 2 * (h + 1))
                n = br["windows"][h]
                at = MARGIN - br["first"][h]
                for a in range(2):
                    chunks = br["chunks"] - a
                    src = ps[:, bank(h, a), :].rearrange("p (i c s) -> p i c s", i=2, s=br["slots"])
                    dst = xcT[:, at:at + (n + 1) * br["w"]]
                    for i in range(2):
                        j = 2 * a + i
                        d = dst[:, j:j + n * br["w"]].rearrange("p (s k) -> p k s", k=br["w"])[:, 0:4 * chunks - 3:4, :]
                        dve.tensor_tensor(d, src[:, i, 0:chunks, 0:n], d, ALU.add).then_inc(xc_ready, 1)

            def xp_add(h):
                hs = slice(h * TH, (h + 1) * TH)
                dve.wait_ge(xc_tok_ps, h + 1)
                dve.tensor_tensor(xp[h][:], ps[:, bank(h, 2), :].rearrange("p (t d) -> p t d", t=TH), xn[:, hs, :],
                                  ALU.add).then_inc(xp_ready, 1)

            def xp_norm(h):
                dve.wait_ge(rstd2_ready, h + 1)
                dve.tensor_tensor(sq[h][:], xp[h][:], spread(rstd2[h][:], 2, D), ALU.mult).then_inc(h_ready, 1)

            def moments(src, h, stats):
                for t in range(TH):
                    step(dve.bn_stats(st2[h][:, t, :], src[:, t, :]))
                settle()
                for t in range(TH):
                    dve.bn_aggr(mv2[h][:, t, :], st2[h][:, t, :]).then_inc(stats, 1)

            def layernorm(src, h, stats, rstd_ready, ready):
                dve.wait_ge(stats, TH * (h + 1))
                dve.wait_ge(rstd_ready, h + 1)
                for t in range(TH):
                    dve.tensor_scalar(xl[h][:, t, :], src[:, t, :], mv2[h][:, t, 0:1], rstd3[h][:, t:t + 1],
                                      ALU.subtract, ALU.mult).then_inc(ready, 1)

            def x1_moments(h):
                dve.wait_ge(ffn_ps, h + 1)
                dve.wait_ge(xs_ready, h + 1)
                dve.tensor_tensor(x1[h][:], ps[:, bank(h, 2), :].rearrange("p (t d) -> p t d", t=TH),
                                  xs[:, h * TH:(h + 1) * TH, :], ALU.add).then_inc(x1_ready, 1)
                dve.wait_ge(x1_ready, h + 1)
                moments(x1[h], h, stats2)

            def x1_norm(h):
                layernorm(x1[h], h, stats2, rstd3_ready, xl_ready)

            def row_max(t):
                dve.wait_ge(s_ps, t + 1)
                dve.tensor_reduce(nmx[:, t:t + 1], score_banks(t)[:, 0:P * (t + 1)], AX.X, ALU.max,
                                  negate=True).then_inc(max_ready, 1)

            def pT_copy(t):
                for n, (engine, a, z) in enumerate(pT_parts(t)):
                    if engine == "dve":
                        dve.wait_ge(pT_ps, parts_before(t) + n + 1)
                        if t >= 2:
                            dve.wait_ge(pv_ps, t - 1)
                        dve.tensor_copy(prT[:, t % 2, a * P:z * P],
                                        ps[:, bank(t // TH, 2), 0:(z - a) * P]).then_inc(pT_dve, 1)

            def x2_tile(t):
                h = t // TH
                dve.wait_ge(p_ready, t + 1)
                step(dve.reciprocal(rden[:, t:t + 1], den[:, t:t + 1]))
                settle()
                dve.wait_ge(pv_ps, t + 1)
                dve.scalar_tensor_tensor(x2[h][:, t % TH, :], ps[:, bank(h, 3), 0:D], rden[:, t:t + 1],
                                         x1[h][:, t % TH, :], ALU.mult, ALU.add).then_inc(x2_ready, 1)

            def x2_moments(h):
                dve.wait_ge(x2_ready, TH * (h + 1))
                moments(x2[h], h, stats3)

            def x2_norm(h):
                layernorm(x2[h], h, stats3, rstd4_ready, xf_ready)

            def xf_low(h):
                dve.wait_ge(xf_high_ready, h + 1)
                dve.tensor_tensor(xf_lo[h][:], xfT[h][:], xf_hi[h][:].bitcast(F32), ALU.subtract).then_inc(xf_low_ready, 1)

            def router_logits(h):
                dve.wait_ge(lg_ps, h + 1)
                logits = ps[:, bank(h, 3), 0:TH * E].rearrange("p (t e) -> p t e", t=TH)
                step(dve.tensor_tensor(lg[h][:], logits, spread(rows_sb[:, R_RB:R_RB + E], 1, TH), ALU.add))
                settle()
                step(dve.tensor_reduce(lmx[h][:], lg[h][:], AX.X, ALU.max))
                settle()
                dve.tensor_tensor(lg[h][:], lg[h][:], spread(lmx[h][:], 2, E), ALU.subtract).then_inc(lg_ready, 1)

            def router(h):
                dve.wait_ge(lexp_ready, h + 1)
                step(dve.tensor_reduce(lsum[h][:], lg[h][:], AX.X, ALU.add))
                settle()
                step(dve.reciprocal(lmx[h][:], lsum[h][:]))
                settle()
                step(dve.tensor_tensor(lg[h][:], lg[h][:], spread(lmx[h][:], 2, E), ALU.mult))
                settle()
                for op, dst in ((ALU.is_gt, gt[h]), (ALU.is_equal, eq[h])):
                    step(dve.tensor_tensor(dst[:].rearrange("p t (e f) -> p t e f", e=E), spread(lg[h][:], 2, E),
                                           spread(lg[h][:], 3, E), op))
                settle()
                step(dve.tensor_tensor(eq[h][:], eq[h][:], spread(tri_sb[:], 1, TH), ALU.mult))
                settle()
                step(dve.tensor_tensor(gt[h][:], gt[h][:], eq[h][:], ALU.add))
                settle()
                step(dve.tensor_reduce(eq[h][:, :, 0:E], gt[h][:].rearrange("p t (e f) -> p t e f", e=E), AX.X, ALU.add))
                settle()
                dve.scalar_tensor_tensor(wts[h][:, :, 0:E], eq[h][:, :, 0:E], 2.0, lg[h][:], ALU.is_lt, ALU.mult)\
                   .then_inc(wts_ready, 1)

            def acc_begin(h):
                dve.wait_ge(b2_ps, h + 1)
                dve.wait_ge(xf_ready, TH * (h + 1))
                dve.tensor_tensor(x2[h], ps[:, bank(h, 3), :].rearrange("p (t d) -> p t d", t=TH), x2[h], ALU.add).then_inc(acc_start, 1)

            def moe_add(h, e):
                k = h * EX + e
                if e == 0:
                    dve.wait_ge(wts_ready, h + 1)
                    dve.wait_ge(acc_start, h + 1)
                else:
                    dve.wait_ge(moe_taken, k * TH)
                dve.wait_ge(moe_ps, k + 1)
                for t in range(TH):
                    g = h * TH + t
                    dve.scalar_tensor_tensor(acc[:, g, :], ps[:, 2 + k % 2, t * D:(t + 1) * D], wts[h][:, t, e:e + 1],
                                             acc[:, g, :], ALU.mult, ALU.add).then_inc(moe_taken, 1)

            for d in range(HD):
                window_product(1, 0, d)
            for d in range(HD):
                window_product(0, 0, d)
            window_scores(1, 0)
            window_scores(0, 0)
            window_sums(1, 0)
            for d in range(HD):
                window_weighted(0, 0, d)
            window_sums(0, 0)
            for d in range(HD):
                window_weighted(1, 0, d)
            value_add(1, 0)
            window_values(0, 0)
            for d in range(HD):
                window_product(0, 1, d)
            window_values(1, 0)
            for d in range(HD):
                window_product(1, 1, d)
            xc_add(0)
            window_scores(0, 1)
            xp_add(0)
            window_sums(0, 1)
            for d in range(HD):
                window_weighted(0, 1, d)
            value_add(0, 1)
            xp_norm(0)
            window_scores(1, 1)
            window_values(0, 1)
            for d in range(HD):
                window_weighted(1, 1, d)
            value_add(1, 1)
            x1_moments(0)
            window_sums(1, 1)
            window_values(1, 1)
            x1_norm(0)
            row_max(0)
            row_max(1)
            xc_add(1)
            row_max(2)
            pT_copy(0)
            row_max(3)
            x2_tile(0)
            xp_add(1)
            pT_copy(2)
            x2_tile(1)
            x2_tile(2)
            xp_norm(1)
            x2_tile(3)
            x2_moments(0)
            x2_norm(0)
            xf_low(0)
            x1_moments(1)
            router_logits(0)
            x1_norm(1)
            router(0)
            row_max(4)
            acc_begin(0)
            moe_add(0, 0)
            pT_copy(4)
            moe_add(0, 1)
            row_max(5)
            moe_add(0, 2)
            x2_tile(4)
            pT_copy(5)
            row_max(6)
            moe_add(0, 3)
            x2_tile(5)
            pT_copy(6)
            row_max(7)
            moe_add(0, 4)
            x2_tile(6)
            pT_copy(7)
            x2_tile(7)
            x2_moments(1)
            moe_add(0, 5)
            x2_norm(1)
            moe_add(0, 6)
            xf_low(1)
            router_logits(1)
            moe_add(0, 7)
            router(1)
            moe_add(0, 8)
            acc_begin(1)
            for t in range(9):
                moe_add(1, t)

        @block.tensor
        def _(pe):
            def mm(dst, lhs, rhs, start=True, stop=True):
                return pe.matmul(dst, lhs, rhs, start=start, stop=stop)

            pe.wait_ge(ld_down, 16)
            mm(ps[:, 7, 0:DI], down_sb[:, DI:DI + P], down_sb[:, 0:DI]).then_inc(setup_ps, 1)
            pe.wait_ge(ld_xT, 16)
            pe.wait_ge(downc_ready, 1)
            for n, part in enumerate(PARTS):
                for t in range(part.start, part.stop):
                    at = (t - part.start) * DI
                    last = mm(ps[:, 1 - n, at:at + DI], xT_sb[:, t * P:(t + 1) * P], downc[:])
                last.then_inc(xi_ps, 1)
            pe.wait_ge(ld_ctx, 48)
            for a in range(2):
                last = mm(ps[:, 6 + a, :], wqT_sb[:], ctxT_sb[:, a * 512:(a + 1) * 512])
            last.then_inc(k_ps, 1)

            def channels(b, n):
                pe.wait_ge(xin_ready, n + 1)
                if n:
                    pe.wait_ge(win_ready[b], 1)
                for t in range(PARTS[n].start, PARTS[n].stop):
                    last = pe.transpose(ps[0:C, 2 + 2 * b + t // 4, (t % 4) * P:(t % 4 + 1) * P],
                                        xi2[:, t, b * C:(b + 1) * C], ident[:])
                last.then_inc(win_ps[b], 1)

            def qkv_rows(b, h):
                br = BRANCHES[b]
                pe.wait_ge(win_ready[b], h + 1)
                if h == 1:
                    pe.wait_ge(win_ready[1], 2)
                cols = winT[b][:, h * XCOLS:h * XCOLS + br["slots"] * br["w"]]
                cols = cols.rearrange("p (s i) -> p i s", i=br["w"])
                n, s = br["cols"], br["slots"]
                for i in range(br["w"]):
                    for g in range(br["groups"]):
                        last = mm(ps[g * s:(g + 1) * s, qkv_bank(b, h), i * n:(i + 1) * n], cols[:, i, :],
                                  qkvw_sb[:, b, g * n:(g + 1) * n])
                last.then_inc(qkv_ps[b], 1)

            pe.wait_ge(ld_vec, 48)
            channels(1, 0)
            channels(0, 0)
            pe.wait_ge(ld_qkvw, 16)
            pe.wait_ge(win_clear, 4)
            pe.wait_ge(xi_taken, 2)
            qkv_rows(1, 0)
            qkv_rows(0, 0)
            channels(1, 1)
            channels(0, 1)

            def scores_side():
                pe.wait_ge(k_ready, 1)
                for a in range(2):
                    last = mm(ps[:, 6 + a, :], wq_sb[:], kT[:, a * 512:(a + 1) * 512])
                last.then_inc(g_ps, 1)

            def proj_up():
                pe.wait_ge(ld_proj, 48)
                pe.wait_ge(qkv_act[1], 1)
                for b in range(2):
                    mm(ps[:, 0, 128 * b:128 + 128 * b], projT_sb[:, b, :], up_sb[:, b, :])
                mm(ps[:, 0, 256:257], upb_sb[:], cols_sb[0:DI, V_PB:V_PB + 1]).then_inc(setup_ps, 1)

            def qk_sum(b, h, n):
                banks = window_sum(b, h)
                if n == 0:
                    pe.wait_ge(qkv_act[b], h + 1)
                    if b == 1 and h == 0:
                        pe.wait_ge(win_ready[0], 2)
                        pe.wait_ge(half_ready, 1)
                    if b == 1 and h == 1:
                        pe.wait_ge(v_ready, 1)
                pe.wait_ge(qk_ready[b], sum(qk_parts(u) for u in range(h)) + n + 1)
                src = prod[b][:, n * HD // qk_parts(h), :]
                for a in range(b + 1):
                    last = mm(banks[:, a, :], half_ident[:], src[:, 400 * a:400 * a + 400],
                              start=(n == 0), stop=(n == qk_parts(h) - 1))
                if n == qk_parts(h) - 1:
                    last.then_inc(qk_ps[b], 1)
                if n == 0:
                    pe.wait_ge(bias_ready, 1)
                    k = BIAS_ROWS if h == 0 else BIAS_MASK
                    for a in range(b + 1):
                        at = BIAS_AT[b] + 400 * a
                        mm(banks[:, a, :], bias_parts[0:k, BIAS_SEL + b * P:BIAS_SEL + (b + 1) * P],
                           bias_parts[0:k, at:at + 400], start=False, stop=False)

            def value_sum(b, h):
                w = BRANCHES[b]["w"]
                if b == 1 and h == 0:
                    pe.wait_ge(pu_ready, 8)
                    pe.wait_ge(out_bias_ready, 1)
                if halved(b, h):
                    pe.wait_ge(va_ready[b], sum(halved(b, u) for u in range(h + 1)))
                    w //= 2
                else:
                    pe.wait_ge(wv_ready[b], HD * (h + 1))
                src = prod[b][:].rearrange("p d (r j) -> p d r j", j=BRANCHES[b]["w"])
                dst = window_out(b, h).rearrange("p (d r) -> p d r", d=HD)
                for j in range(w):
                    last = mm(dst, ident[:], src[:, :, :, j], start=(j == 0), stop=(j == w - 1))
                last.then_inc(wv_ps[b], 1)

            def v_rows():
                pe.wait_ge(g_ready, 1)
                for t in range(NT):
                    last = pe.transpose(ps[:, 6 + t // 4, (t % 4) * P:(t % 4 + 1) * P], kT[:, t * P:(t + 1) * P], ident[:])
                last.then_inc(v_ps, 1)

            def out_columns(b, h):
                br = BRANCHES[b]
                pe.wait_ge(ox_ready[b], br["groups"] * (h + 1))
                if h == 0:
                    pe.wait_ge(ld_ffn, 48)
                s = br["slots"]
                fold_ap = fold_sb[:, 0:64] if b == 0 else fold_sb[:, 64:96]
                for c in range(br["chunks"]):
                    last = mm(ps[:, bank(h, 1 - b), c * s:(c + 1) * s],
                              ox[b][:, 4 * c:4 * c + 4, :].rearrange("p i c -> p (i c)"), fold_ap)
                last.then_inc(ot_ps[b], 1)

            def out_project(b, h):
                br = BRANCHES[b]
                s, n = br["slots"], br["chunks"]
                pe.wait_ge(ot_ready[b], h + 1)
                if b == 0:
                    pe.wait_ge(ot_ready[1], h + 1)
                at = bank(h, 2 * b)
                for i in range(4):
                    cols = (n if i < 2 or br["w"] % 4 == 0 else n - 1) * s
                    last = mm(ps[:, at + i // 2, (i % 2) * 256:(i % 2) * 256 + cols], pu[b][:, i, :], ot[b][:, 0:cols])
                last.then_inc(xc_ps[b], 1)

            def to_tokens(h):
                pe.wait_ge(xc_ready, 4 * (h + 1))
                pe.wait_ge(xc20_ready, 2 * (h + 1))
                for t in range(TH):
                    at = MARGIN + (h * TH + t) * P
                    last = pe.transpose(ps[:, bank(h, 2), t * P:(t + 1) * P], xcT[:, at:at + P], ident[:])
                last.then_inc(xc_tok_ps, 1)

            def h_columns(h):
                pe.wait_ge(h_ready, h + 1)
                for t in range(TH):
                    last = pe.transpose(ps[:, bank(h, 3), t * P:(t + 1) * P], sq[h][:, t, :], ident[:])
                last.then_inc(hT_ps, 1)

            def ffn_hidden(h, c):
                pe.wait_ge(hT_ready, h + 1)
                mm(ps[:, bank(h, c), :], ffn_w1_sb[:, c * P:(c + 1) * P], hT[h][:]).then_inc(ffn_h_ps, 1)

            def ffn_output(h):
                pe.wait_ge(xp_ready, h + 1)
                pe.wait_ge(ffn_h_ready, NC * (h + 1))
                for t in range(TH):
                    for c in range(NC):
                        last = mm(ps[:, bank(h, 2), t * D:(t + 1) * D], ffn_hid[h][:, c, t * P:(t + 1) * P],
                                  ffn_w2_sb[:, c, :], start=(c == 0), stop=(c == NC - 1))
                last.then_inc(ffn_ps, 1)

            def xl_columns(h):
                pe.wait_ge(xl_ready, TH * (h + 1))
                for t in range(TH):
                    last = pe.transpose(ps[:, bank(h, 3), t * P:(t + 1) * P], xl[h][:, t, :], ident[:])
                last.then_inc(xlT_ps, 1)

            def scores(t):
                h = t // TH
                if t % TH == 0:
                    pe.wait_ge(xlT_ready, h + 1)
                    pe.wait_ge(ffn_h_ready, NC * (h + 1))
                if t == 0:
                    pe.wait_ge(g_ready, 1)
                    pe.wait_ge(casts, 2)
                back = 2 if h == 0 else 1
                if t % TH >= back:
                    pe.wait_ge(p_ready, t - back + 1)
                q = xlT[h][:, (t % TH) * P:(t % TH + 1) * P]
                for a in range(t // 4 + 1):
                    n = min(512, P * (t + 1) - a * 512)
                    dst = score_banks(t)[:, a * 512:a * 512 + n]
                    diagonal = a == t // 4
                    last = mm(dst, q, gT[:, a * 512:a * 512 + n], stop=not diagonal)
                    if diagonal:
                        last = mm(dst[:, n - P:n], ident16[:], causal16[:], start=False)
                last.then_inc(s_ps, 1)

            def columns_copied(t, n):
                before = [e for u in range(t) for e, _, _ in pT_parts(u)] + [e for e, _, _ in pT_parts(t)[:n]]
                if before.count("act"):
                    pe.wait_ge(pT_act, before.count("act"))
                if before.count("dve"):
                    pe.wait_ge(pT_dve, before.count("dve"))

            def p_columns(t, n):
                pe.wait_ge(p_ready, t + 1)
                if t % TH == 0:
                    pe.wait_ge(x1_ready, t // TH + 1)
                columns_copied(t, n)
                _, a, z = pT_parts(t)[n]
                for k in range(a, z):
                    last = pe.transpose(ps[:, bank(t // TH, 2), (k - a) * P:(k - a + 1) * P],
                                        pr[:, t % 2, k * P:(k + 1) * P], ident[:])
                last.then_inc(pT_ps, 1)

            def values(t):
                columns_copied(t, len(pT_parts(t)))
                if t % TH:
                    pe.wait_ge(x2_ready, t)
                for k in range(t + 1):
                    last = mm(ps[:, bank(t // TH, 3), 0:D], prT[:, t % 2, k * P:(k + 1) * P], v_sb[:, k, :],
                              start=(k == 0), stop=(k == t))
                last.then_inc(pv_ps, 1)

            def xf_columns(h):
                pe.wait_ge(xf_ready, TH * (h + 1))
                for t in range(TH):
                    last = pe.transpose(ps[:, bank(h, 2), t * P:(t + 1) * P], xl[h][:, t, :], ident[:])
                last.then_inc(xfT_ps, 1)

            def router_logits(h):
                pe.wait_ge(xfT_ready, h + 1)
                pe.wait_ge(ld_router, 48)
                for t in range(TH):
                    last = mm(ps[:, bank(h, 3), t * E:(t + 1) * E], xfT[h][:, t * P:(t + 1) * P], router_sb[:])
                last.then_inc(lg_ps, 1)

            def weight_rows(h):
                pe.wait_ge(wts_ready, h + 1)
                for t in range(TH):
                    last = pe.transpose(ps[0:EX, bank(h, 2), t * P:(t + 1) * P], wts[h][:, t, :], ident[:])
                last.then_inc(wT_ps, 1)

            def expert_bias(h):
                pe.wait_ge(wT_ready, h + 1)
                pe.wait_ge(ld_moe, 48)
                for t in range(TH):
                    last = mm(ps[:, bank(h, 3), t * D:(t + 1) * D], wT[h][:, t * P:(t + 1) * P], moe_b2_sb[:])
                last.then_inc(b2_ps, 1)

            def hidden(h, e, c):
                k = h * EX + e
                if e == 0:
                    pe.wait_ge(xf_low_ready, h + 1)
                if k == 0:
                    pe.wait_ge(w1_low_ready, 1)
                    pe.wait_ge(p_ready, TH)
                else:
                    pe.wait_ge(moe_h_ready, NC * (k - 1) + c + 1)
                cols = slice(c * P, (c + 1) * P)
                mm(ps[:, c, :], w1_hi[:, e, cols], xf_hi[h][:], stop=False)
                mm(ps[:, c, :], w1_lo[:, e, cols], xf_hi[h][:], start=False, stop=False)
                mm(ps[:, c, :], w1_hi[:, e, cols], xf_lo[h][:], start=False).then_inc(moe_h_ps, 1)

            def output(h, e):
                k = h * EX + e
                pe.wait_ge(moe_h_ready, NC * (k + 1))
                if k == 0:
                    pe.wait_ge(wT_ready, 1)
                elif k == 1:
                    pe.wait_ge(acc_start, 1)
                else:
                    pe.wait_ge(moe_taken, TH * (k - 1))
                for t in range(TH):
                    for c in range(NC):
                        last = mm(ps[:, 2 + k % 2, t * D:(t + 1) * D], hid[:, k % 2, c, t * P:(t + 1) * P],
                                  moe_w2_sb[:, e, c, :], start=(c == 0), stop=(c == NC - 1))
                last.then_inc(moe_ps, 1)

            qk_sum(1, 0, 0)
            qk_sum(1, 0, 1)
            proj_up()
            qk_sum(0, 0, 0)
            qk_sum(0, 0, 1)
            scores_side()
            qkv_rows(0, 1)
            v_rows()
            qkv_rows(1, 1)
            value_sum(0, 0)
            value_sum(1, 0)
            out_columns(0, 0)
            qk_sum(0, 1, 0)
            out_columns(1, 0)
            qk_sum(0, 1, 1)
            out_project(1, 0)
            out_project(0, 0)
            qk_sum(0, 1, 2)
            qk_sum(0, 1, 3)
            to_tokens(0)
            for n in range(HD):
                qk_sum(1, 1, n)
            h_columns(0)
            value_sum(0, 1)
            ffn_hidden(0, 0)
            ffn_hidden(0, 1)
            out_columns(0, 1)
            ffn_output(0)
            value_sum(1, 1)
            out_columns(1, 1)
            xl_columns(0)
            out_project(1, 1)
            scores(0)
            scores(1)
            out_project(0, 1)
            scores(2)
            p_columns(0, 0)
            scores(3)
            values(0)
            p_columns(1, 0)
            to_tokens(1)
            p_columns(2, 0)
            values(1)
            p_columns(3, 0)
            values(2)
            values(3)
            h_columns(1)
            ffn_hidden(1, 0)
            ffn_hidden(1, 1)
            xf_columns(0)
            ffn_output(1)
            router_logits(0)
            hidden(0, 0, 0)
            hidden(0, 0, 1)
            hidden(0, 1, 0)
            hidden(0, 1, 1)
            xl_columns(1)
            hidden(0, 2, 0)
            scores(4)
            weight_rows(0)
            hidden(0, 2, 1)
            expert_bias(0)
            output(0, 0)
            p_columns(4, 0)
            output(0, 1)
            p_columns(4, 1)
            scores(5)
            output(0, 2)
            values(4)
            hidden(0, 3, 0)
            hidden(0, 3, 1)
            p_columns(5, 0)
            scores(6)
            p_columns(5, 1)
            output(0, 3)
            values(5)
            hidden(0, 4, 0)
            p_columns(6, 0)
            hidden(0, 4, 1)
            scores(7)
            p_columns(6, 1)
            output(0, 4)
            values(6)
            hidden(0, 5, 0)
            p_columns(7, 0)
            hidden(0, 5, 1)
            p_columns(7, 1)
            hidden(0, 6, 0)
            hidden(0, 6, 1)
            values(7)
            output(0, 5)
            output(0, 6)
            hidden(0, 7, 0)
            hidden(0, 7, 1)
            xf_columns(1)
            hidden(0, 8, 0)
            hidden(0, 8, 1)
            router_logits(1)
            output(0, 7)
            hidden(1, 0, 0)
            output(0, 8)
            hidden(1, 0, 1)
            hidden(1, 1, 0)
            output(1, 0)
            weight_rows(1)
            hidden(1, 1, 1)
            hidden(1, 2, 0)
            expert_bias(1)
            hidden(1, 2, 1)
            output(1, 1)
            output(1, 2)
            hidden(1, 3, 0)
            hidden(1, 3, 1)
            hidden(1, 4, 0)
            hidden(1, 4, 1)
            output(1, 3)
            hidden(1, 5, 0)
            hidden(1, 5, 1)
            output(1, 4)
            hidden(1, 6, 0)
            hidden(1, 6, 1)
            output(1, 5)
            output(1, 6)
            hidden(1, 7, 0)
            hidden(1, 7, 1)
            hidden(1, 8, 0)
            hidden(1, 8, 1)
            output(1, 7)
            output(1, 8)


def kernel(**inputs):
    import numpy as np
    import concourse.bacc as bacc
    from concourse.bass_utils import run_bass_kernel_spmd

    a = {n: np.asarray(v) for n, v in inputs.items()}
    f = np.float32

    def attn(name):
        return a["L0_attn_" + name]

    def moe(name):
        return a["L0_ffn_" + name]

    def grouped(n, groups):
        w = np.concatenate([attn(f"qkv{n}_w"), attn(f"qkv{n}_b")[None]], 0)
        return w.reshape(C + 1, 3, groups, -1).transpose(0, 2, 1, 3).reshape(C + 1, QKV)

    bias = np.zeros((BIAS_ROWS, BIAS_COLS), f)
    for b, (n, br) in enumerate(zip((1, 2), BRANCHES)):
        w, g, nh = br["w"], br["groups"], br["nh"]
        at, sel = BIAS_AT[b], BIAS_SEL + b * P
        i = np.arange(w)
        r = attn(f"rpb{n}")[i[:, None] - i[None, :] + w - 1]
        r = r.reshape(w, w, g, nh).transpose(2, 0, 3, 1).reshape(g, -1)
        apart = (i[:, None] < br["shift"]) != (i[None, :] < br["shift"])
        bias[BIAS_MASK, at:at + r.shape[1]] = np.where(np.repeat(apart[:, None], nh, 1), f(-100), f(0)).reshape(-1)
        for k in (0, BIAS_LOW):
            bias[k:k + g, at:at + r.shape[1]] = r
            bias[k:k + g, sel:sel + P] = np.arange(P) // br["slots"] == np.arange(g)[:, None]
        bias[BIAS_MASK, sel:sel + P] = np.arange(P) % br["slots"] == 0

    cols = np.zeros((P, NV), f)
    cols[:, V_N2] = attn("norm2_w")
    cols[:, V_B1:V_B1 + NC] = attn("ffn_b1").reshape(NC, P).T
    cols[:, V_UPB] = attn("up_b")
    cols[:DI, V_PB] = np.concatenate([attn("proj1_b"), attn("proj2_b")])
    cols[:C, V_N1:V_N1 + 2] = attn("norm1_w").reshape(2, C).T
    b1 = np.concatenate([moe("rb1"), moe("sb1")[None]], 0)
    cols[:, V_EB1:] = b1.reshape(EX * NC, P).T
    rows = np.concatenate([attn("down_b"), attn("ffn_b2"), moe("router_b")])
    slot = np.arange(P)
    arrays = {
        "x": a["x"],
        "x_t": a["x"][0].T,
        "ctx_t": a["ctx_1024"][0, :T].T,
        "wq": a["L0_xattn_Wq"],
        "wq_t": a["L0_xattn_Wq"].T,
        "down_centre": np.concatenate([attn("down_w"), (np.eye(P) - 1.0 / P).astype(f)], 1),
        "identity": np.eye(P, dtype=f),
        "causal": np.triu(np.full((P, P), MASKED, f), 1),
        "up_w": attn("up_w"),
        "proj_t": np.stack([np.tile(attn(f"proj{n}_w").T, (1, 4)) for n in (1, 2)], 1),
        "qkv_w": np.stack([grouped(n, br["groups"]) for n, br in zip((1, 2), BRANCHES)], 1),
        "bias": bias,
        "fold": np.concatenate([slot[:, None] % br["slots"] == np.arange(br["slots"]) for br in BRANCHES], 1).astype(f),
        "ffn_w1": attn("ffn_w1"),
        "ffn_w2": attn("ffn_w2"),
        "router_w": moe("router_w"),
        "tri": np.tile(np.tril(np.ones((E, E), f), -1).reshape(1, -1), (P, 1)),
        "cols": cols,
        "rows": rows,
        "moe_w1": np.concatenate([moe("rw1"), moe("sw1")[None]], 0),
        "moe_w2": np.concatenate([moe("rw2"), moe("sw2")[None]], 0),
        "moe_b2": np.concatenate([moe("rb2"), moe("sb2")[None]], 0),
    }
    arrays = {n: np.ascontiguousarray(v) for n, v in arrays.items()}
    nc = bacc.Bacc("TRN2", target_bir_lowering=False, num_devices=1)
    args = {n: nc.dram_tensor("in_" + n, v.shape, F32, kind="ExternalInput").ap() for n, v in arrays.items()}
    out = nc.dram_tensor("out", (1, T, D), F32, kind="ExternalOutput").ap()
    decoder_layer(nc, out=out, **args)
    r = run_bass_kernel_spmd(nc, [{"in_" + n: v for n, v in arrays.items()}], core_ids=[0])
    return r.results[0]["out"]
```
